# Optimizing a Trainium2 kernel written in Bass

```python
import numpy as np
import jax
import jax.numpy as jnp

def _softmax(x, axis=-1):
    return jax.nn.softmax(x, axis=axis)

def _gelu(x):
    return jax.nn.gelu(x, approximate=True)

def _silu(x):
    return jax.nn.silu(x)

def _sigmoid(x):
    return jax.nn.sigmoid(x)

def _layernorm(x, axis=-1, eps=1e-05):
    m = jnp.mean(x, axis=axis, keepdims=True)
    v = jnp.var(x, axis=axis, keepdims=True)
    return (x - m) / jnp.sqrt(v + eps)

def _scatter_add(tgt, idx, src, axis=0):
    return tgt.at[idx].add(src)

def _segment_sum(src, seg, n):
    return jax.ops.segment_sum(src, seg, n)
kernel_name = 'mk_gnn_resnorm_d2_gnn_r32_68e6a0'

def setup_inputs(seed: int=0):
    np.random.seed(seed)
    _w = jnp.asarray

    def _rec_inputs():
        import jax
        import jax.numpy as jnp
        _gk = jax.random.key(seed)
        x = -0.000202 + 1 * jax.random.normal(jax.random.fold_in(_gk, 1), (3125, 128), jnp.float32)
        src = jax.random.randint(jax.random.fold_in(_gk, 2), (100000,), 0, 3125, jnp.int32)
        dst = jnp.minimum((3125 * jax.random.uniform(jax.random.fold_in(_gk, 3), (100000,)) ** 2.0).astype(jnp.int32), 99999)
        _o = jnp.argsort(dst, stable=True)
        src = src[_o]
        dst = dst[_o]
        edge_type_8 = jax.random.randint(jax.random.fold_in(_gk, 12), (100000,), 0, 8, jnp.int32)
        return (x, src, dst, edge_type_8)
    x, src, dst, edge_type_8 = _rec_inputs()

    def _L0_gnn_setup():
        import jax, jax.numpy as jnp
        import numpy as np
        N_NODES = 50000
        N_EDGES = 15625
        F_DIM = 128
        N_REL = 8
        N_LAYERS = 2
        NEG_SLOPE = 0.2

        def _segment_softmax(logits, seg, num_segments):
            m = jax.ops.segment_max(logits, seg, num_segments=num_segments)
            m = jax.lax.stop_gradient(m)
            e = jnp.exp(logits - m[seg])
            denom = jax.ops.segment_sum(e, seg, num_segments=num_segments)
            return e / (denom[seg] + 1e-16)

        def _rgat_layer(h, src, dst, edge_type, W, q, k, b):
            n = h.shape[0]
            xw = jnp.einsum('nf,rfg->rng', h, W)
            out_j = xw[edge_type, src]
            out_i = xw[edge_type, dst]
            logits = jax.nn.leaky_relu((out_i @ q + out_j @ k)[:, 0], NEG_SLOPE)
            alpha = _segment_softmax(logits, dst, n)
            agg = jax.ops.segment_sum(alpha[:, None] * out_j, dst, num_segments=n)
            return agg + b
        key = jax.random.key(seed)
        ks = jax.random.split(key, 6)
        x = jax.random.normal(ks[0], (N_NODES, F_DIM), dtype=jnp.float32)
        edge_index = jax.random.randint(ks[1], (2, N_EDGES), 0, N_NODES)
        edge_type = jax.random.randint(ks[2], (N_EDGES,), 0, N_REL)
        W = jax.random.normal(ks[3], (N_LAYERS, N_REL, F_DIM, F_DIM), dtype=jnp.float32) * (1.0 / np.sqrt(F_DIM)).astype(np.float32)
        att_q = jax.random.normal(ks[4], (N_LAYERS, F_DIM, 1), dtype=jnp.float32) * 0.1
        att_k = jax.random.normal(ks[5], (N_LAYERS, F_DIM, 1), dtype=jnp.float32) * 0.1
        bias = jnp.zeros((N_LAYERS, F_DIM), dtype=jnp.float32)
        return {'x': x, 'W': W, 'att_q': att_q, 'att_k': att_k, 'bias': bias, 'edge_index': edge_index, 'edge_type': edge_type}
    _L0_gnn_all = _L0_gnn_setup()
    _L0_gnn_in = {k: v for k, v in _L0_gnn_all.items() if k in ('W', 'att_q', 'att_k', 'bias')}
    del _L0_gnn_all

    def _L1_gnn_setup():
        import jax, jax.numpy as jnp
        import numpy as np
        N_NODES = 50000
        N_EDGES = 25000
        EPS = 1e-05

        def _gcn_norm(edge_index, num_nodes):
            loop = jnp.arange(num_nodes, dtype=edge_index.dtype)
            src = jnp.concatenate([edge_index[0], loop])
            dst = jnp.concatenate([edge_index[1], loop])
            deg = jax.ops.segment_sum(jnp.ones_like(dst, dtype=jnp.float32), dst, num_segments=num_nodes)
            dinv = jnp.where(deg > 0, jax.lax.rsqrt(deg), 0.0)
            norm = dinv[src] * dinv[dst]
            return (src, dst, norm)

        def _gcn_conv(x, W, b, src, dst, norm, num_nodes):
            h = x @ W
            msg = h[src] * norm[:, None]
            out = jax.ops.segment_sum(msg, dst, num_segments=num_nodes)
            return out + b

        def _batch_norm(x, gamma, beta):
            mean = jnp.mean(x, axis=0)
            var = jnp.mean((x - mean) ** 2, axis=0)
            return (x - mean) * jax.lax.rsqrt(var + EPS) * gamma + beta
        key = jax.random.key(seed)
        ks = jax.random.split(key, 16)
        s = 0.05
        return {'x': jax.random.uniform(ks[0], (N_NODES, 128), dtype=jnp.float32), 'edge_index': jax.random.randint(ks[1], (2, N_EDGES), 0, N_NODES, dtype=jnp.int32), 'W1': jax.random.normal(ks[2], (128, 256), dtype=jnp.float32) * s, 'b1': jnp.zeros((256,), jnp.float32), 'g1': jnp.ones((256,), jnp.float32), 'beta1': jnp.zeros((256,), jnp.float32), 'W2': jax.random.normal(ks[3], (256, 128), dtype=jnp.float32) * s, 'b2': jnp.zeros((128,), jnp.float32), 'g2': jnp.ones((128,), jnp.float32), 'beta2': jnp.zeros((128,), jnp.float32), 'W3': jax.random.normal(ks[4], (128, 128), dtype=jnp.float32) * s, 'b3': jnp.zeros((128,), jnp.float32), 'g3': jnp.ones((128,), jnp.float32), 'beta3': jnp.zeros((128,), jnp.float32)}
    _L1_gnn_all = _L1_gnn_setup()
    _L1_gnn_in = {k: v for k, v in _L1_gnn_all.items() if k in ('W1', 'b1', 'g1', 'beta1', 'W2', 'b2', 'g2', 'beta2', 'W3', 'b3', 'g3', 'beta3')}
    del _L1_gnn_all
    return {'x': x, 'src': src, 'dst': dst, 'edge_type_8': edge_type_8, 'L0_gnn_W': _L0_gnn_in['W'], 'L0_gnn_att_q': _L0_gnn_in['att_q'], 'L0_gnn_att_k': _L0_gnn_in['att_k'], 'L0_gnn_bias': _L0_gnn_in['bias'], 'L1_gnn_W1': _L1_gnn_in['W1'], 'L1_gnn_b1': _L1_gnn_in['b1'], 'L1_gnn_g1': _L1_gnn_in['g1'], 'L1_gnn_beta1': _L1_gnn_in['beta1'], 'L1_gnn_W2': _L1_gnn_in['W2'], 'L1_gnn_b2': _L1_gnn_in['b2'], 'L1_gnn_g2': _L1_gnn_in['g2'], 'L1_gnn_beta2': _L1_gnn_in['beta2'], 'L1_gnn_W3': _L1_gnn_in['W3'], 'L1_gnn_b3': _L1_gnn_in['b3'], 'L1_gnn_g3': _L1_gnn_in['g3'], 'L1_gnn_beta3': _L1_gnn_in['beta3']}

def reference(x, src, dst, edge_type_8, L0_gnn_W, L0_gnn_att_q, L0_gnn_att_k, L0_gnn_bias, L1_gnn_W1, L1_gnn_b1, L1_gnn_g1, L1_gnn_beta1, L1_gnn_W2, L1_gnn_b2, L1_gnn_g2, L1_gnn_beta2, L1_gnn_W3, L1_gnn_b3, L1_gnn_g3, L1_gnn_beta3):
    import jax
    import jax.numpy as jnp

    def _L0_gnn_ref(x, W, att_q, att_k, bias, edge_index, edge_type):
        import jax, jax.numpy as jnp
        import numpy as np
        N_NODES = 50000
        N_EDGES = 15625
        F_DIM = 128
        N_REL = 8
        N_LAYERS = 2
        NEG_SLOPE = 0.2

        def _segment_softmax(logits, seg, num_segments):
            m = jax.ops.segment_max(logits, seg, num_segments=num_segments)
            m = jax.lax.stop_gradient(m)
            e = jnp.exp(logits - m[seg])
            denom = jax.ops.segment_sum(e, seg, num_segments=num_segments)
            return e / (denom[seg] + 1e-16)

        def _rgat_layer(h, src, dst, edge_type, W, q, k, b):
            n = h.shape[0]
            xw = jnp.einsum('nf,rfg->rng', h, W)
            out_j = xw[edge_type, src]
            out_i = xw[edge_type, dst]
            logits = jax.nn.leaky_relu((out_i @ q + out_j @ k)[:, 0], NEG_SLOPE)
            alpha = _segment_softmax(logits, dst, n)
            agg = jax.ops.segment_sum(alpha[:, None] * out_j, dst, num_segments=n)
            return agg + b
        src, dst = (edge_index[0], edge_index[1])
        h = x
        for l in range(W.shape[0]):
            h = _rgat_layer(h, src, dst, edge_type, W[l], att_q[l], att_k[l], bias[l])
            h = jax.nn.relu(h)
        return h

    def _L1_gnn_ref(x, edge_index, W1, b1, g1, beta1, W2, b2, g2, beta2, W3, b3, g3, beta3):
        import jax, jax.numpy as jnp
        import numpy as np
        N_NODES = 50000
        N_EDGES = 25000
        EPS = 1e-05

        def _gcn_norm(edge_index, num_nodes):
            loop = jnp.arange(num_nodes, dtype=edge_index.dtype)
            src = jnp.concatenate([edge_index[0], loop])
            dst = jnp.concatenate([edge_index[1], loop])
            deg = jax.ops.segment_sum(jnp.ones_like(dst, dtype=jnp.float32), dst, num_segments=num_nodes)
            dinv = jnp.where(deg > 0, jax.lax.rsqrt(deg), 0.0)
            norm = dinv[src] * dinv[dst]
            return (src, dst, norm)

        def _gcn_conv(x, W, b, src, dst, norm, num_nodes):
            h = x @ W
            msg = h[src] * norm[:, None]
            out = jax.ops.segment_sum(msg, dst, num_segments=num_nodes)
            return out + b

        def _batch_norm(x, gamma, beta):
            mean = jnp.mean(x, axis=0)
            var = jnp.mean((x - mean) ** 2, axis=0)
            return (x - mean) * jax.lax.rsqrt(var + EPS) * gamma + beta
        n = x.shape[0]
        src, dst, norm = _gcn_norm(edge_index, n)
        h = _gcn_conv(x, W1, b1, src, dst, norm, n)
        h = _batch_norm(jax.nn.relu(h), g1, beta1)
        h = _gcn_conv(h, W2, b2, src, dst, norm, n)
        h = _batch_norm(jax.nn.relu(h), g2, beta2)
        h = _gcn_conv(h, W3, b3, src, dst, norm, n)
        return _batch_norm(h, g3, beta3)
    edge_index = jnp.stack([src, dst])
    x = _layernorm(x + _L0_gnn_ref(x, L0_gnn_W, L0_gnn_att_q, L0_gnn_att_k, L0_gnn_bias, edge_index, edge_type_8), axis=-1)
    x = _layernorm(x + _L1_gnn_ref(x, edge_index, L1_gnn_W1, L1_gnn_b1, L1_gnn_g1, L1_gnn_beta1, L1_gnn_W2, L1_gnn_b2, L1_gnn_g2, L1_gnn_beta2, L1_gnn_W3, L1_gnn_b3, L1_gnn_g3, L1_gnn_beta3), axis=-1)
    return x

_drawn_inputs = setup_inputs


def setup_inputs(seed=0):
    import zlib

    import numpy as np

    out = dict(_drawn_inputs(seed))
    spreads = {'L0_gnn_bias': (0.0, 0.1),
     'L1_gnn_b1': (0.0, 0.1),
     'L1_gnn_g1': (1.0, 0.2),
     'L1_gnn_beta1': (0.0, 0.1),
     'L1_gnn_b2': (0.0, 0.1),
     'L1_gnn_g2': (1.0, 0.2),
     'L1_gnn_beta2': (0.0, 0.1),
     'L1_gnn_b3': (0.0, 0.1),
     'L1_gnn_g3': (1.0, 0.2),
     'L1_gnn_beta3': (0.0, 0.1)}
    factors = {}
    for name, (base, spread) in spreads.items():
        noise = np.random.default_rng([zlib.crc32(name.encode()), seed]).standard_normal(out[name].shape)
        drawn = base * np.exp(spread * noise) if base else spread * noise
        out[name] = jnp.asarray(drawn.astype(out[name].dtype))
    for name, factor in factors.items():
        out[name] = (out[name] * factor).astype(out[name].dtype)
    return out
```

```python
from collections import namedtuple
from contextlib import ExitStack

import concourse.bass as bass
from concourse import mybir

F32 = mybir.dt.float32
BF16 = mybir.dt.bfloat16
I32 = mybir.dt.int32
ALU = mybir.AluOpType
ACT = mybir.ActivationFunctionType
AX_X = mybir.AxisListType.X

P = 128
EDGE_SPLIT = 125
GROUP = 256
TURN = 8
MASK_UNIT = 2.0 ** 100
NO_MAX = 1e25
FEW = -1e20
ROWS_RELATION = 24
ROWS = 29


LayerSignals = namedtuple("LayerSignals", "wt wts wqk wqks tr hts mm eva evb aip ait aits staged ais xd fd ld no nd pd cd "
                          "td ptd ud ad kd dd")
ConvSignals = namedtuple("ConvSignals", "y stored staged oh ud ad z tr trs mm act bn mm2 y2")


def at_least(engine, semaphore, value):
    if isinstance(value, int) and value <= 0:
        return
    engine.wait_ge(semaphore, value)


def gnn_kernel(nc, x, src, dst, edge_type, W, att_q, att_k, bias,
               W1, b1, g1, beta1, W2, b2, g2, beta2, W3, b3, g3, beta3, out):
    N, F = x.shape
    E = src.shape[0]
    L, R = W.shape[0], W.shape[1]
    NB = -(-N // P)
    FULL, REST = N // P, N % P
    NP = NB * P
    NG_NEEDED = (E + NB * (GROUP - 1)) // GROUP
    TURNS = -(-NG_NEEDED // TURN)
    NG = TURNS * TURN
    GC = -(-NG // P)
    SLOTS = GC * P
    EP = E + GROUP
    EC = E // EDGE_SPLIT
    ROW = F + 2
    NCH = [(o, min(512, NP - o)) for o in range(0, NP, 512)]
    EPS_LN = 1e-5
    EPS_BN = 1e-5
    assert F == P and E % EDGE_SPLIT == 0 and L == 2 and R == 8 and NG <= SLOTS

    def dram(name, shape, dt):
        return nc.dram_tensor(name, shape, dt, kind="Internal").ap()

    src_list = dram("src_list", (EP, 1), I32)
    dst_list = dram("dst_list", (EP, 1), I32)
    type_list = dram("type_list", (EP, 1), I32)
    edge_rows = dram("edge_rows", (ROWS, SLOTS * GROUP), BF16)
    group_block = dram("group_block", (1, SLOTS), I32)
    table = dram("table", (NP * R, ROW), F32)
    node_table = dram("node_table", (NP, F), F32)

    with ExitStack() as ctx:
        def sb(name, shape, dt=F32):
            return ctx.enter_context(nc.sbuf_tensor(name, shape, dt))

        def sem(name):
            return ctx.enter_context(nc.semaphore(name))

        bank = [ctx.enter_context(nc.psum_tensor(f"bank{i}", [P, 512], F32)) for i in range(8)]

        ident = sb("ident", [P, P])
        ident_b = sb("ident_b", [P, P], BF16)
        ones = sb("ones", [P, P])
        iota_row = sb("iota_row", [P, P])
        mask_w = sb("mask_w", [P, P], BF16)
        block_minus = sb("block_minus", [P, NB])
        group_id = sb("group_id", [P, GC])
        pad_i = sb("pad_i", [1, 2 * GROUP], I32)
        xN = sb("xN", [P, NB, F])
        hN = sb("hN", [P, NB, F])
        work = sb("work", [P, NB, F])
        acc = sb("acc", [P, NB + 1, ROW])
        hT = sb("hT", [P, NP])
        H1 = sb("H1", [P, 2, NP])
        dst_sp = sb("dst_sp", [EDGE_SPLIT, EC], I32)
        junk = sb("junk", [EDGE_SPLIT, EC])
        below = sb("below", [EDGE_SPLIT, NB + 1])
        start = sb("start", [P, NB + 1])
        nb_f = sb("nb_f", [P, NB])
        nb_i = sb("nb_i", [P, NB], I32)
        ge = sb("ge", [P, NB])
        gs = sb("gs", [P, NB])
        off = sb("off", [P, NB])
        ind = sb("ind", [P, GC, NB])
        t25 = sb("t25", [P, GC, NB])
        g256 = sb("g256", [P, GC])
        blk = sb("blk", [P, GC])
        blk128 = sb("blk128", [P, GC])
        blk_i = sb("blk_i", [P, GC], I32)
        offs = sb("offs", [P, GC])
        offs_i = sb("offs_i", [P, GC], I32)
        srcG = sb("srcG", [P, GC, GROUP], I32)
        dstG = sb("dstG", [P, GC, GROUP], I32)
        typG = sb("typG", [P, GC, GROUP], I32)
        fG = hT[:, 0:3 * GC * GROUP].rearrange("p (n c e) -> p n c e", n=3, e=GROUP)
        rowsG = H1[:, :, :].rearrange("p v n -> p (v n)").bitcast(BF16)[:, 0:(R + 4) * GC * GROUP].rearrange(
            "p (k e) -> p k e", e=GC * GROUP)
        sqf = sb("sqf", [P, GC * GROUP])
        sqi = sb("sqi", [P, 2, GC * GROUP], I32)
        row_col = sb("row_col", [P, SLOTS, 2], I32)
        src_col = sb("src_col", [P, SLOTS, 2], I32)
        place_col = sb("place_col", [P, SLOTS, 2])
        blk_row = sb("blk_row", [1, SLOTS + 16], I32)
        fresh = sb("fresh", [P, SLOTS])
        blk_bc = sb("blk_bc", [P, SLOTS + 1])
        deg = sb("deg", [P, NB + 1])
        dinv = sb("dinv", [P, NB])
        Wsb = sb("Wsb", [P, L, R, F])
        WT = sb("WT", [P, 2, F])
        qk = sb("qk", [P, L, 2])
        Wqk = sb("Wqk", [P, 2, R])
        bias_bc = sb("bias_bc", [P, L, F])
        W1sb = sb("W1sb", [P, 2 * F])
        W2sb = sb("W2sb", [P, 2, F])
        W3sb = sb("W3sb", [P, F])
        bn_par = sb("bn_par", [P, 3, 4])
        hTs = sb("hTs", [P, 2, P])
        rows_out = sb("rows_out", [P, 2, R, ROW])
        ai = sb("ai", [P, NB, R])
        ai_rest = sb("ai_rest", [P, NB, R])
        ai_parts = sb("ai_parts", [P, NB, 3 * R], BF16)
        aiT = sb("aiT", [P, NB + 1, P], BF16)
        stage = sb("stage", [P, 2, TURN], I32)
        msg = sb("msg", [P, TURN, 2, ROW])
        erows = sb("erows", [P, 2, TURN // 2 * GROUP], BF16)
        aiS = sb("aiS", [P, 2, P], BF16)
        logit = sb("logit", [P, 2, GROUP])
        prob = sb("prob", [P, 2, GROUP])
        probT = sb("probT", [P, 2, GROUP])
        neg_max = sb("neg_max", [P, 4])
        here = sb("here", [P, 4])
        lift = sb("lift", [P, 2, GROUP])
        neg_old = sb("neg_old", [P, 4])
        shrink = sb("shrink", [P, 4])
        cnt = sb("cnt", [P, 2])
        cjunk = sb("cjunk", [P, GROUP])
        onehot = sb("onehot", [P, 2, 2, P])
        stat = sb("stat", [P, 6, NB])
        bst = sb("bst", [P, 6, 2])
        part_id = sb("part_id", [P, 1])

        s_x, s_dst, s_w, s_par, s_lists = sem("s_x"), sem("s_dst"), sem("s_w"), sem("s_par"), sem("s_lists")
        s_zero, s_pad, s_iota = sem("s_zero"), sem("s_pad"), sem("s_iota")
        s_const, s_below, s_start, s_start_sb = sem("s_const"), sem("s_below"), sem("s_start"), sem("s_start_sb")
        s_offs, s_blk, s_blk_st, s_blk_ld = sem("s_offs"), sem("s_blk"), sem("s_blk_st"), sem("s_blk_ld")
        s_groups, s_rows, s_rows_st = sem("s_groups"), sem("s_rows"), sem("s_rows_st")
        s_fG, s_colT, s_col = sem("s_fG"), sem("s_colT"), sem("s_col")
        s_fresh, s_blkf = sem("s_fresh"), sem("s_blkf")
        dve_chain = sem("dve_chain")
        act_chain = sem("act_chain")
        act_turn, pool_turn, dve_turn = sem("act_turn"), sem("pool_turn"), sem("dve_turn")
        s_out = sem("s_out")
        sq_req, sq_done = sem("sq_req"), sem("sq_done")
        s_h = sem("s_h")

        LS = [LayerSignals(*(sem(f"L{l}_{name}") for name in LayerSignals._fields)) for l in range(L)]
        rows_stored = [[sem(f"L{l}_rows_stored{i}") for i in range(2)] for l in range(L)]
        gathered = [sem(f"gathered{k}") for k in range(TURN)]
        er_loaded = [sem(f"er_loaded{h}") for h in range(2)]

        CS = [ConvSignals(*(sem(f"C{c}_{name}") for name in ConvSignals._fields)) for c in range(3)]

        block = ctx.enter_context(nc.Block())

        @block.sync
        def _(sp):
            sp.dma_start(dst_sp[:, :], dst.rearrange("(p c) -> p c", p=EDGE_SPLIT)).then_inc(s_dst, 16)
            for whole, given in ((src_list, src), (dst_list, dst), (type_list, edge_type)):
                sp.dma_start(whole[0:E, :].rearrange("(p c) o -> p (c o)", p=EDGE_SPLIT),
                             given.rearrange("(p c) -> p c", p=EDGE_SPLIT)).then_inc(s_lists, 16)
            sp.wait_ge(s_pad, 2)
            for whole, o in ((src_list, 0), (dst_list, GROUP), (type_list, 0)):
                sp.dma_start(whole[E:EP, :].rearrange("c o -> o c"), pad_i[:, o:o + GROUP]).then_inc(s_lists, 16)
            sp.wait_ge(s_zero, 1)
            sp.dma_start(xN[:, 0:FULL, :], x[0:FULL * P, :].rearrange("(b p) f -> p b f", p=P)).then_inc(s_x, 16)
            sp.dma_start(xN[0:REST, FULL, :], x[FULL * P:N, :]).then_inc(s_x, 16)
            for l in range(L):
                sp.dma_start(Wsb[:, l, :, :], W[l].rearrange("r f g -> f r g")).then_inc(s_w, 16)
                sp.dma_start(qk[:, l, 0:1], att_q[l]).then_inc(s_w, 16)
                sp.dma_start(qk[:, l, 1:2], att_k[l]).then_inc(s_w, 16)
                sp.dma_start(bias_bc[:, l, :], bias[l].partition_broadcast(P)).then_inc(s_w, 16)
            sp.dma_start(W1sb[:, :], W1).then_inc(s_par, 16)
            sp.dma_start(W2sb[:, :, :], W2.rearrange("(c p) n -> p c n", p=P)).then_inc(s_par, 16)
            sp.dma_start(W3sb[:, :], W3).then_inc(s_par, 16)
            for i, (one, two, three) in enumerate(((b1, b2, b3), (g1, g2, g3), (beta1, beta2, beta3))):
                for c in range(2):
                    sp.dma_start(bn_par[:, i, c:c + 1], one[c * P:(c + 1) * P].rearrange("(p o) -> p o", o=1)).then_inc(s_par, 16)
                sp.dma_start(bn_par[:, i, 2:3], two.rearrange("(p o) -> p o", o=1)).then_inc(s_par, 16)
                sp.dma_start(bn_par[:, i, 3:4], three.rearrange("(p o) -> p o", o=1)).then_inc(s_par, 16)
            sp.wait_ge(s_blk, 1)
            with nc.allow_non_contiguous_dma(reason="512 numbers"):
                sp.dma_start(group_block.rearrange("o (c p) -> (o p) c", p=P), blk_i[:, :]).then_inc(s_blk_st, 16)
            sp.wait_ge(s_blk_st, 16)
            sp.dma_start(blk_row[:, 0:SLOTS], group_block).then_inc(s_blk_ld, 16)
            sp.wait_ge(s_rows, 1)
            for k in range(ROWS):
                i = k % R if k < ROWS_RELATION else R + (0 if k < 26 else k - 25)
                sp.dma_start(edge_rows[k:k + 1, :].rearrange("o (c p e) -> (o p) c e", p=P, e=GROUP),
                             rowsG[:, i, :].rearrange("p (c e) -> p c e", c=GC)).then_inc(s_rows_st, 16)
            for l in range(L):
                s = LS[l]
                for b in range(NB):
                    sp.wait_ge(s.eva, b + 1)
                    sp.wait_ge(s.evb, b + 1)
                    sp.dma_start(table[b * P * R:(b + 1) * P * R, :].rearrange("(p r) c -> p (r c)", p=P),
                                 rows_out[:, b % 2, :, :].rearrange("p r c -> p (r c)")).then_inc(rows_stored[l][b % 2], 16)
                sp.wait_ge(s_rows_st, 16 * ROWS)

                def load_rows(i, h):
                    sp.dma_start(erows[0:ROWS, h, :],
                                 edge_rows[:, bass.ds((i * TURN + h * (TURN // 2)) * GROUP, TURN // 2 * GROUP)]
                                 ).then_inc(er_loaded[h], 16)

                for h in range(2):
                    if l:
                        sp.wait_ge(LS[l - 1].xd, NG)
                    else:
                        sp.wait_ge(s_zero, 2)
                    load_rows(0, h)
                with sp.Fori(1, TURNS) as i:
                    for h in range(2):
                        sp.wait_ge(s.xd, (i - 1) * TURN + (h + 1) * (TURN // 2))
                        load_rows(i, h)
            for c in range(3):
                s = CS[c]
                sp.wait_ge(s.y, 1)
                sp.dma_start(node_table.rearrange("(b p) f -> p b f", p=P), work[:, :, :]).then_inc(s.stored, 16)
            sp.wait_ge(s_h, L + 1)
            sp.dma_start(out[0:FULL * P, :].rearrange("(b p) f -> p b f", p=P), hN[:, 0:FULL, :]).then_inc(s_out, 16)
            sp.dma_start(out[FULL * P:N, :], hN[0:REST, FULL, :]).then_inc(s_out, 16)
            sp.wait_ge(s_out, 32)

        @block.gpsimd
        def _(pool):
            pool.memset(pad_i[:, 0:GROUP], 0).then_inc(s_pad, 1)
            pool.memset(pad_i[:, GROUP:2 * GROUP], -1).then_inc(s_pad, 1)
            pool.memset(xN[:, FULL, :], 0.0).then_inc(s_zero, 1)
            pool.memset(erows[:, :, :], 0.0).then_inc(s_zero, 1)
            pool.iota(iota_row[:, :], pattern=[[1, P]], base=0, channel_multiplier=0,
                      allow_small_or_imprecise_dtypes=True).then_inc(s_iota, 1)
            pool.iota(block_minus[:, :], pattern=[[1, NB]], base=-NB, channel_multiplier=0,
                      allow_small_or_imprecise_dtypes=True).then_inc(s_iota, 1)
            pool.iota(group_id[:, :], pattern=[[P, GC]], base=0, channel_multiplier=1,
                      allow_small_or_imprecise_dtypes=True).then_inc(s_iota, 1)
            pool.iota(part_id[:, :], pattern=[[1, 1]], base=0, channel_multiplier=1,
                      allow_small_or_imprecise_dtypes=True).then_inc(s_iota, 1)
            pool.wait_ge(s_offs, 1)
            pool.wait_ge(s_lists, 16 * 6)
            for c in range(GC):
                for whole, there in ((src_list, srcG), (dst_list, dstG), (type_list, typG)):
                    pool.indirect_dma_start(there[:, c, :], None, whole,
                                            bass.IndirectOffsetOnAxis(ap=offs_i[:, c:c + 1], axis=0)).then_inc(s_groups, 16)

            def gathers(i, first, done, staged, index, source, width):
                for h in range(2):
                    if not first:
                        pool.wait_ge(done, (i - 1) * TURN + (h + 1) * (TURN // 2))
                        pool.sem_inc(pool_turn, 1)
                    pool.tensor_copy(stage[:, h, :], index[:, bass.ds(i * 2 * TURN + h * TURN, TURN)]).then_inc(staged, 1)
                    pool.wait_ge(staged, i * 2 + h + 1)
                    pool.sem_inc(pool_turn, 1)
                    for k in range(TURN // 2):
                        for t in range(2):
                            pool.indirect_dma_start(
                                msg[:, h * (TURN // 2) + k, t, 0:width], None, source,
                                bass.IndirectOffsetOnAxis(ap=stage[:, h, 2 * k + t:2 * k + t + 1], axis=0),
                            ).then_inc(gathered[h * (TURN // 2) + k], 16)

            def all_gathers(done, staged, index, source, width):
                gathers(0, True, done, staged, index, source, width)
                with pool.Fori(1, TURNS) as i:
                    gathers(i, False, done, staged, index, source, width)

            rows_flat = row_col[:, :, :].rearrange("p g t -> p (g t)")
            src_flat = src_col[:, :, :].rearrange("p g t -> p (g t)")
            pool.wait_ge(s_col, 6)
            for l in range(L):
                for i in range(2):
                    pool.wait_ge(rows_stored[l][i], 16 * ((NB + 1 - i) // 2))
                if l:
                    pool.wait_ge(LS[l - 1].ud, NG)
                all_gathers(LS[l].ud, LS[l].staged, rows_flat, table, ROW)
            for c in range(3):
                pool.wait_ge(CS[c].stored, 16)
                pool.wait_ge(CS[c - 1].ud if c else LS[L - 1].ud, NG)
                all_gathers(CS[c].ud, CS[c].staged, src_flat, node_table, F)

        @block.vector
        def _(dve):
            chain = [0]

            def link(ins):
                chain[0] += 1
                ins.then_inc(dve_chain, 1)
                dve.wait_ge(dve_chain, chain[0])

            dve.wait_ge(s_iota, 4)
            link(dve.memset(ones[:, :], 1.0))
            link(dve.tensor_tensor(sqf[:, 0:P], iota_row[:, :], iota_row[:, :], ALU.mult))
            link(dve.tensor_copy(sqi[:, 0, 0:P], sqf[:, 0:P]))
            link(dve.tensor_single_scalar(sqi[:, 1, 0:P], sqi[:, 0, 0:P], 255, ALU.bitwise_and))
            link(dve.tensor_copy(sqf[:, P:2 * P], sqi[:, 1, 0:P]))
            link(dve.tensor_tensor(sqf[:, 0:P], sqf[:, 0:P], sqf[:, P:2 * P], ALU.subtract))
            link(dve.memset(sqf[:, 2 * P:3 * P], 0.0))
            for row, part, weight in ((24, sqf[:, 0:P], -MASK_UNIT), (25, sqf[:, P:2 * P], -MASK_UNIT),
                                      (26, iota_row[:, :], 2 * MASK_UNIT), (27, ones[:, :], -MASK_UNIT),
                                      (28, ones[:, :], -MASK_UNIT)):
                link(dve.tensor_scalar(bst[:, 0, 0:1], part_id[:, 0:1], float(row), weight, ALU.is_equal, ALU.mult))
                link(dve.scalar_tensor_tensor(sqf[:, 2 * P:3 * P], part, bst[:, 0, 0:1], sqf[:, 2 * P:3 * P],
                                              ALU.mult, ALU.add))
            link(dve.tensor_copy(mask_w[:, :], sqf[:, 2 * P:3 * P]))
            link(dve.tensor_scalar(ident[:, :], iota_row[:, :], part_id[:, 0:1], None, ALU.is_equal))
            link(dve.tensor_copy(ident_b[:, :], ident[:, :]))
            link(dve.memset(rows_out[:, :, :, :], 1.0))
            link(dve.memset(aiT[:, :, :], 0.0))
            link(dve.memset(acc[:, :, :], 0.0))
            link(dve.memset(deg[:, :], 0.0))
            link(dve.memset(fresh[:, :], 0.0))
            dve.memset(blk_row[:, SLOTS:SLOTS + 16], 0).then_inc(s_const, 1)
            dve.wait_ge(s_dst, 16)
            for b in range(NB + 1):
                link(dve.tensor_scalar(junk[:, :], dst_sp[:, :], float(b * P), 0.0, ALU.is_lt, ALU.add,
                                       accum_out=below[:, b:b + 1]))
            dve.engine_nop().then_inc(s_below, 1)
            dve.wait_ge(s_start, 1)
            link(dve.tensor_copy(start[:, :], bank[0][:, 0:NB + 1]))
            link(dve.tensor_tensor(nb_f[:, :], start[:, 1:NB + 1], start[:, 0:NB], ALU.subtract))
            link(dve.tensor_scalar(nb_i[:, :], nb_f[:, :], float(GROUP - 1), None, ALU.add))
            link(dve.tensor_single_scalar(nb_i[:, :], nb_i[:, :], 8, ALU.arith_shift_right))
            link(dve.tensor_copy(nb_f[:, :], nb_i[:, :]))
            link(dve.tensor_tensor_scan(ge[:, :], ones[:, 0:NB], nb_f[:, :], 0.0, ALU.mult, ALU.add))
            link(dve.tensor_tensor(gs[:, :], ge[:, :], nb_f[:, :], ALU.subtract))
            link(dve.scalar_tensor_tensor(off[:, :], gs[:, :], -float(GROUP), start[:, 0:NB], ALU.mult, ALU.add))
            link(dve.tensor_scalar(off[:, :], off[:, :], -float(E), None, ALU.add))
            link(dve.tensor_scalar(g256[:, :], group_id[:, :], float(GROUP), None, ALU.mult))
            for c in range(GC):
                link(dve.tensor_scalar(t25[:, c, :], gs[:, :], group_id[:, c:c + 1], None, ALU.is_le))
                link(dve.scalar_tensor_tensor(ind[:, c, :], ge[:, :], group_id[:, c:c + 1], t25[:, c, :], ALU.is_gt, ALU.mult))
                link(dve.tensor_tensor(t25[:, c, :], ind[:, c, :], block_minus[:, :], ALU.mult))
                link(dve.tensor_reduce(blk[:, c:c + 1], t25[:, c, :], AX_X, ALU.add))
                link(dve.scalar_tensor_tensor(t25[:, c, :], off[:, :], g256[:, c:c + 1], ind[:, c, :], ALU.add, ALU.mult))
                link(dve.tensor_reduce(offs[:, c:c + 1], t25[:, c, :], AX_X, ALU.add))
            link(dve.tensor_scalar(offs_i[:, :], offs[:, :], float(E), None, ALU.add))
            link(dve.tensor_scalar(blk_i[:, :], blk[:, :], float(NB), None, ALU.add))
            link(dve.tensor_scalar(blk128[:, :], blk[:, :], float(NB), float(P), ALU.add, ALU.mult))
            dve.engine_nop().then_inc(s_offs, 1)
            dve.engine_nop().then_inc(s_blk, 1)
            dve.wait_ge(s_groups, 16 * 3 * GC)
            link(dve.scalar_tensor_tensor(fG[:, 0, :, :], srcG[:, :, :], float(R), typG[:, :, :], ALU.mult, ALU.add))
            link(dve.tensor_copy(fG[:, 1, :, :], srcG[:, :, :]))
            for c in range(GC):
                link(dve.tensor_scalar(fG[:, 2, c, :], dstG[:, c, :], blk128[:, c:c + 1], None, ALU.subtract))
            dve.engine_nop().then_inc(s_fG, 1)
            typ = typG[:, :, :].rearrange("p c e -> p (c e)")
            for r in range(R):
                link(dve.tensor_scalar(rowsG[:, r, :], typ, float(r), None, ALU.is_equal))
            link(dve.memset(rowsG[:, R, :], 1.0))
            place = fG[:, 2, :, :].rearrange("p c e -> p (c e)")
            link(dve.tensor_scalar(sqf[:, :], place, -64.0, 200.0, ALU.max, ALU.min))
            link(dve.tensor_copy(rowsG[:, R + 1, :], sqf[:, :]))
            link(dve.tensor_tensor(sqi[:, 0, :], sqf[:, :], sqf[:, :], ALU.mult))
            link(dve.tensor_single_scalar(sqi[:, 1, :], sqi[:, 0, :], 255, ALU.bitwise_and))
            link(dve.tensor_copy(rowsG[:, R + 3, :], sqi[:, 1, :]))
            link(dve.tensor_tensor(rowsG[:, R + 2, :], sqi[:, 0, :], sqi[:, 1, :], ALU.subtract))
            dve.engine_nop().then_inc(s_rows, 1)
            for n, (there, a) in enumerate(((row_col, 0), (src_col, 1), (place_col, 2))):
                for h in range(2):
                    dve.wait_ge(s_colT, 2 * n + h + 1)
                    link(dve.tensor_copy(there[:, :, h], bank[1 + 2 * n + h][:, 0:SLOTS]))
                    dve.engine_nop().then_inc(s_col, 1)
            dve.wait_ge(s_blk_ld, 16)
            link(dve.tensor_copy(blk_bc[0:1, 1:SLOTS + 1], blk_row[:, 0:SLOTS]))
            link(dve.memset(blk_bc[0:1, 0:1], -1.0))
            dve.tensor_tensor(fresh[0:1, :], blk_bc[0:1, 1:SLOTS + 1], blk_bc[0:1, 0:SLOTS],
                              ALU.not_equal).then_inc(s_blkf, 1)
            dve.wait_ge(s_fresh, 1)
            link(dve.tensor_scalar(fresh[:, :], bank[0][:, 0:SLOTS], 3e38, -3e38, ALU.mult, ALU.add))
            link(dve.scalar_tensor_tensor(fresh[:, :], bank[0][:, 0:SLOTS], NO_MAX, fresh[:, :], ALU.mult, ALU.add))
            dve.wait_ge(s_x, 32)
            dve.wait_ge(s_w, 16 * 4 * L)

            def blocks(first, count):
                return nc.values_load_multi_w_load_instructions(
                    blk_row[0:1, bass.ds(first, count)], engines=(mybir.EngineType.DVE,), min_val=0, max_val=NB,
                    skip_runtime_bounds_check_because="a group's block is 0 to NB by its construction")[1]

            def per_block(column):
                return column.unsqueeze(2).to_broadcast([P, NB, F])

            def square_root(n):
                dve.engine_nop().then_inc(sq_req, 1)
                dve.wait_ge(sq_done, n + 1)

            def layer_norm(buf, result, n):
                square = H1[:, 0, :].rearrange("p (b f) -> p b f", f=F)
                link(dve.tensor_reduce(stat[:, 0, :], buf[:, :, :], AX_X, ALU.add))
                link(dve.tensor_scalar(stat[:, 0, :], stat[:, 0, :], 1.0 / F, None, ALU.mult))
                link(dve.tensor_tensor(buf[:, :, :], buf[:, :, :], per_block(stat[:, 0, :]), ALU.subtract))
                link(dve.tensor_tensor(square, buf[:, :, :], buf[:, :, :], ALU.mult))
                link(dve.tensor_reduce(stat[:, 1, :], square, AX_X, ALU.add))
                link(dve.tensor_scalar(stat[:, 1, :], stat[:, 1, :], 1.0 / F, EPS_LN, ALU.mult, ALU.add))
                square_root(n)
                link(dve.reciprocal(stat[:, 2, :], stat[:, 1, :]))
                link(dve.tensor_tensor(result[:, :, :], buf[:, :, :], per_block(stat[:, 2, :]), ALU.mult))

            for l in range(L):
                s = LS[l]
                if l:
                    link(dve.memset(acc[:, :, :], 0.0))
                link(dve.memset(neg_max[:, :], NO_MAX))
                dve.engine_nop().then_inc(s_h, 1)
                for r in range(R):
                    dve.wait_ge(s.wt, r + 1)
                    if r >= 2:
                        dve.wait_ge(s.wqk, r - 1)
                    dve.tensor_copy(WT[:, r % 2, :], bank[6 + r % 2][:, 0:P]).then_inc(s.wts, 1)
                dve.wait_ge(s.wqk, R)
                dve.tensor_copy(Wqk[:, :, :], bank[5][:, 0:2 * R].rearrange("p (r o) -> p o r", o=2)).then_inc(s.wqks, 1)
                for b in range(NB):
                    dve.wait_ge(s.tr, b + 1)
                    if b >= 2:
                        dve.wait_ge(s.mm, b - 1)
                    dve.tensor_copy(hTs[:, b % 2, :], bank[6 + b % 2][:, 0:P]).then_inc(s.hts, 1)
                    dve.wait_ge(s.mm, b + 1)
                    if b >= 2:
                        dve.wait_ge(rows_stored[l][b % 2], 16 * (b // 2))
                    half = 3 * (b % 2)
                    link(dve.tensor_copy(rows_out[:, b % 2, R // 2:R, 0:F],
                                         bank[half + 1][:, :].rearrange("p (r f) -> p r f", f=F)))
                    link(dve.tensor_copy(rows_out[:, b % 2, :, F + 1], bank[half + 2][:, R:2 * R]))
                    dve.tensor_copy(ai[:, b, :], bank[half + 2][:, 0:R]).then_inc(s.evb, 1)
                dve.wait_ge(s.evb, NB)
                link(dve.tensor_copy(ai_parts[:, :, 0:R], ai[:, :, :]))
                link(dve.tensor_tensor(ai_rest[:, :, :], ai[:, :, :], ai_parts[:, :, 0:R], ALU.subtract))
                link(dve.tensor_copy(ai_parts[:, :, R:2 * R], ai_rest[:, :, :]))
                link(dve.tensor_tensor(ai_rest[:, :, :], ai_rest[:, :, :], ai_parts[:, :, R:2 * R], ALU.subtract))
                dve.tensor_copy(ai_parts[:, :, 2 * R:3 * R], ai_rest[:, :, :]).then_inc(s.aip, 1)

                def accumulate(g, k, b):
                    dve.wait_ge(s.ud, g + 1)
                    dve.wait_ge(s.cd, g + 1)
                    at_least(dve, s.ad, g)
                    dve.scalar_tensor_tensor(acc[:, bass.ds(b, 1), :].rearrange("p o c -> p (o c)"),
                                             acc[:, bass.ds(b, 1), :].rearrange("p o c -> p (o c)"),
                                             shrink[:, k % 4:k % 4 + 1],
                                             bank[4 + k % 2][:, 0:ROW], ALU.mult, ALU.add).then_inc(s.ad, 1)

                def move_probs(g, k):
                    dve.wait_ge(s.td, g + 1)
                    at_least(dve, s.ud, g - 1)
                    dve.tensor_copy(probT[:, k % 2, :], bank[2 + k % 2][:, 0:GROUP]).then_inc(s.ptd, 1)

                def maximum(g, k, b):
                    m, prev = k % 4, (k + 3) % 4
                    dve.wait_ge(s.fd, g + 1)
                    at_least(dve, s.pd, g - 1)
                    if l == 0:
                        at_least(dve, s.kd, g - 1)
                    dve.sem_inc(dve_turn, 1)
                    dve.tensor_tensor_reduce(logit[:, k % 2, :], bank[k % 2][:, 0:GROUP], lift[:, k % 2, :], 1.0, -3e38,
                                             ALU.add, ALU.max, here[:, m:m + 1]).then_inc(s.ld, 1)
                    at_least(dve, s.nd, g)
                    dve.tensor_tensor(neg_old[:, m:m + 1], neg_max[:, prev:prev + 1], fresh[:, bass.ds(g, 1)],
                                      ALU.max).then_inc(s.no, 1)
                    at_least(dve, s.cd, g - 3)
                    dve.wait_ge(s.ld, g + 1)
                    dve.wait_ge(s.no, g + 1)
                    dve.scalar_tensor_tensor(neg_max[:, m:m + 1], here[:, m:m + 1], -1.0, neg_old[:, m:m + 1],
                                             ALU.mult, ALU.min).then_inc(s.nd, 1)
                    if l == 0:
                        at_least(dve, s.dd, g)
                        dve.tensor_scalar(cjunk[:, :], logit[:, k % 2, :], FEW, 0.0, ALU.is_gt, ALU.add,
                                          accum_out=cnt[:, k % 2:k % 2 + 1]).then_inc(s.kd, 1)
                        dve.wait_ge(s.kd, g + 1)
                        dve.tensor_tensor(deg[:, bass.ds(b, 1)], deg[:, bass.ds(b, 1)], cnt[:, k % 2:k % 2 + 1],
                                          ALU.add).then_inc(s.dd, 1)

                def turn(i):
                    first = isinstance(i, int)
                    b = [None, None, *blocks(0, TURN)] if first else blocks(i * TURN - 2, TURN + 2)
                    for k in range(TURN):
                        g = i * TURN + k
                        if not first or k >= 2:
                            accumulate(g - 2, (k - 2) % TURN, b[k])
                        if not first or k >= 1:
                            move_probs(g - 1, (k - 1) % TURN)
                        maximum(g, k, b[k + 2])

                turn(0)
                with dve.Fori(1, TURNS) as i:
                    turn(i)
                b = blocks(NG - 2, 2)
                accumulate(NG - 2, TURN - 2, b[0])
                move_probs(NG - 1, TURN - 1)
                accumulate(NG - 1, TURN - 1, b[1])
                dve.wait_ge(s.ad, NG)
                link(dve.tensor_scalar(stat[:, 0, :], acc[:, 0:NB, F], 1e-16, None, ALU.add))
                link(dve.reciprocal(stat[:, 1, :], stat[:, 0, :]))
                link(dve.tensor_tensor(hN[:, :, :], acc[:, 0:NB, 0:F], per_block(stat[:, 1, :]), ALU.mult))
                link(dve.tensor_tensor(hN[:, :, :], hN[:, :, :], bias_bc[:, l, :].unsqueeze(1).to_broadcast([P, NB, F]), ALU.add))
                link(dve.tensor_scalar(hN[:, :, :], hN[:, :, :], 0.0, None, ALU.max))
            dve.wait_ge(LS[0].dd, NG)
            link(dve.tensor_tensor(hN[:, :, :], hN[:, :, :], xN[:, :, :], ALU.add))
            layer_norm(hN, xN, 0)
            link(dve.tensor_scalar(dinv[:, :], deg[:, 0:NB], 1.0, None, ALU.add))
            square_root(1)
            link(dve.reciprocal(dinv[:, :], dinv[:, :]))
            link(dve.tensor_tensor(work[:, :, :], xN[:, :, :], per_block(dinv[:, :]), ALU.mult))
            dve.wait_ge(s_par, 16 * 15)

            for c in range(3):
                s = CS[c]
                link(dve.memset(acc[:, :, :], 0.0))
                dve.engine_nop().then_inc(s.y, 1)

                def one_hots(g, k):
                    at_least(dve, s.ud, g - 1)
                    for t in range(2):
                        dve.tensor_scalar(onehot[:, k % 2, t, :], iota_row[:, :], place_flat[:, bass.ds(g * 2 + t, 1)],
                                          None, ALU.is_equal).then_inc(s.oh, 1)

                def add_sums(g, k, b):
                    dve.wait_ge(s.ud, g + 1)
                    at_least(dve, s.ad, g)
                    there = acc[:, bass.ds(b, 1), 0:F].rearrange("p o c -> p (o c)")
                    dve.tensor_tensor(there, there, bank[4 + k % 2][:, 0:F], ALU.add).then_inc(s.ad, 1)

                place_flat = place_col[:, :, :].rearrange("p g t -> p (g t)")

                def turn(i):
                    first = isinstance(i, int)
                    b = [None, *blocks(0, TURN)] if first else blocks(i * TURN - 1, TURN + 1)
                    for k in range(TURN):
                        g = i * TURN + k
                        one_hots(g, k)
                        if not first or k >= 1:
                            add_sums(g - 1, (k - 1) % TURN, b[k])

                turn(0)
                with dve.Fori(1, TURNS) as i:
                    turn(i)
                add_sums(NG - 1, TURN - 1, blocks(NG - 1, 2)[0])
                dve.wait_ge(s.ad, NG)
                dve.wait_ge(s.stored, 16)
                link(dve.tensor_tensor(hN[:, :, :], acc[:, 0:NB, 0:F], work[:, :, :], ALU.add))
                link(dve.tensor_tensor(hN[:, :, :], hN[:, :, :], per_block(dinv[:, :]), ALU.mult))
                dve.engine_nop().then_inc(s.z, 1)
                halves = 2 if c == 0 else 1
                if c == 0:
                    for q, (o, n) in enumerate(NCH):
                        dve.wait_ge(s.tr, q + 1)
                        dve.tensor_copy(hT[:, o:o + n], bank[q % 2][:, 0:n]).then_inc(s.trs, 1)
                dve.wait_ge(s.act, halves * len(NCH))
                for v in range(halves):
                    link(dve.tensor_reduce(bst[:, 0, v:v + 1], H1[:, v, 0:N], AX_X, ALU.add))
                    link(dve.tensor_scalar(bst[:, 0, v:v + 1], bst[:, 0, v:v + 1], 1.0 / N, None, ALU.mult))
                    link(dve.tensor_scalar(H1[:, v, :], H1[:, v, :], bst[:, 0, v:v + 1], None, ALU.subtract))
                    link(dve.tensor_tensor(hT[:, 0:N], H1[:, v, 0:N], H1[:, v, 0:N], ALU.mult))
                    link(dve.tensor_reduce(bst[:, 1, v:v + 1], hT[:, 0:N], AX_X, ALU.add))
                link(dve.tensor_scalar(bst[:, 1, 0:halves], bst[:, 1, 0:halves], 1.0 / N, EPS_BN, ALU.mult, ALU.add))
                square_root(2 + c)
                link(dve.reciprocal(bst[:, 2, 0:halves], bst[:, 1, 0:halves]))
                col = 0 if c == 0 else c + 1
                link(dve.tensor_tensor(bst[:, 2, 0:halves], bst[:, 2, 0:halves], bn_par[:, 1, col:col + halves], ALU.mult))
                for v in range(halves):
                    link(dve.tensor_scalar(H1[:, v, :], H1[:, v, :], bst[:, 2, v:v + 1],
                                           bn_par[:, 2, col + v:col + v + 1], ALU.mult, ALU.add))
                dve.engine_nop().then_inc(s.bn, 1)
                for q, (o, n) in enumerate(NCH):
                    dve.wait_ge(s.mm2, q + 1)
                    b0, nb = o // F, n // F
                    got = bank[6 + q % 2][:, 0:n].rearrange("p (b f) -> p b f", f=F)
                    if c < 2:
                        dve.tensor_tensor(work[:, b0:b0 + nb, :], got,
                                          dinv[:, b0:b0 + nb].unsqueeze(2).to_broadcast([P, nb, F]), ALU.mult).then_inc(s.y2, 1)
                    else:
                        dve.tensor_tensor(hN[:, b0:b0 + nb, :], got, xN[:, b0:b0 + nb, :], ALU.add).then_inc(s.y2, 1)
                dve.wait_ge(s.y2, len(NCH))
            layer_norm(hN, hN, 5)
            dve.engine_nop().then_inc(s_h, 1)

        @block.scalar
        def _(act):
            def blocks(first, count):
                return nc.values_load_multi_w_load_instructions(
                    blk_row[0:1, bass.ds(first, count)], engines=(mybir.EngineType.Activation,), min_val=0, max_val=NB,
                    skip_runtime_bounds_check_because="a group's block is 0 to NB by its construction")[1]

            act.wait_ge(s_const, 1)
            act.wait_ge(s_blk_ld, 16)
            for l in range(L):
                s = LS[l]
                for b in range(NB):
                    act.wait_ge(s.mm, b + 1)
                    if b >= 2:
                        act.wait_ge(rows_stored[l][b % 2], 16 * (b // 2))
                    act.activation(rows_out[:, b % 2, 0:R // 2, 0:F],
                                   bank[3 * (b % 2)][:, :].rearrange("p (r f) -> p r f", f=F), ACT.Copy).then_inc(s.eva, 1)
                if l:
                    act.wait_ge(LS[l - 1].ais, NG + 1)
                act.wait_ge(s.ait, 1)
                for j in range(-(-NB // 8)):
                    nb = min(8, NB - 8 * j)
                    act.activation(aiT[0:ROWS_RELATION, 8 * j:8 * j + nb, :],
                                   bank[j][0:ROWS_RELATION, :].bitcast(BF16)[:, 0:nb * P].rearrange("p (b f) -> p b f", f=P),
                                   ACT.Copy).then_inc(s.aits, 1)
                act.wait_ge(s.aits, -(-NB // 8))

                def stage_ai(g, k, b):
                    at_least(act, s.xd, g - 1)
                    act.sem_inc(act_turn, 1)
                    act.activation(aiS[:, k % 2, :], aiT[:, bass.ds(b, 1), :].rearrange("p o d -> p (o d)"),
                                   ACT.Copy).then_inc(s.ais, 1)

                def exps(g, k):
                    m = k % 4
                    act.wait_ge(s.nd, g + 1)
                    at_least(act, s.td, g - 1)
                    act.activation(prob[:, k % 2, :], logit[:, k % 2, :], ACT.Exp, bias=neg_max[:, m:m + 1]).then_inc(s.pd, 1)
                    at_least(act, s.ad, g - 3)
                    act.activation(shrink[:, m:m + 1], neg_old[:, m:m + 1], ACT.Exp, bias=neg_max[:, m:m + 1],
                                   scale=-1.0).then_inc(s.cd, 1)

                def lifts(g, k):
                    act.wait_ge(s.xd, g + 1)
                    at_least(act, s.ld, g - 1)
                    act.activation(lift[:, k % 2, :], bank[k % 2][:, 0:GROUP], ACT.Relu, scale=-0.8).then_inc(s.fd, 1)

                def turn(i):
                    first = isinstance(i, int)
                    b = blocks(i * TURN + 1, TURN)
                    for k in range(TURN):
                        g = i * TURN + k
                        if not first or k >= 1:
                            exps(g - 1, (k - 1) % TURN)
                        stage_ai(g + 1, (k + 1) % TURN, b[k])
                        lifts(g, k)

                stage_ai(0, 0, blocks(0, 2)[0])
                turn(0)
                with act.Fori(1, TURNS) as i:
                    turn(i)
                exps(NG - 1, TURN - 1)

            def square_root(n, what):
                act.wait_ge(sq_req, n + 1)
                act.activation(what, what, ACT.Sqrt).then_inc(sq_done, 1)

            square_root(0, stat[:, 1, :])
            square_root(1, dinv[:, :])
            act.wait_ge(s_par, 16 * 15)
            for c in range(3):
                s = CS[c]
                col = 0 if c == 0 else c + 1
                func = ACT.Relu if c < 2 else ACT.Identity
                if c == 0:
                    for n, (v, (o, w)) in enumerate((v, ch) for v in range(2) for ch in NCH):
                        act.wait_ge(s.mm, n + 1)
                        act.activation(H1[:, v, o:o + w], bank[2 + n % 4][:, 0:w], func,
                                       bias=bn_par[:, 0, v:v + 1]).then_inc(s.act, 1)
                else:
                    for q, (o, w) in enumerate(NCH):
                        act.wait_ge(s.tr, q + 1)
                        act.activation(H1[:, 0, o:o + w], bank[q % 2][:, 0:w], func,
                                       bias=bn_par[:, 0, col:col + 1]).then_inc(s.act, 1)
                square_root(2 + c, bst[:, 1, 0:2 if c == 0 else 1])
            square_root(5, stat[:, 1, :])

        @block.tensor
        def _(pe):
            pe.wait_ge(s_const, 1)
            pe.wait_ge(s_below, 1)
            pe.matmul(bank[0][:, 0:NB + 1], ones[0:EDGE_SPLIT, :], below[:, :], start=True, stop=True).then_inc(s_start, 1)
            pe.wait_ge(s_fG, 1)
            for n in range(3):
                for h in range(2):
                    for c in range(GC):
                        ins = pe.transpose(bank[1 + 2 * n + h][:, c * P:(c + 1) * P], fG[:, n, c, h * P:(h + 1) * P], ident[:, :])
                    ins.then_inc(s_colT, 1)
            pe.wait_ge(s_blkf, 1)
            pe.matmul(bank[0][:, 0:SLOTS], ones[0:1, :], fresh[0:1, :], start=True, stop=True).then_inc(s_fresh, 1)

            for l in range(L):
                s = LS[l]
                h = xN if l == 0 else hN
                loads = 32 * TURNS * l
                row_loads = 16 * TURNS * l
                pe.wait_ge(s_h, l + 1)
                for r in range(R):
                    if r >= 2:
                        pe.wait_ge(s.wts, r - 1)
                    pe.transpose(bank[6 + r % 2][:, 0:P], Wsb[:, l, r, :], ident[:, :]).then_inc(s.wt, 1)
                    pe.wait_ge(s.wts, r + 1)
                    pe.matmul(bank[5][:, 2 * r:2 * r + 2], WT[:, r % 2, :], qk[:, l, :], start=True, stop=True).then_inc(s.wqk, 1)

                def transpose_block(b):
                    if b >= 2:
                        pe.wait_ge(s.hts, b - 1)
                    pe.transpose(bank[6 + b % 2][:, 0:P], h[:, b, :], ident[:, :]).then_inc(s.tr, 1)

                transpose_block(0)
                pe.wait_ge(s.wqks, 1)
                for b in range(NB):
                    if b + 1 < NB:
                        transpose_block(b + 1)
                    pe.wait_ge(s.hts, b + 1)
                    if b >= 2:
                        pe.wait_ge(s.eva, b - 1)
                        pe.wait_ge(s.evb, b - 1)
                    half = 3 * (b % 2)
                    for j in range(2):
                        pe.matmul(bank[half + j][:, :], hTs[:, b % 2, :],
                                  Wsb[:, l, j * (R // 2):(j + 1) * (R // 2), :].rearrange("p r f -> p (r f)"), start=True, stop=True)
                    pe.matmul(bank[half + 2][:, 0:2 * R], hTs[:, b % 2, :], Wqk[:, :, :].rearrange("p o r -> p (o r)"),
                              start=True, stop=True).then_inc(s.mm, 1)
                pe.wait_ge(s.aip, 1)
                pe.wait_ge(s.eva, NB)
                for b in range(NB):
                    there = bank[b // 8][0:ROWS_RELATION, :].bitcast(BF16)
                    ins = pe.transpose(there[:, (b % 8) * P:(b % 8 + 1) * P], ai_parts[:, b, :], ident_b[:, :])
                ins.then_inc(s.ait, 1)
                pe.wait_ge(s.aits, -(-NB // 8))

                def logits(g, k, i):
                    hb = k // (TURN // 2)
                    pe.wait_ge(s.ais, g + 1)
                    at_least(pe, s.ld, g - 1)
                    pe.wait_ge(er_loaded[hb], row_loads + 16 * (i + 1))
                    there = bank[k % 2]
                    cols = erows[:, hb, (k % (TURN // 2)) * GROUP:(k % (TURN // 2) + 1) * GROUP]
                    pe.matmul(there[:, 0:GROUP], mask_w[:, :], cols, start=True, stop=False)
                    pe.matmul(there[:, 0:GROUP], aiS[:, k % 2, :], cols, start=False, stop=False)
                    pe.wait_ge(gathered[k], loads + 32 * (i + 1))
                    for t in range(2):
                        ins = pe.matmul(there[:, t * P:(t + 1) * P], msg[:, k, t, F + 1:F + 2].to_broadcast([P, P]), ident[:, :],
                                        start=False, stop=(t == 1))
                    ins.then_inc(s.xd, 1)

                def turn_probs(g, k):
                    pe.wait_ge(s.pd, g + 1)
                    at_least(pe, s.ptd, g - 1)
                    for t in range(2):
                        ins = pe.transpose(bank[2 + k % 2][:, t * P:(t + 1) * P], prob[:, k % 2, t * P:(t + 1) * P], ident[:, :])
                    ins.then_inc(s.td, 1)

                def sums(g, k):
                    pe.wait_ge(s.ptd, g + 1)
                    at_least(pe, s.ad, g - 1)
                    for t in range(2):
                        ins = pe.matmul(bank[4 + k % 2][:, 0:ROW], probT[:, k % 2, t * P:(t + 1) * P], msg[:, k, t, :],
                                        start=(t == 0), stop=(t == 1))
                    ins.then_inc(s.ud, 1)

                def turn(i):
                    first = isinstance(i, int)
                    for k in range(TURN):
                        g = i * TURN + k
                        logits(g, k, i)
                        if not first or k >= 2:
                            sums(g - 2, (k - 2) % TURN)
                        if not first or k >= 1:
                            turn_probs(g - 1, (k - 1) % TURN)

                turn(0)
                with pe.Fori(1, TURNS) as i:
                    turn(i)
                sums(NG - 2, TURN - 2)
                turn_probs(NG - 1, TURN - 1)
                sums(NG - 1, TURN - 1)

            for c in range(3):
                s = CS[c]
                loads = 32 * TURNS * (L + c)

                def conv_sums(g, k, i):
                    pe.wait_ge(s.oh, 2 * g + 2)
                    at_least(pe, s.ad, g - 1)
                    pe.wait_ge(gathered[k], loads + 32 * (i + 1))
                    for t in range(2):
                        ins = pe.matmul(bank[4 + k % 2][:, 0:F], onehot[:, k % 2, t, :], msg[:, k, t, 0:F],
                                        start=(t == 0), stop=(t == 1))
                    ins.then_inc(s.ud, 1)

                for k in range(TURN):
                    conv_sums(k, k, 0)
                with pe.Fori(1, TURNS) as i:
                    for k in range(TURN):
                        conv_sums(i * TURN + k, k, i)
                pe.wait_ge(s.z, 1)
                for q, (o, n) in enumerate(NCH):
                    if q >= 2:
                        pe.wait_ge(s.trs if c == 0 else s.act, q - 1)
                    for j in range(n // P):
                        ins = pe.transpose(bank[q % 2][:, j * P:(j + 1) * P], hN[:, o // P + j, :], ident[:, :])
                    ins.then_inc(s.tr, 1)
                if c == 0:
                    pe.wait_ge(s.trs, len(NCH))
                    for m, (v, (o, n)) in enumerate((v, ch) for v in range(2) for ch in NCH):
                        if m >= 4:
                            pe.wait_ge(s.act, m - 3)
                        pe.matmul(bank[2 + m % 4][:, 0:n], W1sb[:, v * P:(v + 1) * P], hT[:, o:o + n],
                                  start=True, stop=True).then_inc(s.mm, 1)
                pe.wait_ge(s.bn, 1)
                for q, (o, n) in enumerate(NCH):
                    if q >= 2:
                        pe.wait_ge(s.y2, q - 1)
                    for j in range(n // P):
                        there = bank[6 + q % 2][:, j * P:(j + 1) * P]
                        nodes = slice(o + j * P, o + (j + 1) * P)
                        if c == 0:
                            for v in range(2):
                                ins = pe.matmul(there, H1[:, v, nodes], W2sb[:, v, :], start=(v == 0), stop=(v == 1))
                        elif c == 1:
                            ins = pe.matmul(there, H1[:, 0, nodes], W3sb[:, :], start=True, stop=True)
                        else:
                            ins = pe.transpose(there, H1[:, 0, nodes], ident[:, :])
                    ins.then_inc(s.mm2, 1)


_INS = ["x", "src", "dst", "edge_type_8", "L0_gnn_W", "L0_gnn_att_q", "L0_gnn_att_k", "L0_gnn_bias",
        "L1_gnn_W1", "L1_gnn_b1", "L1_gnn_g1", "L1_gnn_beta1", "L1_gnn_W2", "L1_gnn_b2", "L1_gnn_g2", "L1_gnn_beta2",
        "L1_gnn_W3", "L1_gnn_b3", "L1_gnn_g3", "L1_gnn_beta3"]


def kernel(**inputs):
    import numpy as _np
    import concourse.bacc as _bacc
    from concourse import mybir as _mybir
    from concourse.bass_utils import run_bass_kernel_spmd as _run

    nc = _bacc.Bacc("TRN2", target_bir_lowering=False, num_devices=1)
    arrays, args = {}, []
    for name in _INS:
        a = _np.ascontiguousarray(inputs[name])
        arrays[f"in_{name}_dram"] = a
        args.append(nc.dram_tensor(f"in_{name}_dram", a.shape, _mybir.dt.from_np(a.dtype), kind="ExternalInput").ap())
    out = nc.dram_tensor("out_0_dram", inputs["x"].shape, _mybir.dt.float32, kind="ExternalOutput").ap()
    gnn_kernel(nc, *args, out)
    r = _run(nc, [arrays], core_ids=[0])
    return r.results[0]["out_0_dram"]
```

```python
from collections import namedtuple
from contextlib import ExitStack

import concourse.bass as bass
from concourse import mybir

F32 = mybir.dt.float32
BF16 = mybir.dt.bfloat16
I32 = mybir.dt.int32
ALU = mybir.AluOpType
ACT = mybir.ActivationFunctionType
AX_X = mybir.AxisListType.X

P = 128
EDGE_SPLIT = 125
GROUP = 256
TURN = 8
WINDOW = 8
TILES_PER_GROUP = 3
COUNT_RING = 8
MASK_UNIT = 2.0 ** 100
NO_MAX = 1e25
FEW = -1e20
ROWS_RELATION = 24
ROWS = 29


LayerSignals = namedtuple("LayerSignals", "wt wts wqk wqks tr hts mm eva evb aip ait aits staged ais xd fd ld no nd pd cd "
                          "td ptd ud ad kd dd oh cm rn")
ConvSignals = namedtuple("ConvSignals", "y ud ev tr trs mm act bn mm2 y2")


def at_least(engine, semaphore, value):
    if isinstance(value, int) and value <= 0:
        return
    engine.wait_ge(semaphore, value)


def gnn_kernel(nc, x, src, dst, edge_type, W, att_q, att_k, bias,
               W1, b1, g1, beta1, W2, b2, g2, beta2, W3, b3, g3, beta3, out):
    N, F = x.shape
    E = src.shape[0]
    L, R = W.shape[0], W.shape[1]
    NB = -(-N // P)
    FULL, REST = N // P, N % P
    NP = NB * P
    NG_NEEDED = (E + NB * (GROUP - 1)) // GROUP
    TURNS = -(-NG_NEEDED // TURN)
    NG = TURNS * TURN
    GC = -(-NG // P)
    SLOTS = GC * P
    EP = E + GROUP
    EC = E // EDGE_SPLIT
    ROW = F + 2
    WPB = P // WINDOW
    WINS = NB * WPB
    TILES = TILES_PER_GROUP * NG
    TC = -(-TILES // P)
    KEYS = WINDOW * NB
    SHIFT = 7
    assert E // P + WINS <= TILES and KEYS <= 256
    NCH = [(o, min(512, NP - o)) for o in range(0, NP, 512)]
    EPS_LN = 1e-5
    EPS_BN = 1e-5
    assert F == P and E % EDGE_SPLIT == 0 and L == 2 and R == 8 and NG <= SLOTS

    def dram(name, shape, dt):
        return nc.dram_tensor(name, shape, dt, kind="Internal").ap()

    src_list = dram("src_list", (EP, 1), I32)
    dst_list = dram("dst_list", (EP, 1), I32)
    type_list = dram("type_list", (EP, 1), I32)
    edge_rows = dram("edge_rows", (ROWS, SLOTS * GROUP), BF16)
    group_block = dram("group_block", (1, SLOTS), I32)
    table = dram("table", (NP * R, ROW), F32)
    tile_window = dram("tile_window", (1, TC * P), I32)
    counts = dram("counts", (WINS + COUNT_RING, P, KEYS), F32)

    with ExitStack() as ctx:
        def sb(name, shape, dt=F32):
            return ctx.enter_context(nc.sbuf_tensor(name, shape, dt))

        def sem(name):
            return ctx.enter_context(nc.semaphore(name))

        bank = [ctx.enter_context(nc.psum_tensor(f"bank{i}", [P, 512], F32)) for i in range(8)]

        ident = sb("ident", [P, P])
        ident_b = sb("ident_b", [P, P], BF16)
        ones = sb("ones", [P, P])
        iota_row = sb("iota_row", [P, P])
        mask_w = sb("mask_w", [P, P], BF16)
        block_minus = sb("block_minus", [P, NB])
        group_id = sb("group_id", [P, GC])
        pad_i = sb("pad_i", [1, 2 * GROUP], I32)
        xN = sb("xN", [P, NB, F])
        hN = sb("hN", [P, NB, F])
        work = sb("work", [P, NB, F])
        COUNTS_IN = 3 * WPB * KEYS
        ACC, TCP, OUT2 = (NB + 1) * ROW, TC * P, 2 * R * ROW
        shared = sb("shared", [P, max(COUNTS_IN, ACC + 3 * TCP + OUT2)])
        count_in = shared[:, 0:COUNTS_IN].rearrange("p (i w k) -> p i w k", i=3, k=KEYS)
        acc_flat = shared[:, 0:ACC]
        acc = acc_flat.rearrange("p (b c) -> p b c", c=ROW)
        keep, key_col, low_col = (shared[:, ACC + n * TCP:ACC + (n + 1) * TCP] for n in range(3))
        rows_out = shared[:, ACC + 3 * TCP:ACC + 3 * TCP + OUT2].rearrange("p (i r c) -> p i r c", i=2, c=ROW)
        win = acc_flat[:, 0:7 * WINS].rearrange("p (n w) -> p n w", w=WINS)
        sqi = acc_flat[:, 0:2 * GC * GROUP].bitcast(I32).rearrange("p (n e) -> p n e", n=2)
        hN_flat = hN[:, :, :].rearrange("p b f -> p (b f)")
        dst_sp = hN_flat[0:EDGE_SPLIT, 0:EC].bitcast(I32)
        junk = hN_flat[0:EDGE_SPLIT, EC:2 * EC]
        sqf = hN_flat[:, 2 * EC:2 * EC + GC * GROUP]
        hT = sb("hT", [P, NP])
        H1 = sb("H1", [P, 2, NP])
        below = sb("below", [EDGE_SPLIT, NB + 1])
        start = sb("start", [P, NB + 1])
        nb_f = sb("nb_f", [P, NB])
        nb_i = sb("nb_i", [P, NB], I32)
        ge = sb("ge", [P, NB])
        gs = sb("gs", [P, NB])
        off = sb("off", [P, NB])
        ind = sb("ind", [P, GC, NB])
        t25 = sb("t25", [P, GC, NB])
        g256 = sb("g256", [P, GC])
        blk = sb("blk", [P, GC])
        blk128 = sb("blk128", [P, GC])
        blk_i = sb("blk_i", [P, GC], I32)
        offs = sb("offs", [P, GC])
        offs_i = sb("offs_i", [P, GC], I32)
        fG = hT[:, 0:2 * GC * GROUP].rearrange("p (n c e) -> p n c e", n=2, e=GROUP)
        rowsG = H1[:, :, :].rearrange("p v n -> p (v n)").bitcast(BF16)[:, 0:(R + 4) * GC * GROUP].rearrange(
            "p (k e) -> p k e", e=GC * GROUP)
        srcG, dstG, typG = (work[:, :, :].rearrange("p b f -> p (b f)")[:, n * GC * GROUP:(n + 1) * GC * GROUP].bitcast(
            I32).rearrange("p (c e) -> p c e", c=GC) for n in range(3))
        row_col = sb("row_col", [P, SLOTS, 2], I32)
        blk_row = sb("blk_row", [1, SLOTS + 16], I32)
        fresh = sb("fresh", [P, SLOTS])
        blk_bc = sb("blk_bc", [P, SLOTS + 1])
        deg = sb("deg", [P, NB + 1])
        iota_keys = sb("iota_keys", [P, max(WINS, KEYS)])
        iota_b = sb("iota_b", [P, KEYS], BF16)
        in_window = sb("in_window", [P, WPB])
        tile_id = sb("tile_id", [P, TC])
        win_i = sb("win_i", [P, WINS], I32)
        tile_num = sb("tile_num", [P, 6, TC])
        tile_off = sb("tile_off", [P, TC], I32)
        tile_dest = sb("tile_dest", [P, TC], I32)
        dest_row = sb("dest_row", [1, TC * P], I32)
        oh_low = sb("oh_low", [P, 2 * TILES_PER_GROUP, P], BF16)
        oh_key = sb("oh_key", [P, 2 * TILES_PER_GROUP, KEYS], BF16)
        running = sb("running", [P, COUNT_RING, KEYS])
        dinv = sb("dinv", [P, NB])
        Wsb = sb("Wsb", [P, L, R, F])
        WT = sb("WT", [P, 2, F])
        qk = sb("qk", [P, L, 2])
        Wqk = sb("Wqk", [P, 2, R])
        bias_bc = sb("bias_bc", [P, L, F])
        W1sb = sb("W1sb", [P, 2 * F])
        W2sb = sb("W2sb", [P, 2, F])
        W3sb = sb("W3sb", [P, F])
        bn_par = sb("bn_par", [P, 3, 4])
        H1_flat = H1[:, :, :].rearrange("p v n -> p (v n)")

        def tile_array(n, dt=F32):
            a = H1_flat[:, n * TC * P:(n + 1) * TC * P]
            return (a.bitcast(dt) if dt != F32 else a).rearrange("p (c e) -> p c e", e=P)

        srcT, dstT, highT = (tile_array(n, I32) for n in range(3))
        keyT, lowT = (tile_array(n) for n in (3, 4))
        placeT = hT[:, 0:TC * P].rearrange("p (c e) -> p c e", e=P)
        validT = hT[:, TC * P:2 * TC * P].rearrange("p (c e) -> p c e", e=P)
        hTs = sb("hTs", [P, 2, P])
        ai = sb("ai", [P, NB, R])
        ai_rest = sb("ai_rest", [P, NB, R])
        ai_parts = sb("ai_parts", [P, NB, 3 * R], BF16)
        aiT = sb("aiT", [P, NB + 1, P], BF16)
        stage = sb("stage", [P, 2, TURN], I32)
        msg = sb("msg", [P, TURN, 2, ROW])
        erows = sb("erows", [P, 2, TURN // 2 * GROUP], BF16)
        aiS = sb("aiS", [P, 2, P], BF16)
        logit = sb("logit", [P, 2, GROUP])
        prob = sb("prob", [P, 2, GROUP])
        probT = sb("probT", [P, 2, GROUP])
        neg_max = sb("neg_max", [P, 4])
        here = sb("here", [P, 4])
        lift = sb("lift", [P, 2, GROUP])
        neg_old = sb("neg_old", [P, 4])
        shrink = sb("shrink", [P, 4])
        cnt = sb("cnt", [P, 2])
        cjunk = sb("cjunk", [P, GROUP])
        stat = sb("stat", [P, 6, NB])
        bst = sb("bst", [P, 6, 2])
        part_id = sb("part_id", [P, 1])

        s_x, s_dst, s_w, s_par, s_lists = sem("s_x"), sem("s_dst"), sem("s_w"), sem("s_par"), sem("s_lists")
        s_zero, s_pad, s_iota = sem("s_zero"), sem("s_pad"), sem("s_iota")
        s_const, s_below, s_start, s_start_sb = sem("s_const"), sem("s_below"), sem("s_start"), sem("s_start_sb")
        s_offs, s_blk, s_blk_st, s_blk_ld = sem("s_offs"), sem("s_blk"), sem("s_blk_st"), sem("s_blk_ld")
        s_groups, s_rows, s_rows_st = sem("s_groups"), sem("s_rows"), sem("s_rows_st")
        s_fG, s_colT, s_col = sem("s_fG"), sem("s_colT"), sem("s_col")
        s_fresh, s_blkf = sem("s_fresh"), sem("s_blkf")
        dve_chain = sem("dve_chain")
        act_chain = sem("act_chain")
        act_turn, pool_turn, dve_turn = sem("act_turn"), sem("pool_turn"), sem("dve_turn")
        s_out = sem("s_out")
        s_win_deg, s_win_n, s_tiles, s_keep, s_keep_bc = (sem(n) for n in ("s_win_deg", "s_win_n", "s_tiles", "s_keep", "s_keep_bc"))
        s_dest_st, s_dest_ld, s_tile_edges, s_keys, s_keyT = (
            sem(n) for n in ("s_dest_st", "s_dest_ld", "s_tile_edges", "s_keys", "s_keyT"))
        counted = [sem(f"counted{i}") for i in range(COUNT_RING)]
        counts_in = [sem(f"counts_in{i}") for i in range(3)]
        sq_req, sq_done = sem("sq_req"), sem("sq_done")
        s_h = sem("s_h")

        LS = [LayerSignals(*(None if name in unused else sem(f"L{l}_{name}") for name in LayerSignals._fields)) for l, unused in ((0, ("oh", "cm", "rn")), (1, ("kd", "dd")))]
        rows_stored = [[sem(f"L{l}_rows_stored{i}") for i in range(2)] for l in range(L)]
        gathered = [sem(f"gathered{k}") for k in range(TURN)]
        er_loaded = [sem(f"er_loaded{h}") for h in range(2)]

        CS = [ConvSignals(*(None if c and name in ("trs", "mm") else sem(f"C{c}_{name}") for name in ConvSignals._fields))
              for c in range(3)]

        block = ctx.enter_context(nc.Block())

        @block.sync
        def _(sp):
            sp.dma_start(dst_sp[:, :], dst.rearrange("(p c) -> p c", p=EDGE_SPLIT)).then_inc(s_dst, 16)
            for whole, given in ((src_list, src), (dst_list, dst), (type_list, edge_type)):
                sp.dma_start(whole[0:E, :].rearrange("(p c) o -> p (c o)", p=EDGE_SPLIT),
                             given.rearrange("(p c) -> p c", p=EDGE_SPLIT)).then_inc(s_lists, 16)
            sp.wait_ge(s_pad, 2)
            for whole, o in ((src_list, 0), (dst_list, GROUP), (type_list, 0)):
                sp.dma_start(whole[E:EP, :].rearrange("c o -> o c"), pad_i[:, o:o + GROUP]).then_inc(s_lists, 16)
            sp.wait_ge(s_zero, 1)
            sp.dma_start(xN[:, 0:FULL, :], x[0:FULL * P, :].rearrange("(b p) f -> p b f", p=P)).then_inc(s_x, 16)
            sp.dma_start(xN[0:REST, FULL, :], x[FULL * P:N, :]).then_inc(s_x, 16)
            for l in range(L):
                sp.dma_start(Wsb[:, l, :, :], W[l].rearrange("r f g -> f r g")).then_inc(s_w, 16)
                sp.dma_start(qk[:, l, 0:1], att_q[l]).then_inc(s_w, 16)
                sp.dma_start(qk[:, l, 1:2], att_k[l]).then_inc(s_w, 16)
                sp.dma_start(bias_bc[:, l, :], bias[l].partition_broadcast(P)).then_inc(s_w, 16)
            sp.dma_start(W1sb[:, :], W1).then_inc(s_par, 16)
            sp.dma_start(W2sb[:, :, :], W2.rearrange("(c p) n -> p c n", p=P)).then_inc(s_par, 16)
            sp.dma_start(W3sb[:, :], W3).then_inc(s_par, 16)
            for i, (one, two, three) in enumerate(((b1, b2, b3), (g1, g2, g3), (beta1, beta2, beta3))):
                for c in range(2):
                    sp.dma_start(bn_par[:, i, c:c + 1], one[c * P:(c + 1) * P].rearrange("(p o) -> p o", o=1)).then_inc(s_par, 16)
                sp.dma_start(bn_par[:, i, 2:3], two.rearrange("(p o) -> p o", o=1)).then_inc(s_par, 16)
                sp.dma_start(bn_par[:, i, 3:4], three.rearrange("(p o) -> p o", o=1)).then_inc(s_par, 16)
            sp.wait_ge(s_blk, 1)
            with nc.allow_non_contiguous_dma(reason="512 numbers"):
                sp.dma_start(group_block.rearrange("o (c p) -> (o p) c", p=P), blk_i[:, :]).then_inc(s_blk_st, 16)
            sp.wait_ge(s_blk_st, 16)
            sp.dma_start(blk_row[:, 0:SLOTS], group_block).then_inc(s_blk_ld, 16)
            sp.wait_ge(s_rows, 1)
            for k in range(ROWS):
                i = k % R if k < ROWS_RELATION else R + (0 if k < 26 else k - 25)
                sp.dma_start(edge_rows[k:k + 1, :].rearrange("o (c p e) -> (o p) c e", p=P, e=GROUP),
                             rowsG[:, i, :].rearrange("p (c e) -> p c e", c=GC)).then_inc(s_rows_st, 16)
            for l in range(L):
                s = LS[l]
                for b in range(NB):
                    sp.wait_ge(s.eva, b + 1)
                    sp.wait_ge(s.evb, b + 1)
                    sp.dma_start(table[b * P * R:(b + 1) * P * R, :].rearrange("(p r) c -> p (r c)", p=P),
                                 rows_out[:, b % 2, :, :].rearrange("p r c -> p (r c)")).then_inc(rows_stored[l][b % 2], 16)
                sp.wait_ge(s_rows_st, 16 * ROWS)

                def load_rows(i, h):
                    sp.dma_start(erows[0:ROWS, h, :],
                                 edge_rows[:, bass.ds((i * TURN + h * (TURN // 2)) * GROUP, TURN // 2 * GROUP)]
                                 ).then_inc(er_loaded[h], 16)

                for h in range(2):
                    if l:
                        sp.wait_ge(LS[l - 1].xd, NG)
                    else:
                        sp.wait_ge(s_zero, 2)
                    load_rows(0, h)
                HALF = TILES_PER_GROUP * TURN // 2

                def store_counts(i, h):
                    dests = nc.values_load_multi_w_load_instructions(
                        dest_row[0:1, bass.ds((2 * i + h) * HALF, HALF)], engines=(mybir.EngineType.SP,),
                        min_val=0, max_val=WINS + COUNT_RING - 1,
                        skip_runtime_bounds_check_because="a window, or a spare place by the tile's number")[1]
                    for j in range(HALF):
                        tile = (2 * i + h) * HALF + j
                        k = (h * HALF + j) % COUNT_RING
                        sp.wait_ge(s.rn, tile + 1)
                        sp.dma_start(counts[bass.ds(dests[j], 1), :, :].rearrange("w p k -> (w p) k"),
                                     running[:, k, :]).then_inc(counted[k], 16)

                if l:
                    sp.wait_ge(s_dest_ld, 16)
                with sp.Fori(1, TURNS) as i:
                    for h in range(2):
                        if l:
                            store_counts(i - 1, h)
                        sp.wait_ge(s.xd, (i - 1) * TURN + (h + 1) * (TURN // 2))
                        load_rows(i, h)
                if l:
                    for h in range(2):
                        store_counts(TURNS - 1, h)
                else:
                    sp.wait_ge(s_tiles, 1)
                    with nc.allow_non_contiguous_dma(reason="1280 numbers"):
                        sp.dma_start(tile_window.rearrange("o (c p) -> (o p) c", p=P), tile_dest[:, :]).then_inc(s_dest_st, 16)
                    sp.wait_ge(s_dest_st, 16)
                    sp.dma_start(dest_row[:, :], tile_window).then_inc(s_dest_ld, 16)
            for k in range(COUNT_RING):
                sp.wait_ge(counted[k], 16 * TILES // COUNT_RING)

            sp.wait_ge(CS[0].y, 1)

            def load_counts(c, b, k):
                if not isinstance(b, int) or b >= 3:
                    sp.wait_ge(CS[c].ud, b - 2)
                elif c:
                    sp.wait_ge(CS[c - 1].ud, NB)
                sp.dma_start(count_in[:, k, :, :], counts[bass.ds(b * WPB, WPB), :, :].rearrange("w p k -> p w k")
                             ).then_inc(counts_in[k], 16)

            for c in range(3):
                for b in range(3):
                    load_counts(c, b, b)
                with sp.Fori(1, NB // 3) as i:
                    for k in range(3):
                        load_counts(c, 3 * i + k, k)
                for b in range(NB // 3 * 3, NB):
                    load_counts(c, b, b % 3)
            sp.wait_ge(s_h, L + 1)
            sp.dma_start(out[0:FULL * P, :].rearrange("(b p) f -> p b f", p=P), hN[:, 0:FULL, :]).then_inc(s_out, 16)
            sp.dma_start(out[FULL * P:N, :], hN[0:REST, FULL, :]).then_inc(s_out, 16)
            sp.wait_ge(s_out, 32)

        @block.gpsimd
        def _(pool):
            pool.memset(pad_i[:, 0:GROUP], 0).then_inc(s_pad, 1)
            pool.memset(pad_i[:, GROUP:2 * GROUP], -1).then_inc(s_pad, 1)
            pool.memset(xN[:, FULL, :], 0.0).then_inc(s_zero, 1)
            pool.memset(erows[:, :, :], 0.0).then_inc(s_zero, 1)
            pool.iota(iota_row[:, :], pattern=[[1, P]], base=0, channel_multiplier=0,
                      allow_small_or_imprecise_dtypes=True).then_inc(s_iota, 1)
            pool.iota(block_minus[:, :], pattern=[[1, NB]], base=-NB, channel_multiplier=0,
                      allow_small_or_imprecise_dtypes=True).then_inc(s_iota, 1)
            pool.iota(group_id[:, :], pattern=[[P, GC]], base=0, channel_multiplier=1,
                      allow_small_or_imprecise_dtypes=True).then_inc(s_iota, 1)
            pool.iota(part_id[:, :], pattern=[[1, 1]], base=0, channel_multiplier=1,
                      allow_small_or_imprecise_dtypes=True).then_inc(s_iota, 1)
            pool.iota(iota_keys[:, :], pattern=[[1, max(WINS, KEYS)]], base=0, channel_multiplier=0,
                      allow_small_or_imprecise_dtypes=True).then_inc(s_iota, 1)
            pool.iota(tile_id[:, :], pattern=[[P, TC]], base=0, channel_multiplier=1,
                      allow_small_or_imprecise_dtypes=True).then_inc(s_iota, 1)
            pool.wait_ge(s_offs, 1)
            pool.wait_ge(s_lists, 16 * 6)
            for c in range(GC):
                for whole, there in ((src_list, srcG), (dst_list, dstG), (type_list, typG)):
                    pool.indirect_dma_start(there[:, c, :], None, whole,
                                            bass.IndirectOffsetOnAxis(ap=offs_i[:, c:c + 1], axis=0)).then_inc(s_groups, 16)

            def gathers(i, first, done, staged, index, source, width):
                for h in range(2):
                    if not first:
                        pool.wait_ge(done, (i - 1) * TURN + (h + 1) * (TURN // 2))
                        pool.sem_inc(pool_turn, 1)
                    pool.tensor_copy(stage[:, h, :], index[:, bass.ds(i * 2 * TURN + h * TURN, TURN)]).then_inc(staged, 1)
                    pool.wait_ge(staged, i * 2 + h + 1)
                    pool.sem_inc(pool_turn, 1)
                    for k in range(TURN // 2):
                        for t in range(2):
                            pool.indirect_dma_start(
                                msg[:, h * (TURN // 2) + k, t, 0:width], None, source,
                                bass.IndirectOffsetOnAxis(ap=stage[:, h, 2 * k + t:2 * k + t + 1], axis=0),
                            ).then_inc(gathered[h * (TURN // 2) + k], 16)

            def all_gathers(done, staged, index, source, width):
                gathers(0, True, done, staged, index, source, width)
                with pool.Fori(1, TURNS) as i:
                    gathers(i, False, done, staged, index, source, width)

            rows_flat = row_col[:, :, :].rearrange("p g t -> p (g t)")
            pool.wait_ge(s_col, 2)
            for l in range(L):
                for i in range(2):
                    pool.wait_ge(rows_stored[l][i], 16 * ((NB + 1 - i) // 2))
                if l:
                    pool.wait_ge(LS[l - 1].ud, NG)
                all_gathers(LS[l].ud, LS[l].staged, rows_flat, table, ROW)
                if l == 0:
                    pool.wait_ge(s_tiles, 1)
                    for c in range(TC):
                        for whole, there in ((src_list, srcT), (dst_list, dstT)):
                            pool.indirect_dma_start(there[:, c, :], None, whole,
                                                    bass.IndirectOffsetOnAxis(ap=tile_off[:, c:c + 1], axis=0)
                                                    ).then_inc(s_tile_edges, 16)

        @block.vector
        def _(dve):
            chain = [0]

            def link(ins):
                chain[0] += 1
                ins.then_inc(dve_chain, 1)
                dve.wait_ge(dve_chain, chain[0])

            dve.wait_ge(s_iota, 6)
            link(dve.memset(ones[:, :], 1.0))
            link(dve.tensor_tensor(sqf[:, 0:P], iota_row[:, :], iota_row[:, :], ALU.mult))
            link(dve.tensor_copy(sqi[:, 0, 0:P], sqf[:, 0:P]))
            link(dve.tensor_single_scalar(sqi[:, 1, 0:P], sqi[:, 0, 0:P], 255, ALU.bitwise_and))
            link(dve.tensor_copy(sqf[:, P:2 * P], sqi[:, 1, 0:P]))
            link(dve.tensor_tensor(sqf[:, 0:P], sqf[:, 0:P], sqf[:, P:2 * P], ALU.subtract))
            link(dve.memset(sqf[:, 2 * P:3 * P], 0.0))
            for row, part, weight in ((24, sqf[:, 0:P], -MASK_UNIT), (25, sqf[:, P:2 * P], -MASK_UNIT),
                                      (26, iota_row[:, :], 2 * MASK_UNIT), (27, ones[:, :], -MASK_UNIT),
                                      (28, ones[:, :], -MASK_UNIT)):
                link(dve.tensor_scalar(bst[:, 0, 0:1], part_id[:, 0:1], float(row), weight, ALU.is_equal, ALU.mult))
                link(dve.scalar_tensor_tensor(sqf[:, 2 * P:3 * P], part, bst[:, 0, 0:1], sqf[:, 2 * P:3 * P],
                                              ALU.mult, ALU.add))
            link(dve.tensor_copy(mask_w[:, :], sqf[:, 2 * P:3 * P]))
            link(dve.tensor_scalar(ident[:, :], iota_row[:, :], part_id[:, 0:1], None, ALU.is_equal))
            link(dve.tensor_copy(ident_b[:, :], ident[:, :]))
            link(dve.tensor_copy(iota_b[:, :], iota_keys[:, 0:KEYS]))
            link(dve.tensor_scalar(win[:, 0, 0:WPB], iota_keys[:, 0:WPB], float(WINDOW), None, ALU.mult))
            link(dve.tensor_scalar(win[:, 1, 0:WPB], win[:, 0, 0:WPB], part_id[:, 0:1], None, ALU.is_le))
            link(dve.tensor_scalar(win[:, 2, 0:1], part_id[:, 0:1], -float(WINDOW), None, ALU.add))
            link(dve.scalar_tensor_tensor(in_window[:, :], win[:, 0, 0:WPB], win[:, 2, 0:1], win[:, 1, 0:WPB], ALU.is_gt, ALU.mult))
            link(dve.memset(running[:, :, :], 0.0))
            link(dve.memset(rows_out[:, :, :, :], 1.0))
            link(dve.memset(aiT[:, :, :], 0.0))
            link(dve.memset(deg[:, :], 0.0))
            link(dve.memset(fresh[:, :], 0.0))
            dve.memset(blk_row[:, SLOTS:SLOTS + 16], 0).then_inc(s_const, 1)
            dve.wait_ge(s_dst, 16)
            for b in range(NB + 1):
                link(dve.tensor_scalar(junk[:, :], dst_sp[:, :], float(b * P), 0.0, ALU.is_lt, ALU.add,
                                       accum_out=below[:, b:b + 1]))
            dve.engine_nop().then_inc(s_below, 1)
            dve.wait_ge(s_start, 1)
            link(dve.tensor_copy(start[:, :], bank[0][:, 0:NB + 1]))
            link(dve.tensor_tensor(nb_f[:, :], start[:, 1:NB + 1], start[:, 0:NB], ALU.subtract))
            link(dve.tensor_scalar(nb_i[:, :], nb_f[:, :], float(GROUP - 1), None, ALU.add))
            link(dve.tensor_single_scalar(nb_i[:, :], nb_i[:, :], 8, ALU.arith_shift_right))
            link(dve.tensor_copy(nb_f[:, :], nb_i[:, :]))
            link(dve.tensor_tensor_scan(ge[:, :], ones[:, 0:NB], nb_f[:, :], 0.0, ALU.mult, ALU.add))
            link(dve.tensor_tensor(gs[:, :], ge[:, :], nb_f[:, :], ALU.subtract))
            link(dve.scalar_tensor_tensor(off[:, :], gs[:, :], -float(GROUP), start[:, 0:NB], ALU.mult, ALU.add))
            link(dve.tensor_scalar(off[:, :], off[:, :], -float(E), None, ALU.add))
            link(dve.tensor_scalar(g256[:, :], group_id[:, :], float(GROUP), None, ALU.mult))
            for c in range(GC):
                link(dve.tensor_scalar(t25[:, c, :], gs[:, :], group_id[:, c:c + 1], None, ALU.is_le))
                link(dve.scalar_tensor_tensor(ind[:, c, :], ge[:, :], group_id[:, c:c + 1], t25[:, c, :], ALU.is_gt, ALU.mult))
                link(dve.tensor_tensor(t25[:, c, :], ind[:, c, :], block_minus[:, :], ALU.mult))
                link(dve.tensor_reduce(blk[:, c:c + 1], t25[:, c, :], AX_X, ALU.add))
                link(dve.scalar_tensor_tensor(t25[:, c, :], off[:, :], g256[:, c:c + 1], ind[:, c, :], ALU.add, ALU.mult))
                link(dve.tensor_reduce(offs[:, c:c + 1], t25[:, c, :], AX_X, ALU.add))
            link(dve.tensor_scalar(offs_i[:, :], offs[:, :], float(E), None, ALU.add))
            link(dve.tensor_scalar(blk_i[:, :], blk[:, :], float(NB), None, ALU.add))
            link(dve.tensor_scalar(blk128[:, :], blk[:, :], float(NB), float(P), ALU.add, ALU.mult))
            dve.engine_nop().then_inc(s_offs, 1)
            dve.engine_nop().then_inc(s_blk, 1)
            dve.wait_ge(s_groups, 16 * 3 * GC)
            link(dve.scalar_tensor_tensor(fG[:, 0, :, :], srcG[:, :, :], float(R), typG[:, :, :], ALU.mult, ALU.add))
            for c in range(GC):
                link(dve.tensor_scalar(fG[:, 1, c, :], dstG[:, c, :], blk128[:, c:c + 1], None, ALU.subtract))
            dve.engine_nop().then_inc(s_fG, 1)
            typ = typG[:, :, :].rearrange("p c e -> p (c e)")
            for r in range(R):
                link(dve.tensor_scalar(rowsG[:, r, :], typ, float(r), None, ALU.is_equal))
            link(dve.memset(rowsG[:, R, :], 1.0))
            place = fG[:, 1, :, :].rearrange("p c e -> p (c e)")
            link(dve.tensor_scalar(sqf[:, :], place, -64.0, 200.0, ALU.max, ALU.min))
            link(dve.tensor_copy(rowsG[:, R + 1, :], sqf[:, :]))
            link(dve.tensor_tensor(sqi[:, 0, :], sqf[:, :], sqf[:, :], ALU.mult))
            link(dve.tensor_single_scalar(sqi[:, 1, :], sqi[:, 0, :], 255, ALU.bitwise_and))
            link(dve.tensor_copy(rowsG[:, R + 3, :], sqi[:, 1, :]))
            link(dve.tensor_tensor(rowsG[:, R + 2, :], sqi[:, 0, :], sqi[:, 1, :], ALU.subtract))
            dve.engine_nop().then_inc(s_rows, 1)
            for h in range(2):
                dve.wait_ge(s_colT, h + 1)
                link(dve.tensor_copy(row_col[:, :, h], bank[1 + h][:, 0:SLOTS]))
                dve.engine_nop().then_inc(s_col, 1)
            dve.wait_ge(s_blk_ld, 16)
            link(dve.tensor_copy(blk_bc[0:1, 1:SLOTS + 1], blk_row[:, 0:SLOTS]))
            link(dve.memset(blk_bc[0:1, 0:1], -1.0))
            dve.tensor_tensor(fresh[0:1, :], blk_bc[0:1, 1:SLOTS + 1], blk_bc[0:1, 0:SLOTS],
                              ALU.not_equal).then_inc(s_blkf, 1)
            dve.wait_ge(s_fresh, 1)
            link(dve.tensor_scalar(fresh[:, :], bank[0][:, 0:SLOTS], 3e38, -3e38, ALU.mult, ALU.add))
            link(dve.scalar_tensor_tensor(fresh[:, :], bank[0][:, 0:SLOTS], NO_MAX, fresh[:, :], ALU.mult, ALU.add))
            dve.wait_ge(s_x, 32)
            dve.wait_ge(s_w, 16 * 4 * L)

            def blocks(first, count):
                return nc.values_load_multi_w_load_instructions(
                    blk_row[0:1, bass.ds(first, count)], engines=(mybir.EngineType.DVE,), min_val=0, max_val=NB,
                    skip_runtime_bounds_check_because="a group's block is 0 to NB by its construction")[1]

            def per_block(column):
                return column.unsqueeze(2).to_broadcast([P, NB, F])

            def square_root(n):
                dve.engine_nop().then_inc(sq_req, 1)
                dve.wait_ge(sq_done, n + 1)

            def layer_norm(buf, result, n):
                square = H1[:, 0, :].rearrange("p (b f) -> p b f", f=F)
                link(dve.tensor_reduce(stat[:, 0, :], buf[:, :, :], AX_X, ALU.add))
                link(dve.tensor_scalar(stat[:, 0, :], stat[:, 0, :], 1.0 / F, None, ALU.mult))
                link(dve.tensor_tensor(buf[:, :, :], buf[:, :, :], per_block(stat[:, 0, :]), ALU.subtract))
                link(dve.tensor_tensor(square, buf[:, :, :], buf[:, :, :], ALU.mult))
                link(dve.tensor_reduce(stat[:, 1, :], square, AX_X, ALU.add))
                link(dve.tensor_scalar(stat[:, 1, :], stat[:, 1, :], 1.0 / F, EPS_LN, ALU.mult, ALU.add))
                square_root(n)
                link(dve.reciprocal(stat[:, 2, :], stat[:, 1, :]))
                link(dve.tensor_tensor(result[:, :, :], buf[:, :, :], per_block(stat[:, 2, :]), ALU.mult))

            def tiles_of_windows():
                n_win, start_w, n_tiles, end_t, first_t, off_w, t = (win[:, i, :] for i in range(7))
                one_row = ones[:, 0:1].to_broadcast([P, WINS])
                link(dve.tensor_tensor(win[:, 6, :].rearrange("p (b w) -> p b w", w=WPB),
                                       deg[:, 0:NB].unsqueeze(2).to_broadcast([P, NB, WPB]),
                                       in_window[:, :].unsqueeze(1).to_broadcast([P, NB, WPB]), ALU.mult))
                dve.engine_nop().then_inc(s_win_deg, 1)
                dve.wait_ge(s_win_n, 1)
                link(dve.tensor_copy(n_win, bank[0][:, 0:WINS]))
                link(dve.tensor_tensor_scan(start_w, one_row, n_win, 0.0, ALU.mult, ALU.add))
                link(dve.tensor_tensor(start_w, start_w, n_win, ALU.subtract))
                link(dve.tensor_scalar(win_i[:, :], n_win, float(P - 1), None, ALU.add))
                link(dve.tensor_single_scalar(win_i[:, :], win_i[:, :], SHIFT, ALU.arith_shift_right))
                link(dve.tensor_scalar(n_tiles, win_i[:, :], 1.0, None, ALU.max))
                link(dve.tensor_tensor_scan(end_t, one_row, n_tiles, 0.0, ALU.mult, ALU.add))
                link(dve.tensor_tensor(first_t, end_t, n_tiles, ALU.subtract))
                link(dve.scalar_tensor_tensor(off_w, first_t, -float(P), start_w, ALU.mult, ALU.add))
                link(dve.tensor_scalar(off_w, off_w, -float(E), None, ALU.add))
                link(dve.tensor_scalar(tile_num[:, 5, :], tile_id[:, :], float(P), None, ALU.mult))
                for c in range(TC):
                    link(dve.tensor_scalar(t, first_t, tile_id[:, c:c + 1], None, ALU.is_le))
                    link(dve.scalar_tensor_tensor(n_win, end_t, tile_id[:, c:c + 1], t, ALU.is_gt, ALU.mult))
                    for n, (a, scalar, op) in enumerate(((iota_keys[:, 0:WINS], 1.0, ALU.mult), (off_w, tile_num[:, 5, c:c + 1], ALU.add),
                                                         (end_t, 1.0, ALU.mult), (first_t, 1.0, ALU.mult))):
                        link(dve.scalar_tensor_tensor(t, a, scalar, n_win, op, ALU.mult, accum_out=tile_num[:, n, c:c + 1]))
                window, first_edge, end, first, last, _ = (tile_num[:, n, :] for n in range(6))
                link(dve.tensor_scalar(tile_off[:, :], first_edge, float(E), None, ALU.add))
                link(dve.tensor_scalar(last, tile_id[:, :], 1.0, None, ALU.add))
                link(dve.tensor_tensor(last, last, end, ALU.is_equal))
                spare = win[:, 6, 0:TC]
                link(dve.tensor_copy(win_i[:, 0:1], part_id[:, 0:1]))
                link(dve.tensor_single_scalar(win_i[:, 0:1], win_i[:, 0:1], COUNT_RING - 1, ALU.bitwise_and))
                link(dve.tensor_scalar(win[:, 5, 0:1], win_i[:, 0:1], float(WINS), None, ALU.add))
                link(dve.tensor_scalar(spare, window, win[:, 5, 0:1], None, ALU.subtract))
                link(dve.tensor_tensor(spare, spare, last, ALU.mult))
                link(dve.tensor_scalar(tile_dest[:, :], spare, win[:, 5, 0:1], None, ALU.add))
                dve.engine_nop().then_inc(s_tiles, 1)
                link(dve.tensor_tensor(first, first, tile_id[:, :], ALU.not_equal))
                link(dve.tensor_tensor(keyT, ident[:, :].unsqueeze(1).to_broadcast([P, TC, P]),
                                       first.unsqueeze(2).to_broadcast([P, TC, P]), ALU.mult))
                dve.engine_nop().then_inc(s_keep, 1)
                for n in range(-(-TC // 4)):
                    w = min(4, TC - 4 * n) * P
                    dve.wait_ge(s_keep_bc, 1)
                    link(dve.tensor_copy(keep[:, 512 * n:512 * n + w], bank[1 + n][:, 0:w]))
                dve.wait_ge(s_tile_edges, 16 * 2 * TC)
                link(dve.tensor_scalar(window, window, float(WINDOW), None, ALU.mult))
                link(dve.tensor_tensor(placeT, dstT, window.unsqueeze(2).to_broadcast([P, TC, P]), ALU.subtract))
                link(dve.tensor_scalar(validT, placeT, 0.0, float(WINDOW - 1), ALU.max, ALU.min))
                link(dve.tensor_tensor(validT, validT, placeT, ALU.is_equal))
                link(dve.tensor_single_scalar(highT, srcT, SHIFT, ALU.arith_shift_right))
                link(dve.scalar_tensor_tensor(keyT, placeT, float(NB), highT, ALU.mult, ALU.add))
                link(dve.scalar_tensor_tensor(keyT, keyT, 1.0, validT, ALU.add, ALU.mult))
                link(dve.tensor_scalar(keyT, keyT, -1.0, None, ALU.add))
                link(dve.tensor_single_scalar(highT, srcT, P - 1, ALU.bitwise_and))
                link(dve.tensor_copy(lowT, highT))
                dve.engine_nop().then_inc(s_keys, 1)
                dve.wait_ge(s_keyT, 1)
                for n in range(-(-TC // 4)):
                    w = min(4, TC - 4 * n) * P
                    link(dve.tensor_copy(key_col[:, 512 * n:512 * n + w], bank[1 + n][:, 0:w]))
                    link(dve.tensor_copy(low_col[:, 512 * n:512 * n + w], bank[4 + n][:, 0:w]))

            for l in range(L):
                s = LS[l]
                if l:
                    tiles_of_windows()
                link(dve.memset(acc_flat, 0.0))
                link(dve.memset(neg_max[:, :], NO_MAX))
                dve.engine_nop().then_inc(s_h, 1)
                for r in range(R):
                    dve.wait_ge(s.wt, r + 1)
                    if r >= 2:
                        dve.wait_ge(s.wqk, r - 1)
                    dve.tensor_copy(WT[:, r % 2, :], bank[6 + r % 2][:, 0:P]).then_inc(s.wts, 1)
                dve.wait_ge(s.wqk, R)
                dve.tensor_copy(Wqk[:, :, :], bank[5][:, 0:2 * R].rearrange("p (r o) -> p o r", o=2)).then_inc(s.wqks, 1)
                for b in range(NB):
                    dve.wait_ge(s.tr, b + 1)
                    if b >= 2:
                        dve.wait_ge(s.mm, b - 1)
                    dve.tensor_copy(hTs[:, b % 2, :], bank[6 + b % 2][:, 0:P]).then_inc(s.hts, 1)
                    dve.wait_ge(s.mm, b + 1)
                    if b >= 2:
                        dve.wait_ge(rows_stored[l][b % 2], 16 * (b // 2))
                    half = 3 * (b % 2)
                    link(dve.tensor_copy(rows_out[:, b % 2, R // 2:R, 0:F],
                                         bank[half + 1][:, :].rearrange("p (r f) -> p r f", f=F)))
                    link(dve.tensor_copy(rows_out[:, b % 2, :, F + 1], bank[half + 2][:, R:2 * R]))
                    dve.tensor_copy(ai[:, b, :], bank[half + 2][:, 0:R]).then_inc(s.evb, 1)
                dve.wait_ge(s.evb, NB)
                link(dve.tensor_copy(ai_parts[:, :, 0:R], ai[:, :, :]))
                link(dve.tensor_tensor(ai_rest[:, :, :], ai[:, :, :], ai_parts[:, :, 0:R], ALU.subtract))
                link(dve.tensor_copy(ai_parts[:, :, R:2 * R], ai_rest[:, :, :]))
                link(dve.tensor_tensor(ai_rest[:, :, :], ai_rest[:, :, :], ai_parts[:, :, R:2 * R], ALU.subtract))
                dve.tensor_copy(ai_parts[:, :, 2 * R:3 * R], ai_rest[:, :, :]).then_inc(s.aip, 1)

                def accumulate(g, k, b):
                    dve.wait_ge(s.ud, g + 1)
                    dve.wait_ge(s.cd, g + 1)
                    at_least(dve, s.ad, g)
                    dve.scalar_tensor_tensor(acc[:, bass.ds(b, 1), :].rearrange("p o c -> p (o c)"),
                                             acc[:, bass.ds(b, 1), :].rearrange("p o c -> p (o c)"),
                                             shrink[:, k % 4:k % 4 + 1],
                                             bank[4 + k % 2][:, 0:ROW], ALU.mult, ALU.add).then_inc(s.ad, 1)

                def move_probs(g, k):
                    dve.wait_ge(s.td, g + 1)
                    at_least(dve, s.ud, g - 1)
                    dve.tensor_copy(probT[:, k % 2, :], bank[2 + k % 2][:, 0:GROUP]).then_inc(s.ptd, 1)

                def maximum(g, k, b):
                    m, prev = k % 4, (k + 3) % 4
                    dve.wait_ge(s.fd, g + 1)
                    at_least(dve, s.pd, g - 1)
                    if l == 0:
                        at_least(dve, s.kd, g - 1)
                    dve.sem_inc(dve_turn, 1)
                    dve.tensor_tensor_reduce(logit[:, k % 2, :], bank[k % 2][:, 0:GROUP], lift[:, k % 2, :], 1.0, -3e38,
                                             ALU.add, ALU.max, here[:, m:m + 1]).then_inc(s.ld, 1)
                    at_least(dve, s.nd, g)
                    dve.tensor_tensor(neg_old[:, m:m + 1], neg_max[:, prev:prev + 1], fresh[:, bass.ds(g, 1)],
                                      ALU.max).then_inc(s.no, 1)
                    at_least(dve, s.cd, g - 3)
                    dve.wait_ge(s.ld, g + 1)
                    dve.wait_ge(s.no, g + 1)
                    dve.scalar_tensor_tensor(neg_max[:, m:m + 1], here[:, m:m + 1], -1.0, neg_old[:, m:m + 1],
                                             ALU.mult, ALU.min).then_inc(s.nd, 1)
                    if l == 0:
                        at_least(dve, s.dd, g)
                        dve.tensor_scalar(cjunk[:, :], logit[:, k % 2, :], FEW, 0.0, ALU.is_gt, ALU.add,
                                          accum_out=cnt[:, k % 2:k % 2 + 1]).then_inc(s.kd, 1)
                        dve.wait_ge(s.kd, g + 1)
                        dve.tensor_tensor(deg[:, bass.ds(b, 1)], deg[:, bass.ds(b, 1)], cnt[:, k % 2:k % 2 + 1],
                                          ALU.add).then_inc(s.dd, 1)

                def tile_one_hots(g, k):
                    for j in range(TILES_PER_GROUP):
                        t, place = g * TILES_PER_GROUP + j, (k * TILES_PER_GROUP + j) % (2 * TILES_PER_GROUP)
                        at_least(dve, s.cm, t + 1 - 2 * TILES_PER_GROUP)
                        dve.tensor_scalar(oh_low[:, place, :], iota_b[:, 0:P], low_col[:, bass.ds(t, 1)], None,
                                          ALU.is_equal).then_inc(s.oh, 1)
                        dve.tensor_scalar(oh_key[:, place, :], iota_b[:, :], key_col[:, bass.ds(t, 1)], None,
                                          ALU.is_equal).then_inc(s.oh, 1)

                def run_counts(g, k, i):
                    dve.wait_ge(s.cm, (g + 1) * TILES_PER_GROUP)
                    for j in range(TILES_PER_GROUP):
                        t, kt = g * TILES_PER_GROUP + j, k * TILES_PER_GROUP + j
                        at_least(dve, counted[kt % COUNT_RING],
                                 16 * (i * (TURN * TILES_PER_GROUP // COUNT_RING) + kt // COUNT_RING))
                        at_least(dve, s.rn, t)
                        dve.scalar_tensor_tensor(running[:, kt % COUNT_RING, :], running[:, (kt - 1) % COUNT_RING, :],
                                                 keep[:, bass.ds(t, 1)],
                                                 bank[6 + j // 2][:, (j % 2) * KEYS:(j % 2 + 1) * KEYS],
                                                 ALU.mult, ALU.add).then_inc(s.rn, 1)

                def turn(i):
                    first = isinstance(i, int)
                    b = [None, None, *blocks(0, TURN)] if first else blocks(i * TURN - 2, TURN + 2)
                    for k in range(TURN):
                        g = i * TURN + k
                        if not first or k >= 2:
                            accumulate(g - 2, (k - 2) % TURN, b[k])
                        if l:
                            if not first or k >= 2:
                                run_counts(g - 2, (k - 2) % TURN, i if k >= 2 else i - 1)
                            tile_one_hots(g, k)
                        elif not first or k >= 1:
                            move_probs(g - 1, (k - 1) % TURN)
                        maximum(g, k, b[k + 2])

                turn(0)
                with dve.Fori(1, TURNS) as i:
                    turn(i)
                b = blocks(NG - 2, 2)
                accumulate(NG - 2, TURN - 2, b[0])
                if l:
                    run_counts(NG - 2, TURN - 2, TURNS - 1)
                    run_counts(NG - 1, TURN - 1, TURNS - 1)
                else:
                    move_probs(NG - 1, TURN - 1)
                accumulate(NG - 1, TURN - 1, b[1])
                dve.wait_ge(s.ad, NG)
                link(dve.tensor_scalar(stat[:, 0, :], acc[:, 0:NB, F], 1e-16, None, ALU.add))
                link(dve.reciprocal(stat[:, 1, :], stat[:, 0, :]))
                link(dve.tensor_tensor(hN[:, :, :], acc[:, 0:NB, 0:F], per_block(stat[:, 1, :]), ALU.mult))
                link(dve.tensor_tensor(hN[:, :, :], hN[:, :, :], bias_bc[:, l, :].unsqueeze(1).to_broadcast([P, NB, F]), ALU.add))
                link(dve.tensor_scalar(hN[:, :, :], hN[:, :, :], 0.0, None, ALU.max))
            dve.wait_ge(LS[0].dd, NG)
            link(dve.tensor_tensor(hN[:, :, :], hN[:, :, :], xN[:, :, :], ALU.add))
            layer_norm(hN, xN, 0)
            link(dve.tensor_scalar(dinv[:, :], deg[:, 0:NB], 1.0, None, ALU.add))
            square_root(1)
            link(dve.reciprocal(dinv[:, :], dinv[:, :]))
            link(dve.tensor_tensor(work[:, :, :], xN[:, :, :], per_block(dinv[:, :]), ALU.mult))
            dve.wait_ge(s_par, 16 * 15)

            for c in range(3):
                s = CS[c]
                dve.engine_nop().then_inc(s.y, 1)
                halves = 2 if c == 0 else 1
                if c == 0:
                    for q, (o, n) in enumerate(NCH):
                        dve.wait_ge(s.tr, q + 1)
                        dve.tensor_copy(hT[:, o:o + n], bank[q % 2][:, 0:n]).then_inc(s.trs, 1)
                dve.wait_ge(s.act, halves * len(NCH))
                for v in range(halves):
                    link(dve.tensor_reduce(bst[:, 0, v:v + 1], H1[:, v, 0:N], AX_X, ALU.add))
                    link(dve.tensor_scalar(bst[:, 0, v:v + 1], bst[:, 0, v:v + 1], 1.0 / N, None, ALU.mult))
                    link(dve.tensor_scalar(H1[:, v, :], H1[:, v, :], bst[:, 0, v:v + 1], None, ALU.subtract))
                    link(dve.tensor_tensor(hT[:, 0:N], H1[:, v, 0:N], H1[:, v, 0:N], ALU.mult))
                    link(dve.tensor_reduce(bst[:, 1, v:v + 1], hT[:, 0:N], AX_X, ALU.add))
                link(dve.tensor_scalar(bst[:, 1, 0:halves], bst[:, 1, 0:halves], 1.0 / N, EPS_BN, ALU.mult, ALU.add))
                square_root(2 + c)
                link(dve.reciprocal(bst[:, 2, 0:halves], bst[:, 1, 0:halves]))
                col = 0 if c == 0 else c + 1
                link(dve.tensor_tensor(bst[:, 2, 0:halves], bst[:, 2, 0:halves], bn_par[:, 1, col:col + halves], ALU.mult))
                for v in range(halves):
                    link(dve.tensor_scalar(H1[:, v, :], H1[:, v, :], bst[:, 2, v:v + 1],
                                           bn_par[:, 2, col + v:col + v + 1], ALU.mult, ALU.add))
                dve.engine_nop().then_inc(s.bn, 1)
                for q, (o, n) in enumerate(NCH):
                    dve.wait_ge(s.mm2, q + 1)
                    b0, nb = o // F, n // F
                    got = bank[6 + q % 2][:, 0:n].rearrange("p (b f) -> p b f", f=F)
                    if c < 2:
                        dve.tensor_tensor(work[:, b0:b0 + nb, :], got,
                                          dinv[:, b0:b0 + nb].unsqueeze(2).to_broadcast([P, nb, F]), ALU.mult).then_inc(s.y2, 1)
                    else:
                        dve.tensor_tensor(hN[:, b0:b0 + nb, :], got, xN[:, b0:b0 + nb, :], ALU.add).then_inc(s.y2, 1)
                dve.wait_ge(s.y2, len(NCH))
            layer_norm(hN, hN, 5)
            dve.engine_nop().then_inc(s_h, 1)

        @block.scalar
        def _(act):
            def blocks(first, count):
                return nc.values_load_multi_w_load_instructions(
                    blk_row[0:1, bass.ds(first, count)], engines=(mybir.EngineType.Activation,), min_val=0, max_val=NB,
                    skip_runtime_bounds_check_because="a group's block is 0 to NB by its construction")[1]

            act.wait_ge(s_const, 1)
            act.wait_ge(s_blk_ld, 16)
            for l in range(L):
                s = LS[l]
                for b in range(NB):
                    act.wait_ge(s.mm, b + 1)
                    if b >= 2:
                        act.wait_ge(rows_stored[l][b % 2], 16 * (b // 2))
                    act.activation(rows_out[:, b % 2, 0:R // 2, 0:F],
                                   bank[3 * (b % 2)][:, :].rearrange("p (r f) -> p r f", f=F), ACT.Copy).then_inc(s.eva, 1)
                if l:
                    act.wait_ge(LS[l - 1].ais, NG + 1)
                act.wait_ge(s.ait, 1)
                for j in range(-(-NB // 8)):
                    nb = min(8, NB - 8 * j)
                    act.activation(aiT[0:ROWS_RELATION, 8 * j:8 * j + nb, :],
                                   bank[j][0:ROWS_RELATION, :].bitcast(BF16)[:, 0:nb * P].rearrange("p (b f) -> p b f", f=P),
                                   ACT.Copy).then_inc(s.aits, 1)
                act.wait_ge(s.aits, -(-NB // 8))

                def stage_ai(g, k, b):
                    at_least(act, s.xd, g - 1)
                    act.sem_inc(act_turn, 1)
                    act.activation(aiS[:, k % 2, :], aiT[:, bass.ds(b, 1), :].rearrange("p o d -> p (o d)"),
                                   ACT.Copy).then_inc(s.ais, 1)

                def exps(g, k):
                    m = k % 4
                    act.wait_ge(s.nd, g + 1)
                    at_least(act, s.td, g - 1)
                    act.activation(prob[:, k % 2, :], logit[:, k % 2, :], ACT.Exp, bias=neg_max[:, m:m + 1]).then_inc(s.pd, 1)
                    at_least(act, s.ad, g - 3)
                    act.activation(shrink[:, m:m + 1], neg_old[:, m:m + 1], ACT.Exp, bias=neg_max[:, m:m + 1],
                                   scale=-1.0).then_inc(s.cd, 1)

                def lifts(g, k):
                    act.wait_ge(s.xd, g + 1)
                    at_least(act, s.ld, g - 1)
                    act.activation(lift[:, k % 2, :], bank[k % 2][:, 0:GROUP], ACT.Relu, scale=-0.8).then_inc(s.fd, 1)

                def move_probs(g, k):
                    act.wait_ge(s.td, g + 1)
                    at_least(act, s.ud, g - 1)
                    act.activation(probT[:, k % 2, :], bank[2 + k % 2][:, 0:GROUP], ACT.Copy).then_inc(s.ptd, 1)

                def turn(i):
                    first = isinstance(i, int)
                    b = blocks(i * TURN + 1, TURN)
                    for k in range(TURN):
                        g = i * TURN + k
                        if not first or k >= 1:
                            exps(g - 1, (k - 1) % TURN)
                        stage_ai(g + 1, (k + 1) % TURN, b[k])
                        if l and (not first or k >= 1):
                            move_probs(g - 1, (k - 1) % TURN)
                        lifts(g, k)

                stage_ai(0, 0, blocks(0, 2)[0])
                turn(0)
                with act.Fori(1, TURNS) as i:
                    turn(i)
                exps(NG - 1, TURN - 1)
                if l:
                    move_probs(NG - 1, TURN - 1)

            def square_root(n, what):
                act.wait_ge(sq_req, n + 1)
                act.activation(what, what, ACT.Sqrt).then_inc(sq_done, 1)

            square_root(0, stat[:, 1, :])
            square_root(1, dinv[:, :])
            act.wait_ge(s_par, 16 * 15)
            for c in range(3):
                s = CS[c]
                col = 0 if c == 0 else c + 1
                func = ACT.Relu if c < 2 else ACT.Identity

                def scale_sums(b, k):
                    act.wait_ge(s.ud, b + 1)
                    act.sem_inc(act_turn, 1)
                    act.activation(hN[:, bass.ds(b, 1), :].rearrange("p o f -> p (o f)"), bank[k][:, 0:F], ACT.Copy,
                                   scale=dinv[:, bass.ds(b, 1)]).then_inc(s.ev, 1)

                with act.Fori(0, NB // 3) as i:
                    for k in range(3):
                        scale_sums(3 * i + k, k)
                for b in range(NB // 3 * 3, NB):
                    scale_sums(b, b % 3)
                if c == 0:
                    for n, (v, (o, w)) in enumerate((v, ch) for v in range(2) for ch in NCH):
                        act.wait_ge(s.mm, n + 1)
                        act.activation(H1[:, v, o:o + w], bank[2 + n % 4][:, 0:w], func,
                                       bias=bn_par[:, 0, v:v + 1]).then_inc(s.act, 1)
                else:
                    for q, (o, w) in enumerate(NCH):
                        act.wait_ge(s.tr, q + 1)
                        act.activation(H1[:, 0, o:o + w], bank[q % 2][:, 0:w], func,
                                       bias=bn_par[:, 0, col:col + 1]).then_inc(s.act, 1)
                square_root(2 + c, bst[:, 1, 0:2 if c == 0 else 1])
            square_root(5, stat[:, 1, :])

        @block.tensor
        def _(pe):
            pe.wait_ge(s_const, 1)
            pe.wait_ge(s_below, 1)
            pe.matmul(bank[0][:, 0:NB + 1], ones[0:EDGE_SPLIT, :], below[:, :], start=True, stop=True).then_inc(s_start, 1)
            pe.wait_ge(s_fG, 1)
            for h in range(2):
                for c in range(GC):
                    ins = pe.transpose(bank[1 + h][:, c * P:(c + 1) * P], fG[:, 0, c, h * P:(h + 1) * P], ident[:, :])
                ins.then_inc(s_colT, 1)
            pe.wait_ge(s_blkf, 1)
            pe.matmul(bank[0][:, 0:SLOTS], ones[0:1, :], fresh[0:1, :], start=True, stop=True).then_inc(s_fresh, 1)

            for l in range(L):
                s = LS[l]
                h = xN if l == 0 else hN
                loads = 32 * TURNS * l
                row_loads = 16 * TURNS * l
                if l:
                    pe.wait_ge(s_win_deg, 1)
                    pe.matmul(bank[0][:, 0:WINS], ones[:, :], win[:, 6, :], start=True, stop=True).then_inc(s_win_n, 1)
                    pe.wait_ge(s_keep, 1)
                    for n in range(TC):
                        ins = pe.matmul(bank[1 + n // 4][:, (n % 4) * P:(n % 4 + 1) * P], ones[:, :], keyT[:, n, :],
                                        start=True, stop=True)
                    ins.then_inc(s_keep_bc, 1)
                    pe.wait_ge(s_keys, 1)
                    for n in range(TC):
                        pe.transpose(bank[1 + n // 4][:, (n % 4) * P:(n % 4 + 1) * P], keyT[:, n, :], ident[:, :])
                        ins = pe.transpose(bank[4 + n // 4][:, (n % 4) * P:(n % 4 + 1) * P], lowT[:, n, :], ident[:, :])
                    ins.then_inc(s_keyT, 1)
                pe.wait_ge(s_h, l + 1)
                for r in range(R):
                    if r >= 2:
                        pe.wait_ge(s.wts, r - 1)
                    pe.transpose(bank[6 + r % 2][:, 0:P], Wsb[:, l, r, :], ident[:, :]).then_inc(s.wt, 1)
                    pe.wait_ge(s.wts, r + 1)
                    pe.matmul(bank[5][:, 2 * r:2 * r + 2], WT[:, r % 2, :], qk[:, l, :], start=True, stop=True).then_inc(s.wqk, 1)

                def transpose_block(b):
                    if b >= 2:
                        pe.wait_ge(s.hts, b - 1)
                    pe.transpose(bank[6 + b % 2][:, 0:P], h[:, b, :], ident[:, :]).then_inc(s.tr, 1)

                transpose_block(0)
                pe.wait_ge(s.wqks, 1)
                for b in range(NB):
                    if b + 1 < NB:
                        transpose_block(b + 1)
                    pe.wait_ge(s.hts, b + 1)
                    if b >= 2:
                        pe.wait_ge(s.eva, b - 1)
                        pe.wait_ge(s.evb, b - 1)
                    half = 3 * (b % 2)
                    for j in range(2):
                        pe.matmul(bank[half + j][:, :], hTs[:, b % 2, :],
                                  Wsb[:, l, j * (R // 2):(j + 1) * (R // 2), :].rearrange("p r f -> p (r f)"), start=True, stop=True)
                    pe.matmul(bank[half + 2][:, 0:2 * R], hTs[:, b % 2, :], Wqk[:, :, :].rearrange("p o r -> p (o r)"),
                              start=True, stop=True).then_inc(s.mm, 1)
                pe.wait_ge(s.aip, 1)
                pe.wait_ge(s.eva, NB)
                for b in range(NB):
                    there = bank[b // 8][0:ROWS_RELATION, :].bitcast(BF16)
                    ins = pe.transpose(there[:, (b % 8) * P:(b % 8 + 1) * P], ai_parts[:, b, :], ident_b[:, :])
                ins.then_inc(s.ait, 1)
                pe.wait_ge(s.aits, -(-NB // 8))

                def logits(g, k, i):
                    hb = k // (TURN // 2)
                    pe.wait_ge(s.ais, g + 1)
                    at_least(pe, s.ld, g - 1)
                    pe.wait_ge(er_loaded[hb], row_loads + 16 * (i + 1))
                    there = bank[k % 2]
                    cols = erows[:, hb, (k % (TURN // 2)) * GROUP:(k % (TURN // 2) + 1) * GROUP]
                    pe.matmul(there[:, 0:GROUP], mask_w[:, :], cols, start=True, stop=False)
                    pe.matmul(there[:, 0:GROUP], aiS[:, k % 2, :], cols, start=False, stop=False)
                    pe.wait_ge(gathered[k], loads + 32 * (i + 1))
                    for t in range(2):
                        ins = pe.matmul(there[:, t * P:(t + 1) * P], msg[:, k, t, F + 1:F + 2].to_broadcast([P, P]), ident[:, :],
                                        start=False, stop=(t == 1))
                    ins.then_inc(s.xd, 1)

                def turn_probs(g, k):
                    pe.wait_ge(s.pd, g + 1)
                    at_least(pe, s.ptd, g - 1)
                    for t in range(2):
                        ins = pe.transpose(bank[2 + k % 2][:, t * P:(t + 1) * P], prob[:, k % 2, t * P:(t + 1) * P], ident[:, :])
                    ins.then_inc(s.td, 1)

                def sums(g, k):
                    pe.wait_ge(s.ptd, g + 1)
                    at_least(pe, s.ad, g - 1)
                    for t in range(2):
                        ins = pe.matmul(bank[4 + k % 2][:, 0:ROW], probT[:, k % 2, t * P:(t + 1) * P], msg[:, k, t, :],
                                        start=(t == 0), stop=(t == 1))
                    ins.then_inc(s.ud, 1)

                def count_edges(g, k):
                    at_least(pe, s.rn, g * TILES_PER_GROUP)
                    for j in range(TILES_PER_GROUP):
                        place = (k * TILES_PER_GROUP + j) % (2 * TILES_PER_GROUP)
                        pe.wait_ge(s.oh, 2 * (g * TILES_PER_GROUP + j + 1))
                        pe.matmul(bank[6 + j // 2][:, (j % 2) * KEYS:(j % 2 + 1) * KEYS], oh_low[:, place, :],
                                  oh_key[:, place, :], start=True, stop=True).then_inc(s.cm, 1)

                def turn(i):
                    first = isinstance(i, int)
                    for k in range(TURN):
                        g = i * TURN + k
                        logits(g, k, i)
                        if not first or k >= 2:
                            sums(g - 2, (k - 2) % TURN)
                        if not first or k >= 1:
                            turn_probs(g - 1, (k - 1) % TURN)
                        if l and (not first or k >= 1):
                            count_edges(g - 1, (k - 1) % TURN)

                turn(0)
                with pe.Fori(1, TURNS) as i:
                    turn(i)
                sums(NG - 2, TURN - 2)
                turn_probs(NG - 1, TURN - 1)
                if l:
                    count_edges(NG - 1, TURN - 1)
                sums(NG - 1, TURN - 1)

            for c in range(3):
                s = CS[c]
                pe.wait_ge(s.y, 1)

                by_source_block = count_in[:, :, :, :].rearrange("p i w (d s) -> p i (w d) s", s=NB)

                def block_sums(b, k, turn):
                    at_least(pe, s.ev, b - 2)
                    pe.wait_ge(counts_in[k], 16 * (c * (NB // 3 + (k < NB % 3)) + turn + 1))
                    for j in range(NB):
                        pe.matmul(bank[k][:, 0:F], by_source_block[:, k, :, j], work[:, j, :],
                                  start=(j == 0), stop=False)
                    pe.matmul(bank[k][:, 0:F], ident[:, :], work[:, bass.ds(b, 1), :].rearrange("p o f -> p (o f)"),
                              start=False, stop=True).then_inc(s.ud, 1)

                for k in range(3):
                    block_sums(k, k, 0)
                with pe.Fori(1, NB // 3) as i:
                    for k in range(3):
                        block_sums(3 * i + k, k, i)
                for b in range(NB // 3 * 3, NB):
                    block_sums(b, b % 3, b // 3)
                pe.wait_ge(s.ev, NB)
                for q, (o, n) in enumerate(NCH):
                    if q >= 2:
                        pe.wait_ge(s.trs if c == 0 else s.act, q - 1)
                    for j in range(n // P):
                        ins = pe.transpose(bank[q % 2][:, j * P:(j + 1) * P], hN[:, o // P + j, :], ident[:, :])
                    ins.then_inc(s.tr, 1)
                if c == 0:
                    pe.wait_ge(s.trs, len(NCH))
                    for m, (v, (o, n)) in enumerate((v, ch) for v in range(2) for ch in NCH):
                        if m >= 4:
                            pe.wait_ge(s.act, m - 3)
                        pe.matmul(bank[2 + m % 4][:, 0:n], W1sb[:, v * P:(v + 1) * P], hT[:, o:o + n],
                                  start=True, stop=True).then_inc(s.mm, 1)
                pe.wait_ge(s.bn, 1)
                for q, (o, n) in enumerate(NCH):
                    if q >= 2:
                        pe.wait_ge(s.y2, q - 1)
                    for j in range(n // P):
                        there = bank[6 + q % 2][:, j * P:(j + 1) * P]
                        nodes = slice(o + j * P, o + (j + 1) * P)
                        if c == 0:
                            for v in range(2):
                                ins = pe.matmul(there, H1[:, v, nodes], W2sb[:, v, :], start=(v == 0), stop=(v == 1))
                        elif c == 1:
                            ins = pe.matmul(there, H1[:, 0, nodes], W3sb[:, :], start=True, stop=True)
                        else:
                            ins = pe.transpose(there, H1[:, 0, nodes], ident[:, :])
                    ins.then_inc(s.mm2, 1)


_INS = ["x", "src", "dst", "edge_type_8", "L0_gnn_W", "L0_gnn_att_q", "L0_gnn_att_k", "L0_gnn_bias",
        "L1_gnn_W1", "L1_gnn_b1", "L1_gnn_g1", "L1_gnn_beta1", "L1_gnn_W2", "L1_gnn_b2", "L1_gnn_g2", "L1_gnn_beta2",
        "L1_gnn_W3", "L1_gnn_b3", "L1_gnn_g3", "L1_gnn_beta3"]


def kernel(**inputs):
    import numpy as _np
    import concourse.bacc as _bacc
    from concourse import mybir as _mybir
    from concourse.bass_utils import run_bass_kernel_spmd as _run

    nc = _bacc.Bacc("TRN2", target_bir_lowering=False, num_devices=1)
    arrays, args = {}, []
    for name in _INS:
        a = _np.ascontiguousarray(inputs[name])
        arrays[f"in_{name}_dram"] = a
        args.append(nc.dram_tensor(f"in_{name}_dram", a.shape, _mybir.dt.from_np(a.dtype), kind="ExternalInput").ap())
    out = nc.dram_tensor("out_0_dram", inputs["x"].shape, _mybir.dt.float32, kind="ExternalOutput").ap()
    gnn_kernel(nc, *args, out)
    r = _run(nc, [arrays], core_ids=[0])
    return r.results[0]["out_0_dram"]
```

```python
from collections import namedtuple
from contextlib import ExitStack

import concourse.bass as bass
from concourse import mybir

F32 = mybir.dt.float32
BF16 = mybir.dt.bfloat16
I32 = mybir.dt.int32
ALU = mybir.AluOpType
ACT = mybir.ActivationFunctionType
AX_X = mybir.AxisListType.X

P = 128
EDGE_SPLIT = 125
GROUP = 256
TURN = 8
GATHER_PARTS = 4
WINDOW = 8
TILES_PER_GROUP = 3
COUNT_RING = 8
DIGIT_BITS = 4
DIGITS = 2 ** DIGIT_BITS
MASK_UNIT = 2.0 ** 100
NO_MAX = 1e25
FEW = -1e20
ROWS_RELATION = 24
ROWS = 29


LayerSignals = namedtuple("LayerSignals", "wt wts wqk wqks tr hts mm eva evb aip ait aits staged ais xd fd ld no nd pd cd "
                          "td ptd ud ad kd dd oh cm rn")
ConvSignals = namedtuple("ConvSignals", "y ud ev tr trs mm act bn mm2 y2")


def at_least(engine, semaphore, value):
    if isinstance(value, int) and value <= 0:
        return
    engine.wait_ge(semaphore, value)


def gnn_kernel(nc, x, src, dst, edge_type, W, att_q, att_k, bias,
               W1, b1, g1, beta1, W2, b2, g2, beta2, W3, b3, g3, beta3, out):
    N, F = x.shape
    E = src.shape[0]
    L, R = W.shape[0], W.shape[1]
    NB = -(-N // P)
    FULL, REST = N // P, N % P
    NP = NB * P
    NG_NEEDED = (E + NB * (GROUP - 1)) // GROUP
    TURNS = -(-NG_NEEDED // TURN)
    NG = TURNS * TURN
    GC = -(-NG // P)
    SLOTS = GC * P
    EP = E + GROUP
    EC = E // EDGE_SPLIT
    ROW = F + 2
    WPB = P // WINDOW
    WINS = NB * WPB
    TILES = TILES_PER_GROUP * NG
    TC = -(-TILES // P)
    KEYS = WINDOW * NB
    SHIFT = 7
    assert E // P + WINS <= TILES and KEYS <= 256
    NCH = [(o, min(512, NP - o)) for o in range(0, NP, 512)]
    EPS_LN = 1e-5
    EPS_BN = 1e-5
    PASSES = -(-(N - 1).bit_length() // DIGIT_BITS)
    assert F == P and E % EDGE_SPLIT == 0 and L == 2 and R == 8 and NG <= SLOTS

    def dram(name, shape, dt):
        return nc.dram_tensor(name, shape, dt, kind="Internal").ap()

    src_list = dram("src_list", (EP, 1), I32)
    dst_list = dram("dst_list", (EP, 1), I32)
    type_list = dram("type_list", (EP, 1), I32)
    sorted_by = [dram(f"sorted_by{i}", (E, 4), I32) for i in range(PASSES)]
    edge_rows = dram("edge_rows", (ROWS, SLOTS * GROUP), BF16)
    group_block = dram("group_block", (1, SLOTS), I32)
    table = dram("table", (NP * R, ROW), F32)
    tile_window = dram("tile_window", (1, TC * P), I32)
    counts = dram("counts", (WINS + COUNT_RING, P, KEYS), F32)

    with ExitStack() as ctx:
        def sb(name, shape, dt=F32):
            return ctx.enter_context(nc.sbuf_tensor(name, shape, dt))

        def sem(name):
            return ctx.enter_context(nc.semaphore(name))

        bank = [ctx.enter_context(nc.psum_tensor(f"bank{i}", [P, 512], F32)) for i in range(8)]

        ident = sb("ident", [P, P])
        ident_b = sb("ident_b", [P, P], BF16)
        ones = sb("ones", [P, P])
        iota_row = sb("iota_row", [P, P])
        mask_w = sb("mask_w", [P, P], BF16)
        block_minus = sb("block_minus", [P, NB])
        group_id = sb("group_id", [P, GC])
        pad_i = sb("pad_i", [1, 2 * GROUP], I32)
        xN = sb("xN", [P, NB, F])
        hN = sb("hN", [P, NB, F])
        work = sb("work", [P, NB, F])
        COUNTS_IN = 3 * WPB * KEYS
        ACC, TCP, OUT2 = (NB + 1) * ROW, TC * P, 2 * R * ROW
        shared = sb("shared", [P, max(COUNTS_IN, ACC + 3 * TCP + OUT2)])
        count_in = shared[:, 0:COUNTS_IN].rearrange("p (i w k) -> p i w k", i=3, k=KEYS)
        acc_flat = shared[:, 0:ACC]
        acc = acc_flat.rearrange("p (b c) -> p b c", c=ROW)
        keep, key_col, low_col = (shared[:, ACC + n * TCP:ACC + (n + 1) * TCP] for n in range(3))
        rows_out = shared[:, ACC + 3 * TCP:ACC + 3 * TCP + OUT2].rearrange("p (i r c) -> p i r c", i=2, c=ROW)
        win = acc_flat[:, 0:7 * WINS].rearrange("p (n w) -> p n w", w=WINS)
        sqi = acc_flat[:, 0:2 * GC * GROUP].bitcast(I32).rearrange("p (n e) -> p n e", n=2)
        hN_flat = hN[:, :, :].rearrange("p b f -> p (b f)")
        dst_sp = hN_flat[0:EDGE_SPLIT, 0:EC].bitcast(I32)
        junk = hN_flat[0:EDGE_SPLIT, EC:2 * EC]
        sqf = hN_flat[:, 2 * EC:2 * EC + GC * GROUP]
        hT = sb("hT", [P, NP])
        H1 = sb("H1", [P, 2, NP])
        below = sb("below", [EDGE_SPLIT, NB + 2])
        start = sb("start", [P, NB + 2])
        unsorted = sb("unsorted", [P, 1], I32)
        records = H1[0:EDGE_SPLIT, 0, 0:4 * EC].bitcast(I32).rearrange("p (e n) -> p e n", n=4)
        dst_next = H1[0:EDGE_SPLIT, 0, 0:EC].bitcast(I32)
        plain = H1[0:EDGE_SPLIT, 1, 0:3 * EC].bitcast(I32).rearrange("p (n e) -> p n e", n=3)
        digit, same, upto, place_of = (H1[0:EDGE_SPLIT, 1, n * EC:(n + 1) * EC] for n in range(4))
        record_now = sb("record_now", [EDGE_SPLIT, 4], I32)
        place_now = sb("place_now", [EDGE_SPLIT, 1], I32)
        place_i = hT[0:EDGE_SPLIT, 0:EC].bitcast(I32)
        earlier = hT[:, EC:EC + P]
        number = sb("number", [P, 4, DIGITS])
        nb_f = sb("nb_f", [P, NB])
        nb_i = sb("nb_i", [P, NB], I32)
        ge = sb("ge", [P, NB])
        gs = sb("gs", [P, NB])
        off = sb("off", [P, NB])
        ind = sb("ind", [P, GC, NB])
        t25 = sb("t25", [P, GC, NB])
        g256 = sb("g256", [P, GC])
        blk = sb("blk", [P, GC])
        blk128 = sb("blk128", [P, GC])
        blk_i = sb("blk_i", [P, GC], I32)
        offs = sb("offs", [P, GC])
        offs_i = sb("offs_i", [P, GC], I32)
        fG = hT[:, 0:2 * GC * GROUP].rearrange("p (n c e) -> p n c e", n=2, e=GROUP)
        rowsG = H1[:, :, :].rearrange("p v n -> p (v n)").bitcast(BF16)[:, 0:(R + 4) * GC * GROUP].rearrange(
            "p (k e) -> p k e", e=GC * GROUP)
        srcG, dstG, typG = (work[:, :, :].rearrange("p b f -> p (b f)")[:, n * GC * GROUP:(n + 1) * GC * GROUP].bitcast(
            I32).rearrange("p (c e) -> p c e", c=GC) for n in range(3))
        row_col = sb("row_col", [P, SLOTS, 2], I32)
        blk_row = sb("blk_row", [1, SLOTS + 16], I32)
        fresh = sb("fresh", [P, SLOTS])
        blk_bc = sb("blk_bc", [P, SLOTS + 1])
        deg = sb("deg", [P, NB + 1])
        iota_keys = sb("iota_keys", [P, max(WINS, KEYS)])
        iota_b = sb("iota_b", [P, KEYS], BF16)
        in_window = sb("in_window", [P, WPB])
        tile_id = sb("tile_id", [P, TC])
        win_i = sb("win_i", [P, WINS], I32)
        tile_num = sb("tile_num", [P, 6, TC])
        tile_off = sb("tile_off", [P, TC], I32)
        tile_dest = sb("tile_dest", [P, TC], I32)
        dest_row = sb("dest_row", [1, TC * P], I32)
        oh_low = sb("oh_low", [P, 2 * TILES_PER_GROUP, P], BF16)
        oh_key = sb("oh_key", [P, 2 * TILES_PER_GROUP, KEYS], BF16)
        running = sb("running", [P, COUNT_RING, KEYS])
        dinv = sb("dinv", [P, NB])
        Wsb = sb("Wsb", [P, L, R, F])
        WT = sb("WT", [P, 2, F])
        qk = sb("qk", [P, L, 2])
        Wqk = sb("Wqk", [P, 2, R])
        bias_bc = sb("bias_bc", [P, L, F])
        W1sb = sb("W1sb", [P, 2 * F])
        W2sb = sb("W2sb", [P, 2, F])
        W3sb = sb("W3sb", [P, F])
        bn_par = sb("bn_par", [P, 3, 4])
        H1_flat = H1[:, :, :].rearrange("p v n -> p (v n)")

        def tile_array(n, dt=F32):
            a = H1_flat[:, n * TC * P:(n + 1) * TC * P]
            return (a.bitcast(dt) if dt != F32 else a).rearrange("p (c e) -> p c e", e=P)

        srcT, dstT, highT = (tile_array(n, I32) for n in range(3))
        keyT, lowT = (tile_array(n) for n in (3, 4))
        placeT = hT[:, 0:TC * P].rearrange("p (c e) -> p c e", e=P)
        validT = hT[:, TC * P:2 * TC * P].rearrange("p (c e) -> p c e", e=P)
        hTs = sb("hTs", [P, 2, P])
        ai = sb("ai", [P, NB, R])
        ai_rest = sb("ai_rest", [P, NB, R])
        ai_parts = sb("ai_parts", [P, NB, 3 * R], BF16)
        aiT = sb("aiT", [P, NB + 1, P], BF16)
        stage = sb("stage", [P, GATHER_PARTS, 2 * TURN // GATHER_PARTS], I32)
        msg = sb("msg", [P, TURN, 2, ROW])
        erows = sb("erows", [P, 2, TURN // 2 * GROUP], BF16)
        aiS = sb("aiS", [P, 2, P], BF16)
        logit = sb("logit", [P, 2, GROUP])
        prob = sb("prob", [P, 2, GROUP])
        probT = sb("probT", [P, 2, GROUP])
        neg_max = sb("neg_max", [P, 4])
        here = sb("here", [P, 4])
        lift = sb("lift", [P, 2, GROUP])
        neg_old = sb("neg_old", [P, 4])
        shrink = sb("shrink", [P, 4])
        cnt = sb("cnt", [P, 2])
        cjunk = sb("cjunk", [P, 2, GROUP])
        stat = sb("stat", [P, 6, NB])
        bst = sb("bst", [P, 6, 2])
        part_id = sb("part_id", [P, 1])

        s_x, s_dst, s_w, s_par, s_lists = sem("s_x"), sem("s_dst"), sem("s_w"), sem("s_par"), sem("s_lists")
        s_zero, s_pad, s_iota = sem("s_zero"), sem("s_pad"), sem("s_iota")
        s_const, s_below, s_start, s_start_sb = sem("s_const"), sem("s_below"), sem("s_start"), sem("s_start_sb")
        s_next, s_ready, s_load, s_number, s_before, s_place, s_moved = (
            sem(n) for n in ("s_next", "s_ready", "s_load", "s_number", "s_before", "s_place", "s_moved"))
        sort_chain, s_record = sem("sort_chain"), sem("s_record")
        scattered = [sem(f"scattered{i}") for i in range(PASSES)]
        s_offs, s_blk, s_blk_st, s_blk_ld = sem("s_offs"), sem("s_blk"), sem("s_blk_st"), sem("s_blk_ld")
        s_groups, s_rows, s_rows_st = sem("s_groups"), sem("s_rows"), sem("s_rows_st")
        s_fG, s_colT, s_col = sem("s_fG"), sem("s_colT"), sem("s_col")
        s_fresh, s_blkf = sem("s_fresh"), sem("s_blkf")
        dve_chain = sem("dve_chain")
        act_chain = sem("act_chain")
        act_turn, pool_turn, dve_turn = sem("act_turn"), sem("pool_turn"), sem("dve_turn")
        s_out = sem("s_out")
        s_win_deg, s_win_n, s_tiles, s_keep, s_keep_bc = (sem(n) for n in ("s_win_deg", "s_win_n", "s_tiles", "s_keep", "s_keep_bc"))
        s_dest_st, s_dest_ld, s_tile_edges, s_keys, s_keyT = (
            sem(n) for n in ("s_dest_st", "s_dest_ld", "s_tile_edges", "s_keys", "s_keyT"))
        counted = [sem(f"counted{i}") for i in range(COUNT_RING)]
        counts_in = [sem(f"counts_in{i}") for i in range(3)]
        sq_req, sq_done = sem("sq_req"), sem("sq_done")
        s_h = sem("s_h")

        LS = [LayerSignals(*(None if name in unused else sem(f"L{l}_{name}") for name in LayerSignals._fields)) for l, unused in ((0, ("oh", "cm", "rn")), (1, ("kd", "dd")))]
        rows_stored = [[sem(f"L{l}_rows_stored{i}") for i in range(2)] for l in range(L)]
        gathered = [sem(f"gathered{k}") for k in range(TURN)]
        er_loaded = [sem(f"er_loaded{h}") for h in range(2)]

        CS = ConvSignals(*(sem(f"conv_{name}") for name in ConvSignals._fields))
        QN = len(NCH)

        def conv_before(c):
            return c * NB, c * QN, (c + 1) * QN if c else 0

        block = ctx.enter_context(nc.Block())

        @block.sync
        def _(sp):
            sp.dma_start(dst_sp[:, :], dst.rearrange("(p c) -> p c", p=EDGE_SPLIT)).then_inc(s_dst, 16)
            for whole, given in ((src_list, src), (dst_list, dst), (type_list, edge_type)):
                sp.dma_start(whole[0:E, :].rearrange("(p c) o -> p (c o)", p=EDGE_SPLIT),
                             given.rearrange("(p c) -> p c", p=EDGE_SPLIT)).then_inc(s_lists, 16)
            sp.wait_ge(s_pad, 2)
            for whole, o in ((src_list, 0), (dst_list, GROUP), (type_list, 0)):
                sp.dma_start(whole[E:EP, :].rearrange("c o -> o c"), pad_i[:, o:o + GROUP]).then_inc(s_lists, 16)
            sp.wait_ge(s_lists, 16 * 6)
            sp.dma_start(dst_next, dst_list[1:E + 1, :].rearrange("(p c) o -> p (c o)", p=EDGE_SPLIT)).then_inc(s_next, 16)

            sp.wait_ge(s_zero, 1)
            sp.dma_start(xN[:, 0:FULL, :], x[0:FULL * P, :].rearrange("(b p) f -> p b f", p=P)).then_inc(s_x, 16)
            sp.dma_start(xN[0:REST, FULL, :], x[FULL * P:N, :]).then_inc(s_x, 16)
            for l in range(L):
                sp.dma_start(Wsb[:, l, :, :], W[l].rearrange("r f g -> f r g")).then_inc(s_w, 16)
                sp.dma_start(qk[:, l, 0:1], att_q[l]).then_inc(s_w, 16)
                sp.dma_start(qk[:, l, 1:2], att_k[l]).then_inc(s_w, 16)
                sp.dma_start(bias_bc[:, l, :], bias[l].partition_broadcast(P)).then_inc(s_w, 16)

            def sort():
                lists = (src_list, dst_list, type_list)
                for n, whole in enumerate(lists):
                    sp.dma_start(plain[:, n, :], whole[0:E, :].rearrange("(p c) o -> p (c o)", p=EDGE_SPLIT)).then_inc(s_load, 16)
                for n in range(PASSES):
                    sp.wait_ge(s_moved, n + 1)
                    sp.dma_start(records, sorted_by[n].rearrange("(p c) n -> p c n", p=EDGE_SPLIT)).then_inc(s_load, 16)
                sp.wait_ge(s_place, PASSES + 1)
                for n, whole in enumerate(lists):
                    sp.dma_start(whole[0:E, :].rearrange("(p c) o -> p (c o)", p=EDGE_SPLIT), plain[:, n, :]).then_inc(s_load, 16)
                sp.wait_ge(s_load, 16 * (PASSES + 6))

            sp.wait_ge(s_blk, 1)
            with sp.If(sp.value_load(unsorted[0:1, 0:1], min_val=0, max_val=1) == 1):
                sort()
            sp.sem_inc(s_ready, 1)
            sp.dma_start(W1sb[:, :], W1).then_inc(s_par, 16)
            sp.dma_start(W2sb[:, :, :], W2.rearrange("(c p) n -> p c n", p=P)).then_inc(s_par, 16)
            sp.dma_start(W3sb[:, :], W3).then_inc(s_par, 16)
            for i, (one, two, three) in enumerate(((b1, b2, b3), (g1, g2, g3), (beta1, beta2, beta3))):
                for c in range(2):
                    sp.dma_start(bn_par[:, i, c:c + 1], one[c * P:(c + 1) * P].rearrange("(p o) -> p o", o=1)).then_inc(s_par, 16)
                sp.dma_start(bn_par[:, i, 2:3], two.rearrange("(p o) -> p o", o=1)).then_inc(s_par, 16)
                sp.dma_start(bn_par[:, i, 3:4], three.rearrange("(p o) -> p o", o=1)).then_inc(s_par, 16)
            sp.wait_ge(s_blk, 2)
            with nc.allow_non_contiguous_dma(reason="512 numbers"):
                sp.dma_start(group_block.rearrange("o (c p) -> (o p) c", p=P), blk_i[:, :]).then_inc(s_blk_st, 16)
            sp.wait_ge(s_blk_st, 16)
            sp.dma_start(blk_row[:, 0:SLOTS], group_block).then_inc(s_blk_ld, 16)
            for l in range(L):
                s = LS[l]
                for b in range(NB):
                    sp.wait_ge(s.eva, b + 1)
                    sp.wait_ge(s.evb, b + 1)
                    sp.dma_start(table[b * P * R:(b + 1) * P * R, :].rearrange("(p r) c -> p (r c)", p=P),
                                 rows_out[:, b % 2, :, :].rearrange("p r c -> p (r c)")).then_inc(rows_stored[l][b % 2], 16)
                if l == 0:
                    sp.wait_ge(s_rows, 1)
                    for k in range(ROWS):
                        i = k % R if k < ROWS_RELATION else R + (0 if k < 26 else k - 25)
                        sp.dma_start(edge_rows[k:k + 1, :].rearrange("o (c p e) -> (o p) c e", p=P, e=GROUP),
                                     rowsG[:, i, :].rearrange("p (c e) -> p c e", c=GC)).then_inc(s_rows_st, 16)
                    sp.wait_ge(s_rows_st, 16 * ROWS)

                def load_rows(i, h):
                    sp.dma_start(erows[0:ROWS, h, :],
                                 edge_rows[:, bass.ds((i * TURN + h * (TURN // 2)) * GROUP, TURN // 2 * GROUP)]
                                 ).then_inc(er_loaded[h], 16)

                for h in range(2):
                    if l:
                        sp.wait_ge(LS[l - 1].xd, NG)
                    else:
                        sp.wait_ge(s_zero, 2)
                    load_rows(0, h)
                HALF = TILES_PER_GROUP * TURN // 2

                def store_counts(i, h):
                    dests = nc.values_load_multi_w_load_instructions(
                        dest_row[0:1, bass.ds((2 * i + h) * HALF, HALF)], engines=(mybir.EngineType.SP,),
                        min_val=0, max_val=WINS + COUNT_RING - 1,
                        skip_runtime_bounds_check_because="a window, or a spare place by the tile's number")[1]
                    for j in range(HALF):
                        tile = (2 * i + h) * HALF + j
                        k = (h * HALF + j) % COUNT_RING
                        sp.wait_ge(s.rn, tile + 1)
                        sp.dma_start(counts[bass.ds(dests[j], 1), :, :].rearrange("w p k -> (w p) k"),
                                     running[:, k, :]).then_inc(counted[k], 16)

                if l:
                    sp.wait_ge(s_dest_ld, 16)
                with sp.Fori(1, TURNS) as i:
                    for h in range(2):
                        if l:
                            store_counts(i - 1, h)
                        sp.wait_ge(s.xd, (i - 1) * TURN + (h + 1) * (TURN // 2))
                        load_rows(i, h)
                if l:
                    for h in range(2):
                        store_counts(TURNS - 1, h)
                else:
                    sp.wait_ge(s_tiles, 1)
                    with nc.allow_non_contiguous_dma(reason="1280 numbers"):
                        sp.dma_start(tile_window.rearrange("o (c p) -> (o p) c", p=P), tile_dest[:, :]).then_inc(s_dest_st, 16)
                    sp.wait_ge(s_dest_st, 16)
                    sp.dma_start(dest_row[:, :], tile_window).then_inc(s_dest_ld, 16)
            for k in range(COUNT_RING):
                sp.wait_ge(counted[k], 16 * TILES // COUNT_RING)

            sp.wait_ge(CS.y, 1)

            def load_counts(c, b, k):
                if not isinstance(b, int) or b >= 3:
                    sp.wait_ge(CS.ud, c * NB + b - 2)
                elif c:
                    sp.wait_ge(CS.ud, c * NB)
                sp.dma_start(count_in[:, k, :, :], counts[bass.ds(b * WPB, WPB), :, :].rearrange("w p k -> p w k")
                             ).then_inc(counts_in[k], 16)

            for c in range(3):
                for b in range(3):
                    load_counts(c, b, b)
                with sp.Fori(1, NB // 3) as i:
                    for k in range(3):
                        load_counts(c, 3 * i + k, k)
                for b in range(NB // 3 * 3, NB):
                    load_counts(c, b, b % 3)
            sp.wait_ge(s_h, L + 1)
            sp.dma_start(out[0:FULL * P, :].rearrange("(b p) f -> p b f", p=P), hN[:, 0:FULL, :]).then_inc(s_out, 16)
            sp.dma_start(out[FULL * P:N, :], hN[0:REST, FULL, :]).then_inc(s_out, 16)
            sp.wait_ge(s_out, 32)

        @block.gpsimd
        def _(pool):
            pool.memset(pad_i[:, 0:GROUP], 0).then_inc(s_pad, 1)
            pool.memset(pad_i[:, GROUP:2 * GROUP], -1).then_inc(s_pad, 1)
            pool.memset(xN[:, FULL, :], 0.0).then_inc(s_zero, 1)
            pool.memset(erows[:, :, :], 0.0).then_inc(s_zero, 1)
            pool.iota(iota_row[:, :], pattern=[[1, P]], base=0, channel_multiplier=0,
                      allow_small_or_imprecise_dtypes=True).then_inc(s_iota, 1)
            pool.iota(block_minus[:, :], pattern=[[1, NB]], base=-NB, channel_multiplier=0,
                      allow_small_or_imprecise_dtypes=True).then_inc(s_iota, 1)
            pool.iota(group_id[:, :], pattern=[[P, GC]], base=0, channel_multiplier=1,
                      allow_small_or_imprecise_dtypes=True).then_inc(s_iota, 1)
            pool.iota(part_id[:, :], pattern=[[1, 1]], base=0, channel_multiplier=1,
                      allow_small_or_imprecise_dtypes=True).then_inc(s_iota, 1)
            pool.iota(iota_keys[:, :], pattern=[[1, max(WINS, KEYS)]], base=0, channel_multiplier=0,
                      allow_small_or_imprecise_dtypes=True).then_inc(s_iota, 1)
            pool.iota(tile_id[:, :], pattern=[[P, TC]], base=0, channel_multiplier=1,
                      allow_small_or_imprecise_dtypes=True).then_inc(s_iota, 1)
            def move_record(n, j):
                if not isinstance(j, int) or j:
                    pool.wait_ge(scattered[n], 16 * j)
                    pool.sem_inc(pool_turn, 1)
                pool.tensor_copy(place_now[:, :], place_i[:, bass.ds(j, 1)]).then_inc(s_record, 1)
                pool.tensor_copy(record_now[:, :], records[:, bass.ds(j, 1), :].rearrange("p o n -> p (o n)")).then_inc(s_record, 1)
                pool.wait_ge(s_record, 2 * (n * EC + j + 1))
                pool.sem_inc(pool_turn, 1)
                pool.indirect_dma_start(sorted_by[n], bass.IndirectOffsetOnAxis(ap=place_now[:, :], axis=0),
                                        record_now[:, :], None).then_inc(scattered[n], 16)

            pool.wait_ge(s_blk, 1)
            with pool.If(pool.value_load(unsorted[0:1, 0:1], min_val=0, max_val=1) == 1):
                for n in range(PASSES):
                    pool.wait_ge(s_place, n + 1)
                    move_record(n, 0)
                    with pool.Fori(1, EC) as j:
                        move_record(n, j)
                    pool.wait_ge(scattered[n], 16 * EC)
                    pool.sem_inc(s_moved, 1)
            pool.wait_ge(s_offs, 1)
            pool.wait_ge(s_ready, 1)
            for c in range(GC):
                for whole, there in ((src_list, srcG), (dst_list, dstG), (type_list, typG)):
                    pool.indirect_dma_start(there[:, c, :], None, whole,
                                            bass.IndirectOffsetOnAxis(ap=offs_i[:, c:c + 1], axis=0)).then_inc(s_groups, 16)

            def gathers(i, first, done, staged, index, source, width):
                each = TURN // GATHER_PARTS
                for h in range(GATHER_PARTS):
                    if not first:
                        pool.wait_ge(done, (i - 1) * TURN + (h + 1) * each)
                        pool.sem_inc(pool_turn, 1)
                    pool.tensor_copy(stage[:, h, :], index[:, bass.ds((i * TURN + h * each) * 2, 2 * each)]).then_inc(staged, 1)
                    pool.wait_ge(staged, i * GATHER_PARTS + h + 1)
                    pool.sem_inc(pool_turn, 1)
                    for k in range(each):
                        for t in range(2):
                            pool.indirect_dma_start(
                                msg[:, h * each + k, t, 0:width], None, source,
                                bass.IndirectOffsetOnAxis(ap=stage[:, h, 2 * k + t:2 * k + t + 1], axis=0),
                            ).then_inc(gathered[h * each + k], 16)

            def all_gathers(done, staged, index, source, width):
                gathers(0, True, done, staged, index, source, width)
                with pool.Fori(1, TURNS) as i:
                    gathers(i, False, done, staged, index, source, width)

            rows_flat = row_col[:, :, :].rearrange("p g t -> p (g t)")
            pool.wait_ge(s_col, 2)
            for l in range(L):
                for i in range(2):
                    pool.wait_ge(rows_stored[l][i], 16 * ((NB + 1 - i) // 2))
                if l:
                    pool.wait_ge(LS[l - 1].ud, NG)
                all_gathers(LS[l].ud, LS[l].staged, rows_flat, table, ROW)
                if l == 0:
                    pool.wait_ge(s_tiles, 1)
                    for c in range(TC):
                        for whole, there in ((src_list, srcT), (dst_list, dstT)):
                            pool.indirect_dma_start(there[:, c, :], None, whole,
                                                    bass.IndirectOffsetOnAxis(ap=tile_off[:, c:c + 1], axis=0)
                                                    ).then_inc(s_tile_edges, 16)

        @block.vector
        def _(dve):
            chain = [0]

            def link(ins):
                chain[0] += 1
                ins.then_inc(dve_chain, 1)
                dve.wait_ge(dve_chain, chain[0])

            dve.wait_ge(s_iota, 6)
            link(dve.memset(ones[:, :], 1.0))
            dve.wait_ge(s_dst, 16)
            for b in range(NB + 1):
                link(dve.tensor_scalar(junk[:, :], dst_sp[:, :], float(b * P), 0.0, ALU.is_lt, ALU.add,
                                       accum_out=below[:, b:b + 1]))
            dve.wait_ge(s_next, 16)
            dve.scalar_tensor_tensor(junk, dst_sp, 1.0, dst_next, ALU.mult, ALU.is_gt,
                                     accum_out=below[:, NB + 1:NB + 2]).then_inc(s_below, 1)
            dve.wait_ge(s_start, 1)
            link(dve.tensor_copy(start[:, :], bank[0][:, 0:NB + 2]))
            link(dve.tensor_scalar(unsorted[:, :], start[:, NB + 1:NB + 2], 1.5, None, ALU.is_gt))
            dve.engine_nop().then_inc(s_blk, 1)

            def sort():
                steps = [0]

                def then(ins):
                    steps[0] += 1
                    ins.then_inc(sort_chain, 1)
                    dve.wait_ge(sort_chain, steps[0])

                dve.wait_ge(s_load, 16 * 3)
                then(dve.memset(records, 0))
                for n in range(3):
                    then(dve.tensor_copy(records[:, :, n], plain[:, n, :]))
                then(dve.tensor_scalar(earlier, iota_row[:, :], part_id[:, 0:1], None, ALU.is_gt))
                for n in range(PASSES):
                    if n:
                        dve.wait_ge(s_load, 16 * (3 + n))
                    then(dve.tensor_copy(place_i, records[:, :, 1]))
                    then(dve.tensor_single_scalar(place_i, place_i, DIGIT_BITS * n, ALU.arith_shift_right))
                    then(dve.tensor_single_scalar(place_i, place_i, DIGITS - 1, ALU.bitwise_and))
                    then(dve.tensor_copy(digit, place_i))
                    then(dve.memset(number[:, :, :], 0.0))
                    for d in range(DIGITS):
                        then(dve.tensor_scalar(same, digit, float(d), 0.0, ALU.is_equal, ALU.add,
                                               accum_out=number[0:EDGE_SPLIT, 0, d:d + 1]))
                    dve.engine_nop().then_inc(s_number, 1)
                    dve.wait_ge(s_before, n + 1)
                    then(dve.tensor_copy(number[:, 1:3, :], bank[0][:, 0:2 * DIGITS].rearrange("p (i d) -> p i d", i=2)))
                    then(dve.tensor_tensor_scan(number[:, 3, :], ones[:, 0:DIGITS], number[:, 2, :], 0.0, ALU.mult, ALU.add))
                    then(dve.tensor_tensor(number[:, 3, :], number[:, 3, :], number[:, 2, :], ALU.subtract))
                    then(dve.tensor_tensor(number[:, 3, :], number[:, 3, :], number[:, 1, :], ALU.add))
                    then(dve.memset(place_of, -1.0))
                    for d in range(DIGITS):
                        then(dve.tensor_scalar(same, digit, float(d), None, ALU.is_equal))
                        then(dve.tensor_tensor_scan(upto, ones[0:EDGE_SPLIT, 0:1].to_broadcast([EDGE_SPLIT, EC]), same, 0.0,
                                                    ALU.mult, ALU.add))
                        then(dve.scalar_tensor_tensor(upto, upto, number[0:EDGE_SPLIT, 3, d:d + 1], same, ALU.add, ALU.mult))
                        then(dve.tensor_tensor(place_of, place_of, upto, ALU.add))
                    then(dve.tensor_copy(place_i, place_of))
                    dve.engine_nop().then_inc(s_place, 1)
                dve.wait_ge(s_load, 16 * (3 + PASSES))
                for n in range(3):
                    then(dve.tensor_copy(plain[:, n, :], records[:, :, n]))
                dve.engine_nop().then_inc(s_place, 1)

            with dve.If(dve.value_load(unsorted[0:1, 0:1], min_val=0, max_val=1) == 1):
                sort()
            link(dve.tensor_tensor(nb_f[:, :], start[:, 1:NB + 1], start[:, 0:NB], ALU.subtract))
            link(dve.tensor_scalar(nb_i[:, :], nb_f[:, :], float(GROUP - 1), None, ALU.add))
            link(dve.tensor_single_scalar(nb_i[:, :], nb_i[:, :], 8, ALU.arith_shift_right))
            link(dve.tensor_copy(nb_f[:, :], nb_i[:, :]))
            link(dve.tensor_tensor_scan(ge[:, :], ones[:, 0:NB], nb_f[:, :], 0.0, ALU.mult, ALU.add))
            link(dve.tensor_tensor(gs[:, :], ge[:, :], nb_f[:, :], ALU.subtract))
            link(dve.scalar_tensor_tensor(off[:, :], gs[:, :], -float(GROUP), start[:, 0:NB], ALU.mult, ALU.add))
            link(dve.tensor_scalar(off[:, :], off[:, :], -float(E), None, ALU.add))
            link(dve.tensor_scalar(g256[:, :], group_id[:, :], float(GROUP), None, ALU.mult))
            for c in range(GC):
                link(dve.tensor_scalar(t25[:, c, :], gs[:, :], group_id[:, c:c + 1], None, ALU.is_le))
                link(dve.scalar_tensor_tensor(ind[:, c, :], ge[:, :], group_id[:, c:c + 1], t25[:, c, :], ALU.is_gt, ALU.mult))
                link(dve.tensor_tensor(t25[:, c, :], ind[:, c, :], block_minus[:, :], ALU.mult))
                link(dve.tensor_reduce(blk[:, c:c + 1], t25[:, c, :], AX_X, ALU.add))
                link(dve.scalar_tensor_tensor(t25[:, c, :], off[:, :], g256[:, c:c + 1], ind[:, c, :], ALU.add, ALU.mult))
                link(dve.tensor_reduce(offs[:, c:c + 1], t25[:, c, :], AX_X, ALU.add))
            link(dve.tensor_scalar(offs_i[:, :], offs[:, :], float(E), None, ALU.add))
            link(dve.tensor_scalar(blk_i[:, :], blk[:, :], float(NB), None, ALU.add))
            link(dve.tensor_scalar(blk128[:, :], blk[:, :], float(NB), float(P), ALU.add, ALU.mult))
            dve.engine_nop().then_inc(s_offs, 1)
            dve.engine_nop().then_inc(s_blk, 1)
            link(dve.tensor_tensor(sqf[:, 0:P], iota_row[:, :], iota_row[:, :], ALU.mult))
            link(dve.tensor_copy(sqi[:, 0, 0:P], sqf[:, 0:P]))
            link(dve.tensor_single_scalar(sqi[:, 1, 0:P], sqi[:, 0, 0:P], 255, ALU.bitwise_and))
            link(dve.tensor_copy(sqf[:, P:2 * P], sqi[:, 1, 0:P]))
            link(dve.tensor_tensor(sqf[:, 0:P], sqf[:, 0:P], sqf[:, P:2 * P], ALU.subtract))
            link(dve.memset(sqf[:, 2 * P:3 * P], 0.0))
            for row, part, weight in ((24, sqf[:, 0:P], -MASK_UNIT), (25, sqf[:, P:2 * P], -MASK_UNIT),
                                      (26, iota_row[:, :], 2 * MASK_UNIT), (27, ones[:, :], -MASK_UNIT),
                                      (28, ones[:, :], -MASK_UNIT)):
                link(dve.tensor_scalar(bst[:, 0, 0:1], part_id[:, 0:1], float(row), weight, ALU.is_equal, ALU.mult))
                link(dve.scalar_tensor_tensor(sqf[:, 2 * P:3 * P], part, bst[:, 0, 0:1], sqf[:, 2 * P:3 * P],
                                              ALU.mult, ALU.add))
            link(dve.tensor_copy(mask_w[:, :], sqf[:, 2 * P:3 * P]))
            link(dve.tensor_scalar(ident[:, :], iota_row[:, :], part_id[:, 0:1], None, ALU.is_equal))
            link(dve.tensor_copy(ident_b[:, :], ident[:, :]))
            link(dve.tensor_copy(iota_b[:, :], iota_keys[:, 0:KEYS]))
            link(dve.tensor_scalar(win[:, 0, 0:WPB], iota_keys[:, 0:WPB], float(WINDOW), None, ALU.mult))
            link(dve.tensor_scalar(win[:, 1, 0:WPB], win[:, 0, 0:WPB], part_id[:, 0:1], None, ALU.is_le))
            link(dve.tensor_scalar(win[:, 2, 0:1], part_id[:, 0:1], -float(WINDOW), None, ALU.add))
            link(dve.scalar_tensor_tensor(in_window[:, :], win[:, 0, 0:WPB], win[:, 2, 0:1], win[:, 1, 0:WPB], ALU.is_gt, ALU.mult))
            link(dve.memset(running[:, :, :], 0.0))
            link(dve.memset(rows_out[:, :, :, :], 1.0))
            link(dve.memset(aiT[:, :, :], 0.0))
            link(dve.memset(deg[:, :], 0.0))
            link(dve.memset(fresh[:, :], 0.0))
            dve.memset(blk_row[:, SLOTS:SLOTS + 16], 0).then_inc(s_const, 1)
            dve.wait_ge(s_x, 32)
            dve.wait_ge(s_w, 16 * 4 * L)

            def blocks(first, count):
                return nc.values_load_multi_w_load_instructions(
                    blk_row[0:1, bass.ds(first, count)], engines=(mybir.EngineType.DVE,), min_val=0, max_val=NB,
                    skip_runtime_bounds_check_because="a group's block is 0 to NB by its construction")[1]

            def per_block(column):
                return column.unsqueeze(2).to_broadcast([P, NB, F])

            def square_root(n):
                dve.engine_nop().then_inc(sq_req, 1)
                dve.wait_ge(sq_done, n + 1)

            def layer_norm(buf, result, n):
                square = H1[:, 0, :].rearrange("p (b f) -> p b f", f=F)
                link(dve.tensor_reduce(stat[:, 0, :], buf[:, :, :], AX_X, ALU.add))
                link(dve.tensor_scalar(stat[:, 0, :], stat[:, 0, :], 1.0 / F, None, ALU.mult))
                link(dve.tensor_tensor(buf[:, :, :], buf[:, :, :], per_block(stat[:, 0, :]), ALU.subtract))
                link(dve.tensor_tensor(square, buf[:, :, :], buf[:, :, :], ALU.mult))
                link(dve.tensor_reduce(stat[:, 1, :], square, AX_X, ALU.add))
                link(dve.tensor_scalar(stat[:, 1, :], stat[:, 1, :], 1.0 / F, EPS_LN, ALU.mult, ALU.add))
                square_root(n)
                link(dve.reciprocal(stat[:, 2, :], stat[:, 1, :]))
                link(dve.tensor_tensor(result[:, :, :], buf[:, :, :], per_block(stat[:, 2, :]), ALU.mult))

            def edges_of_groups():
                dve.wait_ge(s_groups, 16 * 3 * GC)
                link(dve.scalar_tensor_tensor(fG[:, 0, :, :], srcG[:, :, :], float(R), typG[:, :, :], ALU.mult, ALU.add))
                for c in range(GC):
                    link(dve.tensor_scalar(fG[:, 1, c, :], dstG[:, c, :], blk128[:, c:c + 1], None, ALU.subtract))
                dve.engine_nop().then_inc(s_fG, 1)
                typ = typG[:, :, :].rearrange("p c e -> p (c e)")
                for r in range(R):
                    link(dve.tensor_scalar(rowsG[:, r, :], typ, float(r), None, ALU.is_equal))
                link(dve.memset(rowsG[:, R, :], 1.0))
                place = fG[:, 1, :, :].rearrange("p c e -> p (c e)")
                link(dve.tensor_scalar(sqf[:, :], place, -64.0, 200.0, ALU.max, ALU.min))
                link(dve.tensor_copy(rowsG[:, R + 1, :], sqf[:, :]))
                link(dve.tensor_tensor(sqi[:, 0, :], sqf[:, :], sqf[:, :], ALU.mult))
                link(dve.tensor_single_scalar(sqi[:, 1, :], sqi[:, 0, :], 255, ALU.bitwise_and))
                link(dve.tensor_copy(rowsG[:, R + 3, :], sqi[:, 1, :]))
                link(dve.tensor_tensor(rowsG[:, R + 2, :], sqi[:, 0, :], sqi[:, 1, :], ALU.subtract))
                dve.engine_nop().then_inc(s_rows, 1)
                for h in range(2):
                    dve.wait_ge(s_colT, h + 1)
                    link(dve.tensor_copy(row_col[:, :, h], bank[1 + h][:, 0:SLOTS]))
                    dve.engine_nop().then_inc(s_col, 1)
                dve.wait_ge(s_blk_ld, 16)
                link(dve.tensor_copy(blk_bc[0:1, 1:SLOTS + 1], blk_row[:, 0:SLOTS]))
                link(dve.memset(blk_bc[0:1, 0:1], -1.0))
                dve.tensor_tensor(fresh[0:1, :], blk_bc[0:1, 1:SLOTS + 1], blk_bc[0:1, 0:SLOTS],
                                  ALU.not_equal).then_inc(s_blkf, 1)
                dve.wait_ge(s_fresh, 1)
                link(dve.tensor_scalar(fresh[:, :], bank[0][:, 0:SLOTS], 3e38, -3e38, ALU.mult, ALU.add))
                link(dve.scalar_tensor_tensor(fresh[:, :], bank[0][:, 0:SLOTS], NO_MAX, fresh[:, :], ALU.mult, ALU.add))
                dve.engine_nop().then_inc(s_blkf, 1)

            def tiles_of_windows():
                n_win, start_w, n_tiles, end_t, first_t, off_w, t = (win[:, i, :] for i in range(7))
                one_row = ones[:, 0:1].to_broadcast([P, WINS])
                link(dve.tensor_tensor(win[:, 6, :].rearrange("p (b w) -> p b w", w=WPB),
                                       deg[:, 0:NB].unsqueeze(2).to_broadcast([P, NB, WPB]),
                                       in_window[:, :].unsqueeze(1).to_broadcast([P, NB, WPB]), ALU.mult))
                dve.engine_nop().then_inc(s_win_deg, 1)
                dve.wait_ge(s_win_n, 1)
                link(dve.tensor_copy(n_win, bank[0][:, 0:WINS]))
                link(dve.tensor_tensor_scan(start_w, one_row, n_win, 0.0, ALU.mult, ALU.add))
                link(dve.tensor_tensor(start_w, start_w, n_win, ALU.subtract))
                link(dve.tensor_scalar(win_i[:, :], n_win, float(P - 1), None, ALU.add))
                link(dve.tensor_single_scalar(win_i[:, :], win_i[:, :], SHIFT, ALU.arith_shift_right))
                link(dve.tensor_scalar(n_tiles, win_i[:, :], 1.0, None, ALU.max))
                link(dve.tensor_tensor_scan(end_t, one_row, n_tiles, 0.0, ALU.mult, ALU.add))
                link(dve.tensor_tensor(first_t, end_t, n_tiles, ALU.subtract))
                link(dve.scalar_tensor_tensor(off_w, first_t, -float(P), start_w, ALU.mult, ALU.add))
                link(dve.tensor_scalar(off_w, off_w, -float(E), None, ALU.add))
                link(dve.tensor_scalar(tile_num[:, 5, :], tile_id[:, :], float(P), None, ALU.mult))
                for c in range(TC):
                    link(dve.tensor_scalar(t, first_t, tile_id[:, c:c + 1], None, ALU.is_le))
                    link(dve.scalar_tensor_tensor(n_win, end_t, tile_id[:, c:c + 1], t, ALU.is_gt, ALU.mult))
                    for n, (a, scalar, op) in enumerate(((iota_keys[:, 0:WINS], 1.0, ALU.mult), (off_w, tile_num[:, 5, c:c + 1], ALU.add),
                                                         (end_t, 1.0, ALU.mult), (first_t, 1.0, ALU.mult))):
                        link(dve.scalar_tensor_tensor(t, a, scalar, n_win, op, ALU.mult, accum_out=tile_num[:, n, c:c + 1]))
                window, first_edge, end, first, last, _ = (tile_num[:, n, :] for n in range(6))
                link(dve.tensor_scalar(tile_off[:, :], first_edge, float(E), None, ALU.add))
                link(dve.tensor_scalar(last, tile_id[:, :], 1.0, None, ALU.add))
                link(dve.tensor_tensor(last, last, end, ALU.is_equal))
                spare = win[:, 6, 0:TC]
                link(dve.tensor_copy(win_i[:, 0:1], part_id[:, 0:1]))
                link(dve.tensor_single_scalar(win_i[:, 0:1], win_i[:, 0:1], COUNT_RING - 1, ALU.bitwise_and))
                link(dve.tensor_scalar(win[:, 5, 0:1], win_i[:, 0:1], float(WINS), None, ALU.add))
                link(dve.tensor_scalar(spare, window, win[:, 5, 0:1], None, ALU.subtract))
                link(dve.tensor_tensor(spare, spare, last, ALU.mult))
                link(dve.tensor_scalar(tile_dest[:, :], spare, win[:, 5, 0:1], None, ALU.add))
                dve.engine_nop().then_inc(s_tiles, 1)
                link(dve.tensor_tensor(first, first, tile_id[:, :], ALU.not_equal))
                link(dve.tensor_tensor(keyT, ident[:, :].unsqueeze(1).to_broadcast([P, TC, P]),
                                       first.unsqueeze(2).to_broadcast([P, TC, P]), ALU.mult))
                dve.engine_nop().then_inc(s_keep, 1)

            def keys_of_tiles():
                window = tile_num[:, 0, :]
                for n in range(-(-TC // 4)):
                    w = min(4, TC - 4 * n) * P
                    dve.wait_ge(s_keep_bc, 1)
                    link(dve.tensor_copy(keep[:, 512 * n:512 * n + w], bank[1 + n][:, 0:w]))
                dve.wait_ge(s_tile_edges, 16 * 2 * TC)
                link(dve.tensor_scalar(window, window, float(WINDOW), None, ALU.mult))
                link(dve.tensor_tensor(placeT, dstT, window.unsqueeze(2).to_broadcast([P, TC, P]), ALU.subtract))
                link(dve.tensor_scalar(validT, placeT, 0.0, float(WINDOW - 1), ALU.max, ALU.min))
                link(dve.tensor_tensor(validT, validT, placeT, ALU.is_equal))
                link(dve.tensor_single_scalar(highT, srcT, SHIFT, ALU.arith_shift_right))
                link(dve.scalar_tensor_tensor(keyT, placeT, float(NB), highT, ALU.mult, ALU.add))
                link(dve.scalar_tensor_tensor(keyT, keyT, 1.0, validT, ALU.add, ALU.mult))
                link(dve.tensor_scalar(keyT, keyT, -1.0, None, ALU.add))
                link(dve.tensor_single_scalar(highT, srcT, P - 1, ALU.bitwise_and))
                link(dve.tensor_copy(lowT, highT))
                dve.engine_nop().then_inc(s_keys, 1)
                dve.wait_ge(s_keyT, 1)
                for n in range(-(-TC // 4)):
                    w = min(4, TC - 4 * n) * P
                    link(dve.tensor_copy(key_col[:, 512 * n:512 * n + w], bank[1 + n][:, 0:w]))
                    link(dve.tensor_copy(low_col[:, 512 * n:512 * n + w], bank[4 + n][:, 0:w]))
                dve.engine_nop().then_inc(s_keys, 1)

            for l in range(L):
                s = LS[l]
                dve.engine_nop().then_inc(s_h, 1)
                if l:
                    tiles_of_windows()
                for r in range(R):
                    dve.wait_ge(s.wt, r + 1)
                    if r >= 2:
                        dve.wait_ge(s.wqk, r - 1)
                    dve.tensor_copy(WT[:, r % 2, :], bank[6 + r % 2][:, 0:P]).then_inc(s.wts, 1)
                dve.wait_ge(s.wqk, R)
                dve.tensor_copy(Wqk[:, :, :], bank[5][:, 0:2 * R].rearrange("p (r o) -> p o r", o=2)).then_inc(s.wqks, 1)

                def move_block(b):
                    dve.wait_ge(s.tr, b + 1)
                    if b >= 2:
                        dve.wait_ge(s.mm, b - 1)
                    dve.tensor_copy(hTs[:, b % 2, :], bank[6 + b % 2][:, 0:P]).then_inc(s.hts, 1)

                move_block(0)
                for b in range(NB):
                    if b + 1 < NB:
                        move_block(b + 1)
                    dve.wait_ge(s.mm, b + 1)
                    if b >= 2:
                        dve.wait_ge(rows_stored[l][b % 2], 16 * (b // 2))
                    half = 3 * (b % 2)
                    link(dve.tensor_copy(rows_out[:, b % 2, R // 2:R, 0:F],
                                         bank[half + 1][:, :].rearrange("p (r f) -> p r f", f=F)))
                    link(dve.tensor_copy(rows_out[:, b % 2, :, F + 1], bank[half + 2][:, R:2 * R]))
                    dve.tensor_copy(ai[:, b, :], bank[half + 2][:, 0:R]).then_inc(s.evb, 1)
                dve.wait_ge(s.evb, NB)
                link(dve.tensor_copy(ai_parts[:, :, 0:R], ai[:, :, :]))
                link(dve.tensor_tensor(ai_rest[:, :, :], ai[:, :, :], ai_parts[:, :, 0:R], ALU.subtract))
                link(dve.tensor_copy(ai_parts[:, :, R:2 * R], ai_rest[:, :, :]))
                link(dve.tensor_tensor(ai_rest[:, :, :], ai_rest[:, :, :], ai_parts[:, :, R:2 * R], ALU.subtract))
                dve.tensor_copy(ai_parts[:, :, 2 * R:3 * R], ai_rest[:, :, :]).then_inc(s.aip, 1)
                if l:
                    keys_of_tiles()
                else:
                    edges_of_groups()
                link(dve.memset(acc_flat, 0.0))
                link(dve.memset(neg_max[:, :], NO_MAX))

                def accumulate(g, k, b):
                    dve.wait_ge(s.ud, g + 1)
                    dve.wait_ge(s.cd, g + 1)
                    at_least(dve, s.ad, g)
                    dve.scalar_tensor_tensor(acc[:, bass.ds(b, 1), :].rearrange("p o c -> p (o c)"),
                                             acc[:, bass.ds(b, 1), :].rearrange("p o c -> p (o c)"),
                                             shrink[:, k % 4:k % 4 + 1],
                                             bank[4 + k % 2][:, 0:ROW], ALU.mult, ALU.add).then_inc(s.ad, 1)

                def maximum(g, k):
                    m, prev = k % 4, (k + 3) % 4
                    dve.wait_ge(s.fd, g + 1)
                    at_least(dve, s.pd, g - 1)
                    if l == 0:
                        at_least(dve, s.kd, g - 1)
                    dve.sem_inc(dve_turn, 1)
                    dve.tensor_tensor_reduce(logit[:, k % 2, :], bank[k % 2][:, 0:GROUP], lift[:, k % 2, :], 1.0, -3e38,
                                             ALU.add, ALU.max, here[:, m:m + 1]).then_inc(s.ld, 1)
                    at_least(dve, s.nd, g)
                    dve.tensor_tensor(neg_old[:, m:m + 1], neg_max[:, prev:prev + 1], fresh[:, bass.ds(g, 1)],
                                      ALU.max).then_inc(s.no, 1)

                def new_maximum(g, k):
                    m = k % 4
                    at_least(dve, s.cd, g - 3)
                    dve.wait_ge(s.ld, g + 1)
                    dve.wait_ge(s.no, g + 1)
                    dve.scalar_tensor_tensor(neg_max[:, m:m + 1], here[:, m:m + 1], -1.0, neg_old[:, m:m + 1],
                                             ALU.mult, ALU.min).then_inc(s.nd, 1)

                def count_group(g, k):
                    dve.wait_ge(s.ld, g + 1)
                    at_least(dve, s.dd, g - 1)
                    dve.tensor_scalar(cjunk[:, k % 2, :], logit[:, k % 2, :], FEW, 0.0, ALU.is_gt, ALU.add,
                                      accum_out=cnt[:, k % 2:k % 2 + 1]).then_inc(s.kd, 1)

                def add_degrees(g, k, b):
                    dve.wait_ge(s.kd, g + 1)
                    at_least(dve, s.dd, g)
                    dve.tensor_tensor(deg[:, bass.ds(b, 1)], deg[:, bass.ds(b, 1)], cnt[:, k % 2:k % 2 + 1],
                                      ALU.add).then_inc(s.dd, 1)

                def tile_one_hots(g, k, j):
                    t, place = g * TILES_PER_GROUP + j, (k * TILES_PER_GROUP + j) % (2 * TILES_PER_GROUP)
                    dve.tensor_scalar(oh_low[:, place, :], iota_b[:, 0:P], low_col[:, bass.ds(t, 1)], None,
                                      ALU.is_equal).then_inc(s.oh, 1)
                    dve.tensor_scalar(oh_key[:, place, :], iota_b[:, :], key_col[:, bass.ds(t, 1)], None,
                                      ALU.is_equal).then_inc(s.oh, 1)

                def run_counts(g, k, i, j):
                    t, kt = g * TILES_PER_GROUP + j, k * TILES_PER_GROUP + j
                    if j == 0:
                        dve.wait_ge(s.cm, (g + 1) * TILES_PER_GROUP)
                    at_least(dve, counted[kt % COUNT_RING],
                             16 * (i * (TURN * TILES_PER_GROUP // COUNT_RING) + kt // COUNT_RING))
                    at_least(dve, s.rn, t)
                    dve.scalar_tensor_tensor(running[:, kt % COUNT_RING, :], running[:, (kt - 1) % COUNT_RING, :],
                                             keep[:, bass.ds(t, 1)],
                                             bank[6 + j // 2][:, (j % 2) * KEYS:(j % 2 + 1) * KEYS],
                                             ALU.mult, ALU.add).then_inc(s.rn, 1)

                def turn(i):
                    first = isinstance(i, int)
                    b = [None, None, *blocks(0, TURN)] if first else blocks(i * TURN - 2, TURN + 2)
                    for k in range(TURN):
                        g = i * TURN + k
                        if not first or k >= 2:
                            accumulate(g - 2, (k - 2) % TURN, b[k])
                        if l:
                            for j in range(TILES_PER_GROUP):
                                if j == TILES_PER_GROUP - 1:
                                    maximum(g, k)
                                if not first or k >= 2:
                                    run_counts(g - 2, (k - 2) % TURN, i if k >= 2 else i - 1, j)
                                if j == TILES_PER_GROUP - 1:
                                    new_maximum(g, k)
                                tile_one_hots(g, k, j)
                        else:
                            maximum(g, k)
                            count_group(g, k)
                            new_maximum(g, k)
                            add_degrees(g, k, b[k + 2])

                turn(0)
                with dve.Fori(1, TURNS) as i:
                    turn(i)
                b = blocks(NG - 2, 2)
                accumulate(NG - 2, TURN - 2, b[0])
                if l:
                    for g, k in ((NG - 2, TURN - 2), (NG - 1, TURN - 1)):
                        for j in range(TILES_PER_GROUP):
                            run_counts(g, k, TURNS - 1, j)
                accumulate(NG - 1, TURN - 1, b[1])
                dve.wait_ge(s.ad, NG)
                link(dve.tensor_scalar(stat[:, 0, :], acc[:, 0:NB, F], 1e-16, None, ALU.add))
                link(dve.reciprocal(stat[:, 1, :], stat[:, 0, :]))
                link(dve.tensor_tensor(hN[:, :, :], acc[:, 0:NB, 0:F], per_block(stat[:, 1, :]), ALU.mult))
                link(dve.tensor_tensor(hN[:, :, :], hN[:, :, :], bias_bc[:, l, :].unsqueeze(1).to_broadcast([P, NB, F]), ALU.add))
                link(dve.tensor_scalar(hN[:, :, :], hN[:, :, :], 0.0, None, ALU.max))
            dve.wait_ge(LS[0].dd, NG)
            link(dve.tensor_tensor(hN[:, :, :], hN[:, :, :], xN[:, :, :], ALU.add))
            layer_norm(hN, xN, 0)
            link(dve.tensor_scalar(dinv[:, :], deg[:, 0:NB], 1.0, None, ALU.add))
            square_root(1)
            link(dve.reciprocal(dinv[:, :], dinv[:, :]))
            link(dve.tensor_tensor(work[:, :, :], xN[:, :, :], per_block(dinv[:, :]), ALU.mult))
            dve.wait_ge(s_par, 16 * 15)

            for c in range(3):
                s = CS
                _, chunks, acts = conv_before(c)
                dve.engine_nop().then_inc(s.y, 1)
                halves = 2 if c == 0 else 1
                if c == 0:
                    for q, (o, n) in enumerate(NCH):
                        dve.wait_ge(s.tr, chunks + q + 1)
                        dve.tensor_copy(hT[:, o:o + n], bank[q % 2][:, 0:n]).then_inc(s.trs, 1)
                dve.wait_ge(s.act, acts + halves * QN)
                for v in range(halves):
                    link(dve.tensor_reduce(bst[:, 0, v:v + 1], H1[:, v, 0:N], AX_X, ALU.add))
                    link(dve.tensor_scalar(bst[:, 0, v:v + 1], bst[:, 0, v:v + 1], 1.0 / N, None, ALU.mult))
                    link(dve.tensor_scalar(H1[:, v, :], H1[:, v, :], bst[:, 0, v:v + 1], None, ALU.subtract))
                    link(dve.scalar_tensor_tensor(hT[:, 0:N], H1[:, v, 0:N], 1.0, H1[:, v, 0:N], ALU.mult, ALU.mult,
                                                  accum_out=bst[:, 1, v:v + 1]))
                link(dve.tensor_scalar(bst[:, 1, 0:halves], bst[:, 1, 0:halves], 1.0 / N, EPS_BN, ALU.mult, ALU.add))
                square_root(2 + c)
                link(dve.reciprocal(bst[:, 2, 0:halves], bst[:, 1, 0:halves]))
                col = 0 if c == 0 else c + 1
                link(dve.tensor_tensor(bst[:, 2, 0:halves], bst[:, 2, 0:halves], bn_par[:, 1, col:col + halves], ALU.mult))
                for v in range(halves):
                    link(dve.tensor_scalar(H1[:, v, :], H1[:, v, :], bst[:, 2, v:v + 1],
                                           bn_par[:, 2, col + v:col + v + 1], ALU.mult, ALU.add))
                dve.engine_nop().then_inc(s.bn, 1)
                for q, (o, n) in enumerate(NCH):
                    dve.wait_ge(s.mm2, chunks + q + 1)
                    b0, nb = o // F, n // F
                    got = bank[6 + q % 2][:, 0:n].rearrange("p (b f) -> p b f", f=F)
                    if c < 2:
                        dve.tensor_tensor(work[:, b0:b0 + nb, :], got,
                                          dinv[:, b0:b0 + nb].unsqueeze(2).to_broadcast([P, nb, F]), ALU.mult).then_inc(s.y2, 1)
                    else:
                        dve.tensor_tensor(hN[:, b0:b0 + nb, :], got, xN[:, b0:b0 + nb, :], ALU.add).then_inc(s.y2, 1)
                dve.wait_ge(s.y2, chunks + QN)
            layer_norm(hN, hN, 5)
            dve.engine_nop().then_inc(s_h, 1)

        @block.scalar
        def _(act):
            def blocks(first, count):
                return nc.values_load_multi_w_load_instructions(
                    blk_row[0:1, bass.ds(first, count)], engines=(mybir.EngineType.Activation,), min_val=0, max_val=NB,
                    skip_runtime_bounds_check_because="a group's block is 0 to NB by its construction")[1]

            act.wait_ge(s_const, 1)
            act.wait_ge(s_blk_ld, 16)
            for l in range(L):
                s = LS[l]
                for b in range(NB):
                    act.wait_ge(s.mm, b + 1)
                    if b >= 2:
                        act.wait_ge(rows_stored[l][b % 2], 16 * (b // 2))
                    act.activation(rows_out[:, b % 2, 0:R // 2, 0:F],
                                   bank[3 * (b % 2)][:, :].rearrange("p (r f) -> p r f", f=F), ACT.Copy).then_inc(s.eva, 1)
                if l:
                    act.wait_ge(LS[l - 1].ais, NG + 1)
                act.wait_ge(s.ait, 1)
                for j in range(-(-NB // 8)):
                    nb = min(8, NB - 8 * j)
                    act.activation(aiT[0:ROWS_RELATION, 8 * j:8 * j + nb, :],
                                   bank[j][0:ROWS_RELATION, :].bitcast(BF16)[:, 0:nb * P].rearrange("p (b f) -> p b f", f=P),
                                   ACT.Copy).then_inc(s.aits, 1)
                act.wait_ge(s.aits, -(-NB // 8))

                def stage_ai(g, k, b):
                    at_least(act, s.xd, g - 1)
                    act.sem_inc(act_turn, 1)
                    act.activation(aiS[:, k % 2, :], aiT[:, bass.ds(b, 1), :].rearrange("p o d -> p (o d)"),
                                   ACT.Copy).then_inc(s.ais, 1)

                def exps(g, k):
                    m = k % 4
                    act.wait_ge(s.nd, g + 1)
                    at_least(act, s.td, g - 1)
                    act.activation(prob[:, k % 2, :], logit[:, k % 2, :], ACT.Exp, bias=neg_max[:, m:m + 1]).then_inc(s.pd, 1)
                    at_least(act, s.ad, g - 3)
                    act.activation(shrink[:, m:m + 1], neg_old[:, m:m + 1], ACT.Exp, bias=neg_max[:, m:m + 1],
                                   scale=-1.0).then_inc(s.cd, 1)

                def lifts(g, k):
                    act.wait_ge(s.xd, g + 1)
                    at_least(act, s.ld, g - 1)
                    act.activation(lift[:, k % 2, :], bank[k % 2][:, 0:GROUP], ACT.Relu, scale=-0.8).then_inc(s.fd, 1)

                def move_probs(g, k):
                    act.wait_ge(s.td, g + 1)
                    at_least(act, s.ud, g - 1)
                    act.activation(probT[:, k % 2, :], bank[2 + k % 2][:, 0:GROUP], ACT.Copy).then_inc(s.ptd, 1)

                def turn(i):
                    first = isinstance(i, int)
                    b = blocks(i * TURN + 1, TURN)
                    for k in range(TURN):
                        g = i * TURN + k
                        if not first or k >= 1:
                            exps(g - 1, (k - 1) % TURN)
                        lifts(g, k)
                        stage_ai(g + 1, (k + 1) % TURN, b[k])
                        if not first or k >= 1:
                            move_probs(g - 1, (k - 1) % TURN)

                stage_ai(0, 0, blocks(0, 2)[0])
                turn(0)
                with act.Fori(1, TURNS) as i:
                    turn(i)
                exps(NG - 1, TURN - 1)
                move_probs(NG - 1, TURN - 1)

            def square_root(n, what):
                act.wait_ge(sq_req, n + 1)
                act.activation(what, what, ACT.Sqrt).then_inc(sq_done, 1)

            square_root(0, stat[:, 1, :])
            square_root(1, dinv[:, :])
            act.wait_ge(s_par, 16 * 15)
            for c in range(3):
                s = CS
                done, chunks, acts = conv_before(c)
                col = 0 if c == 0 else c + 1
                func = ACT.Relu if c < 2 else ACT.Identity

                def scale_sums(b, k):
                    act.wait_ge(s.ud, done + b + 1)
                    act.sem_inc(act_turn, 1)
                    act.activation(hN[:, bass.ds(b, 1), :].rearrange("p o f -> p (o f)"), bank[k][:, 0:F], ACT.Copy,
                                   scale=dinv[:, bass.ds(b, 1)]).then_inc(s.ev, 1)

                with act.Fori(0, NB // 3) as i:
                    for k in range(3):
                        scale_sums(3 * i + k, k)
                for b in range(NB // 3 * 3, NB):
                    scale_sums(b, b % 3)
                if c == 0:
                    for n, (v, (o, w)) in enumerate((v, ch) for v in range(2) for ch in NCH):
                        act.wait_ge(s.mm, n + 1)
                        act.activation(H1[:, v, o:o + w], bank[2 + n % 4][:, 0:w], func,
                                       bias=bn_par[:, 0, v:v + 1]).then_inc(s.act, 1)
                else:
                    for q, (o, w) in enumerate(NCH):
                        act.wait_ge(s.tr, chunks + q + 1)
                        act.activation(H1[:, 0, o:o + w], bank[q % 2][:, 0:w], func,
                                       bias=bn_par[:, 0, col:col + 1]).then_inc(s.act, 1)
                square_root(2 + c, bst[:, 1, 0:2 if c == 0 else 1])
            square_root(5, stat[:, 1, :])

        @block.tensor
        def _(pe):
            pe.wait_ge(s_below, 1)
            pe.matmul(bank[0][:, 0:NB + 2], ones[0:EDGE_SPLIT, :], below[:, :], start=True, stop=True).then_inc(s_start, 1)
            pe.wait_ge(s_blk, 1)
            with pe.If(pe.value_load(unsorted[0:1, 0:1], min_val=0, max_val=1) == 1):
                for n in range(PASSES):
                    pe.wait_ge(s_number, n + 1)
                    pe.matmul(bank[0][:, 0:DIGITS], earlier, number[:, 0, :], start=True, stop=True)
                    pe.matmul(bank[0][:, DIGITS:2 * DIGITS], ones[:, :], number[:, 0, :], start=True, stop=True).then_inc(s_before, 1)
            pe.wait_ge(s_const, 1)
            for l in range(L):
                s = LS[l]
                h = xN if l == 0 else hN
                loads = 32 * TURNS * l
                row_loads = 16 * TURNS * l
                if l:
                    pe.wait_ge(s_win_deg, 1)
                    pe.matmul(bank[0][:, 0:WINS], ones[:, :], win[:, 6, :], start=True, stop=True).then_inc(s_win_n, 1)
                pe.wait_ge(s_h, l + 1)
                for r in range(R):
                    if r >= 2:
                        pe.wait_ge(s.wts, r - 1)
                    pe.transpose(bank[6 + r % 2][:, 0:P], Wsb[:, l, r, :], ident[:, :]).then_inc(s.wt, 1)
                    pe.wait_ge(s.wts, r + 1)
                    pe.matmul(bank[5][:, 2 * r:2 * r + 2], WT[:, r % 2, :], qk[:, l, :], start=True, stop=True).then_inc(s.wqk, 1)

                def transpose_block(b):
                    if b >= 2:
                        pe.wait_ge(s.hts, b - 1)
                    pe.transpose(bank[6 + b % 2][:, 0:P], h[:, b, :], ident[:, :]).then_inc(s.tr, 1)

                transpose_block(0)
                pe.wait_ge(s.wqks, 1)
                for b in range(NB):
                    if b + 1 < NB:
                        transpose_block(b + 1)
                    pe.wait_ge(s.hts, b + 1)
                    if b >= 2:
                        pe.wait_ge(s.eva, b - 1)
                        pe.wait_ge(s.evb, b - 1)
                    half = 3 * (b % 2)
                    for j in range(2):
                        pe.matmul(bank[half + j][:, :], hTs[:, b % 2, :],
                                  Wsb[:, l, j * (R // 2):(j + 1) * (R // 2), :].rearrange("p r f -> p (r f)"), start=True, stop=True)
                    pe.matmul(bank[half + 2][:, 0:2 * R], hTs[:, b % 2, :], Wqk[:, :, :].rearrange("p o r -> p (o r)"),
                              start=True, stop=True).then_inc(s.mm, 1)
                pe.wait_ge(s.aip, 1)
                pe.wait_ge(s.eva, NB)
                for b in range(NB):
                    there = bank[b // 8][0:ROWS_RELATION, :].bitcast(BF16)
                    ins = pe.transpose(there[:, (b % 8) * P:(b % 8 + 1) * P], ai_parts[:, b, :], ident_b[:, :])
                ins.then_inc(s.ait, 1)
                pe.wait_ge(s.aits, -(-NB // 8))
                if l:
                    pe.wait_ge(s_keep, 1)
                    for n in range(TC):
                        ins = pe.matmul(bank[1 + n // 4][:, (n % 4) * P:(n % 4 + 1) * P], ones[:, :], keyT[:, n, :],
                                        start=True, stop=True)
                    ins.then_inc(s_keep_bc, 1)
                    pe.wait_ge(s_keys, 1)
                    for n in range(TC):
                        pe.transpose(bank[1 + n // 4][:, (n % 4) * P:(n % 4 + 1) * P], keyT[:, n, :], ident[:, :])
                        ins = pe.transpose(bank[4 + n // 4][:, (n % 4) * P:(n % 4 + 1) * P], lowT[:, n, :], ident[:, :])
                    ins.then_inc(s_keyT, 1)
                    pe.wait_ge(s_keys, 2)
                else:
                    pe.wait_ge(s_fG, 1)
                    for h in range(2):
                        for c in range(GC):
                            ins = pe.transpose(bank[1 + h][:, c * P:(c + 1) * P], fG[:, 0, c, h * P:(h + 1) * P], ident[:, :])
                        ins.then_inc(s_colT, 1)
                    pe.wait_ge(s_blkf, 1)
                    pe.matmul(bank[0][:, 0:SLOTS], ones[0:1, :], fresh[0:1, :], start=True, stop=True).then_inc(s_fresh, 1)
                    pe.wait_ge(s_blkf, 2)

                def logits(g, k, i):
                    hb = k // (TURN // 2)
                    pe.wait_ge(s.ais, g + 1)
                    at_least(pe, s.ld, g - 1)
                    pe.wait_ge(er_loaded[hb], row_loads + 16 * (i + 1))
                    there = bank[k % 2]
                    cols = erows[:, hb, (k % (TURN // 2)) * GROUP:(k % (TURN // 2) + 1) * GROUP]
                    pe.matmul(there[:, 0:GROUP], mask_w[:, :], cols, start=True, stop=False)
                    pe.matmul(there[:, 0:GROUP], aiS[:, k % 2, :], cols, start=False, stop=False)
                    pe.wait_ge(gathered[k], loads + 32 * (i + 1))
                    for t in range(2):
                        ins = pe.matmul(there[:, t * P:(t + 1) * P], msg[:, k, t, F + 1:F + 2].to_broadcast([P, P]), ident[:, :],
                                        start=False, stop=(t == 1))
                    ins.then_inc(s.xd, 1)

                def turn_probs(g, k):
                    pe.wait_ge(s.pd, g + 1)
                    at_least(pe, s.ptd, g - 1)
                    for t in range(2):
                        ins = pe.transpose(bank[2 + k % 2][:, t * P:(t + 1) * P], prob[:, k % 2, t * P:(t + 1) * P], ident[:, :])
                    ins.then_inc(s.td, 1)

                def sums(g, k):
                    pe.wait_ge(s.ptd, g + 1)
                    at_least(pe, s.ad, g - 1)
                    for t in range(2):
                        ins = pe.matmul(bank[4 + k % 2][:, 0:ROW], probT[:, k % 2, t * P:(t + 1) * P], msg[:, k, t, :],
                                        start=(t == 0), stop=(t == 1))
                    ins.then_inc(s.ud, 1)

                def count_edges(g, k):
                    at_least(pe, s.rn, g * TILES_PER_GROUP)
                    for j in range(TILES_PER_GROUP):
                        place = (k * TILES_PER_GROUP + j) % (2 * TILES_PER_GROUP)
                        pe.wait_ge(s.oh, 2 * (g * TILES_PER_GROUP + j + 1))
                        pe.matmul(bank[6 + j // 2][:, (j % 2) * KEYS:(j % 2 + 1) * KEYS], oh_low[:, place, :],
                                  oh_key[:, place, :], start=True, stop=True).then_inc(s.cm, 1)

                def turn(i):
                    first = isinstance(i, int)
                    for k in range(TURN):
                        g = i * TURN + k
                        logits(g, k, i)
                        if not first or k >= 2:
                            sums(g - 2, (k - 2) % TURN)
                        if l and (not first or k >= 2):
                            count_edges(g - 2, (k - 2) % TURN)
                        if not first or k >= 1:
                            turn_probs(g - 1, (k - 1) % TURN)

                turn(0)
                with pe.Fori(1, TURNS) as i:
                    turn(i)
                sums(NG - 2, TURN - 2)
                turn_probs(NG - 1, TURN - 1)
                if l:
                    count_edges(NG - 2, TURN - 2)
                sums(NG - 1, TURN - 1)
                if l:
                    count_edges(NG - 1, TURN - 1)

            for c in range(3):
                s = CS
                done, chunks, acts = conv_before(c)
                pe.wait_ge(s.y, c + 1)

                by_source_block = count_in[:, :, :, :].rearrange("p i w (d s) -> p i (w d) s", s=NB)

                def block_sums(b, k, turn):
                    at_least(pe, s.ev, done + b - 2)
                    pe.wait_ge(counts_in[k], 16 * (c * (NB // 3 + (k < NB % 3)) + turn + 1))
                    for j in range(NB):
                        pe.matmul(bank[k][:, 0:F], by_source_block[:, k, :, j], work[:, j, :],
                                  start=(j == 0), stop=False)
                    pe.matmul(bank[k][:, 0:F], ident[:, :], work[:, bass.ds(b, 1), :].rearrange("p o f -> p (o f)"),
                              start=False, stop=True).then_inc(s.ud, 1)

                for k in range(3):
                    block_sums(k, k, 0)
                with pe.Fori(1, NB // 3) as i:
                    for k in range(3):
                        block_sums(3 * i + k, k, i)
                for b in range(NB // 3 * 3, NB):
                    block_sums(b, b % 3, b // 3)
                pe.wait_ge(s.ev, done + NB)
                for q, (o, n) in enumerate(NCH):
                    if q >= 2:
                        pe.wait_ge(s.trs if c == 0 else s.act, acts + q - 1)
                    for j in range(n // P):
                        ins = pe.transpose(bank[q % 2][:, j * P:(j + 1) * P], hN[:, o // P + j, :], ident[:, :])
                    ins.then_inc(s.tr, 1)
                if c == 0:
                    pe.wait_ge(s.trs, len(NCH))
                    for m, (v, (o, n)) in enumerate((v, ch) for v in range(2) for ch in NCH):
                        if m >= 4:
                            pe.wait_ge(s.act, m - 3)
                        pe.matmul(bank[2 + m % 4][:, 0:n], W1sb[:, v * P:(v + 1) * P], hT[:, o:o + n],
                                  start=True, stop=True).then_inc(s.mm, 1)
                pe.wait_ge(s.bn, c + 1)
                for q, (o, n) in enumerate(NCH):
                    if q >= 2:
                        pe.wait_ge(s.y2, chunks + q - 1)
                    for j in range(n // P):
                        there = bank[6 + q % 2][:, j * P:(j + 1) * P]
                        nodes = slice(o + j * P, o + (j + 1) * P)
                        if c == 0:
                            for v in range(2):
                                ins = pe.matmul(there, H1[:, v, nodes], W2sb[:, v, :], start=(v == 0), stop=(v == 1))
                        elif c == 1:
                            ins = pe.matmul(there, H1[:, 0, nodes], W3sb[:, :], start=True, stop=True)
                        else:
                            ins = pe.transpose(there, H1[:, 0, nodes], ident[:, :])
                    ins.then_inc(s.mm2, 1)


_INS = ["x", "src", "dst", "edge_type_8", "L0_gnn_W", "L0_gnn_att_q", "L0_gnn_att_k", "L0_gnn_bias",
        "L1_gnn_W1", "L1_gnn_b1", "L1_gnn_g1", "L1_gnn_beta1", "L1_gnn_W2", "L1_gnn_b2", "L1_gnn_g2", "L1_gnn_beta2",
        "L1_gnn_W3", "L1_gnn_b3", "L1_gnn_g3", "L1_gnn_beta3"]


def kernel(**inputs):
    import numpy as _np
    import concourse.bacc as _bacc
    from concourse import mybir as _mybir
    from concourse.bass_utils import run_bass_kernel_spmd as _run

    nc = _bacc.Bacc("TRN2", target_bir_lowering=False, num_devices=1)
    arrays, args = {}, []
    for name in _INS:
        a = _np.ascontiguousarray(inputs[name])
        arrays[f"in_{name}_dram"] = a
        args.append(nc.dram_tensor(f"in_{name}_dram", a.shape, _mybir.dt.from_np(a.dtype), kind="ExternalInput").ap())
    out = nc.dram_tensor("out_0_dram", inputs["x"].shape, _mybir.dt.float32, kind="ExternalOutput").ap()
    gnn_kernel(nc, *args, out)
    r = _run(nc, [arrays], core_ids=[0])
    return r.results[0]["out_0_dram"]
```
